# Optimizing a Trainium2 kernel written in Bass

```python
import numpy as np
import jax
import jax.numpy as jnp

def _softmax(x, axis=-1):
    return jax.nn.softmax(x, axis=axis)

def _gelu(x):
    return jax.nn.gelu(x, approximate=True)

def _silu(x):
    return jax.nn.silu(x)

def _sigmoid(x):
    return jax.nn.sigmoid(x)

def _layernorm(x, axis=-1, eps=1e-05):
    m = jnp.mean(x, axis=axis, keepdims=True)
    v = jnp.var(x, axis=axis, keepdims=True)
    return (x - m) / jnp.sqrt(v + eps)

def _scatter_add(tgt, idx, src, axis=0):
    return tgt.at[idx].add(src)

def _segment_sum(src, seg, n):
    return jax.ops.segment_sum(src, seg, n)
kernel_name = 'mk_adaln_d1_jaxref_r8_cfd7ed'

def setup_inputs(seed: int=0):
    np.random.seed(seed)
    _w = jnp.asarray

    def _L0_attn_setup():
        import jax, jax.numpy as jnp
        import numpy as np
        import math
        BATCH = 4
        SEQ = 512
        EMBED = 128
        NUM_HEADS = 16
        HEAD_DIM = EMBED // NUM_HEADS
        WINDOW_SIZE = 128
        RADIUS = 2 * WINDOW_SIZE
        CHUNK = RADIUS
        key = jax.random.key(seed)
        ks = jax.random.split(key, 9)
        init = lambda k, shape: (0.02 * jax.random.normal(k, shape)).astype(jnp.float32)
        return {'hidden_states': jax.random.normal(ks[0], (BATCH, SEQ, EMBED), dtype=jnp.float32), 'wq': init(ks[1], (EMBED, EMBED)), 'bq': init(ks[2], (EMBED,)), 'wk': init(ks[3], (EMBED, EMBED)), 'bk': init(ks[4], (EMBED,)), 'wv': init(ks[5], (EMBED, EMBED)), 'bv': init(ks[6], (EMBED,)), 'wo': init(ks[7], (EMBED, EMBED)), 'bo': init(ks[8], (EMBED,))}
    _L0_attn_in = _L0_attn_setup()

    def _L0_ffn_setup():
        import jax, jax.numpy as jnp
        import numpy as np
        from jax.scipy.linalg import expm
        D = 128
        E = 6
        K = 2
        H = 2 * D
        A4 = 4 * D
        NROT = 4
        LN_EPS = 1e-05

        def _xavier(key, shape):
            fan_in, fan_out = (shape[-2], shape[-1])
            lim = np.sqrt(6.0 / (fan_in + fan_out))
            return jax.random.uniform(key, shape, jnp.float32, -lim, lim)

        def _layernorm(x, g, b):
            mu = jnp.mean(x, axis=-1, keepdims=True)
            var = jnp.var(x, axis=-1, keepdims=True)
            return (x - mu) * jax.lax.rsqrt(var + LN_EPS) * g + b

        def _moe(xn, gate_w, gate_b, ew1, eb1, ew2, eb2):
            logits = xn @ gate_w + gate_b
            tw, ti = jax.lax.top_k(logits, K)
            tw = jax.nn.softmax(tw, axis=-1)
            w_full = jnp.sum(tw[..., None] * jax.nn.one_hot(ti, E, dtype=tw.dtype), axis=-2)
            h = jax.nn.gelu(jnp.einsum('bsd,edh->besh', xn, ew1) + eb1[None, :, None, :], approximate=False)
            eo = jnp.einsum('besh,ehd->besd', h, ew2) + eb2[None, :, None, :]
            return jnp.einsum('bse,besd->bsd', w_full, eo)

        def _rotate(x, gens):
            for i in range(NROT):
                x = x @ expm(gens[i])
            return x
        key = jax.random.key(seed)
        ks = jax.random.split(key, 16)
        x = jax.random.normal(ks[0], (4, 256, D), jnp.float32)
        gens_raw = _xavier(ks[1], (NROT, D, D))
        gens = 0.5 * (gens_raw - jnp.swapaxes(gens_raw, -1, -2))
        return {'x': x, 'ln_g': jnp.ones((D,), jnp.float32), 'ln_b': jnp.zeros((D,), jnp.float32), 'aw1': _xavier(ks[2], (D, A4)), 'ab1': jnp.zeros((A4,), jnp.float32), 'aw2': _xavier(ks[3], (A4, D)), 'ab2': jnp.zeros((D,), jnp.float32), 'gate_w': _xavier(ks[4], (D, E)), 'gate_b': jnp.zeros((E,), jnp.float32), 'ew1': _xavier(ks[5], (E, D, H)), 'eb1': jnp.zeros((E, H), jnp.float32), 'ew2': _xavier(ks[6], (E, H, D)), 'eb2': jnp.zeros((E, D), jnp.float32), 'gens': gens, 'gc_w': _xavier(ks[7], (2 * D, 1)), 'gc_b': jnp.zeros((1,), jnp.float32)}
    _L0_ffn_in = _L0_ffn_setup()
    _L0_c = _w((lambda *s: np.random.randn(*s).astype(np.float32) * 0.05)(16, 128))
    _L0_wmod = _w((lambda *s: np.random.randn(*s).astype(np.float32) * 0.05)(128, 6 * 128) * 128 ** (-0.5))
    _d = {'L0_attn_hidden_states': _L0_attn_in['hidden_states'], 'L0_attn_wq': _L0_attn_in['wq'], 'L0_attn_bq': _L0_attn_in['bq'], 'L0_attn_wk': _L0_attn_in['wk'], 'L0_attn_bk': _L0_attn_in['bk'], 'L0_attn_wv': _L0_attn_in['wv'], 'L0_attn_bv': _L0_attn_in['bv'], 'L0_attn_wo': _L0_attn_in['wo'], 'L0_attn_bo': _L0_attn_in['bo'], 'L0_ffn_ln_g': _L0_ffn_in['ln_g'], 'L0_ffn_ln_b': _L0_ffn_in['ln_b'], 'L0_ffn_aw1': _L0_ffn_in['aw1'], 'L0_ffn_ab1': _L0_ffn_in['ab1'], 'L0_ffn_aw2': _L0_ffn_in['aw2'], 'L0_ffn_ab2': _L0_ffn_in['ab2'], 'L0_ffn_gate_w': _L0_ffn_in['gate_w'], 'L0_ffn_gate_b': _L0_ffn_in['gate_b'], 'L0_ffn_ew1': _L0_ffn_in['ew1'], 'L0_ffn_eb1': _L0_ffn_in['eb1'], 'L0_ffn_ew2': _L0_ffn_in['ew2'], 'L0_ffn_eb2': _L0_ffn_in['eb2'], 'L0_ffn_gens': _L0_ffn_in['gens'], 'L0_ffn_gc_w': _L0_ffn_in['gc_w'], 'L0_ffn_gc_b': _L0_ffn_in['gc_b'], 'L0_c': _L0_c, 'L0_wmod': _L0_wmod}
    _x0 = _d['L0_attn_hidden_states']
    _d['L0_attn_hidden_states'] = jax.random.normal(jax.random.fold_in(jax.random.key(seed), 1), (16, 256, 128), dtype=_x0.dtype)
    del _x0
    return _d

def reference(L0_attn_hidden_states, L0_attn_wq, L0_attn_bq, L0_attn_wk, L0_attn_bk, L0_attn_wv, L0_attn_bv, L0_attn_wo, L0_attn_bo, L0_ffn_ln_g, L0_ffn_ln_b, L0_ffn_aw1, L0_ffn_ab1, L0_ffn_aw2, L0_ffn_ab2, L0_ffn_gate_w, L0_ffn_gate_b, L0_ffn_ew1, L0_ffn_eb1, L0_ffn_ew2, L0_ffn_eb2, L0_ffn_gens, L0_ffn_gc_w, L0_ffn_gc_b, L0_c, L0_wmod):

    def _L0_attn_ref(hidden_states, wq, bq, wk, bk, wv, bv, wo, bo):
        import jax, jax.numpy as jnp
        import numpy as np
        import math
        BATCH = 4
        SEQ = 512
        EMBED = 128
        NUM_HEADS = 16
        HEAD_DIM = EMBED // NUM_HEADS
        WINDOW_SIZE = 128
        RADIUS = 2 * WINDOW_SIZE
        CHUNK = RADIUS
        B, T, E = hidden_states.shape
        H, D = (NUM_HEADS, HEAD_DIM)
        c = CHUNK
        nC = T // c

        def proj(w, b):
            y = hidden_states @ w + b
            return y.reshape(B, T, H, D).transpose(0, 2, 1, 3)
        q = proj(wq, bq)
        k = proj(wk, bk)
        v = proj(wv, bv)
        scale = jnp.sqrt(jnp.asarray(D, dtype=q.dtype))
        kp = jnp.pad(k, ((0, 0), (0, 0), (c, c), (0, 0)))
        vp = jnp.pad(v, ((0, 0), (0, 0), (c, c), (0, 0)))
        idx = jnp.arange(nC)[:, None] * c + jnp.arange(3 * c)[None, :]
        kb = kp[:, :, idx, :]
        vb = vp[:, :, idx, :]
        qb = q.reshape(B, H, nC, c, D)
        scores = jnp.einsum('bhncd,bhnkd->bhnck', qb, kb) / scale
        qpos = (jnp.arange(nC) * c)[:, None] + jnp.arange(c)
        kpos = (jnp.arange(nC) * c)[:, None] - c + jnp.arange(3 * c)
        valid = (jnp.abs(qpos[:, :, None] - kpos[:, None, :]) <= RADIUS) & (kpos[:, None, :] >= 0) & (kpos[:, None, :] < T)
        scores = jnp.where(valid[None, None], scores, -jnp.inf)
        p = jax.nn.softmax(scores, axis=-1)
        o = jnp.einsum('bhnck,bhnkd->bhncd', p, vb)
        o = o.reshape(B, H, T, D).transpose(0, 2, 1, 3).reshape(B, T, E)
        return o @ wo + bo

    def _L0_ffn_ref(x, ln_g, ln_b, aw1, ab1, aw2, ab2, gate_w, gate_b, ew1, eb1, ew2, eb2, gens, gc_w, gc_b):
        import jax, jax.numpy as jnp
        import numpy as np
        from jax.scipy.linalg import expm
        D = 128
        E = 6
        K = 2
        H = 2 * D
        A4 = 4 * D
        NROT = 4
        LN_EPS = 1e-05

        def _xavier(key, shape):
            fan_in, fan_out = (shape[-2], shape[-1])
            lim = np.sqrt(6.0 / (fan_in + fan_out))
            return jax.random.uniform(key, shape, jnp.float32, -lim, lim)

        def _layernorm(x, g, b):
            mu = jnp.mean(x, axis=-1, keepdims=True)
            var = jnp.var(x, axis=-1, keepdims=True)
            return (x - mu) * jax.lax.rsqrt(var + LN_EPS) * g + b

        def _moe(xn, gate_w, gate_b, ew1, eb1, ew2, eb2):
            logits = xn @ gate_w + gate_b
            tw, ti = jax.lax.top_k(logits, K)
            tw = jax.nn.softmax(tw, axis=-1)
            w_full = jnp.sum(tw[..., None] * jax.nn.one_hot(ti, E, dtype=tw.dtype), axis=-2)
            h = jax.nn.gelu(jnp.einsum('bsd,edh->besh', xn, ew1) + eb1[None, :, None, :], approximate=False)
            eo = jnp.einsum('besh,ehd->besd', h, ew2) + eb2[None, :, None, :]
            return jnp.einsum('bse,besd->bsd', w_full, eo)

        def _rotate(x, gens):
            for i in range(NROT):
                x = x @ expm(gens[i])
            return x
        residual = x
        xn = _layernorm(x, ln_g, ln_b)
        abel = jax.nn.gelu(xn @ aw1 + ab1, approximate=False) @ aw2 + ab2
        nonabel = _rotate(_moe(xn, gate_w, gate_b, ew1, eb1, ew2, eb2), gens)
        combined = jnp.concatenate([abel, nonabel], axis=-1)
        gate = jax.nn.sigmoid(combined @ gc_w + gc_b)
        mixed = abel * (1.0 - gate) + nonabel * gate
        return residual + mixed
    x = L0_attn_hidden_states
    mod = (_silu(L0_c) @ L0_wmod).reshape(L0_c.shape[0], 6, 1, -1)
    sa, ca, ga, sb, cb, gb = (mod[:, 0], mod[:, 1], mod[:, 2], mod[:, 3], mod[:, 4], mod[:, 5])
    ga = (2 * (ga >= 0) - 1) * jnp.maximum(jnp.abs(ga), 0.25)
    gb = (2 * (gb >= 0) - 1) * jnp.maximum(jnp.abs(gb), 0.25)
    h = _layernorm(x, axis=-1) * (1 + ca) + sa
    x = x + ga * _L0_attn_ref(h, L0_attn_wq, L0_attn_bq, L0_attn_wk, L0_attn_bk, L0_attn_wv, L0_attn_bv, L0_attn_wo, L0_attn_bo)
    h = _layernorm(x, axis=-1) * (1 + cb) + sb
    x = x + gb * _L0_ffn_ref(h, L0_ffn_ln_g, L0_ffn_ln_b, L0_ffn_aw1, L0_ffn_ab1, L0_ffn_aw2, L0_ffn_ab2, L0_ffn_gate_w, L0_ffn_gate_b, L0_ffn_ew1, L0_ffn_eb1, L0_ffn_ew2, L0_ffn_eb2, L0_ffn_gens, L0_ffn_gc_w, L0_ffn_gc_b)
    return x

_drawn_inputs = setup_inputs


def setup_inputs(seed=0):
    import zlib

    import numpy as np

    out = dict(_drawn_inputs(seed))
    spreads = {'L0_ffn_ln_g': (1.0, 0.58),
     'L0_ffn_ln_b': (0.0, 0.477),
     'L0_ffn_ab1': (0.0, 0.8),
     'L0_ffn_ab2': (0.0, 0.592),
     'L0_ffn_gate_b': (0.0, 0.694),
     'L0_ffn_eb1': (0.0, 0.8),
     'L0_ffn_eb2': (0.0, 0.8)}
    factors = {'L0_attn_wq': 8.0,
     'L0_attn_bq': 8.0,
     'L0_attn_wk': 8.0,
     'L0_attn_bk': 8.0,
     'L0_attn_wv': 8.0,
     'L0_attn_bv': 8.0,
     'L0_attn_wo': 8.0,
     'L0_attn_bo': 8.0}
    for name, (base, spread) in spreads.items():
        noise = np.random.default_rng([zlib.crc32(name.encode()), seed]).standard_normal(out[name].shape)
        drawn = base * np.exp(spread * noise) if base else spread * noise
        out[name] = jnp.asarray(drawn.astype(out[name].dtype))
    for name, factor in factors.items():
        out[name] = (out[name] * factor).astype(out[name].dtype)
    return out
```

```python
from contextlib import ExitStack

import numpy as np

import concourse.bass as bass
from concourse import mybir

F32 = mybir.dt.float32
F32R = mybir.dt.float32r
U32 = mybir.dt.uint32
ALU = mybir.AluOpType
ACT = mybir.ActivationFunctionType
AX_X = mybir.AxisListType.X

P = 128
BATCH, SEQ, EMB = 16, 256, 128
HEADS = 16
HDIM = EMB // HEADS
TILES = BATCH * SEQ // P
TPB = SEQ // P
NG = 4
SQUARINGS = 16
TAYLOR = 10
EPS = 1e-5
SCALE = float(1.0 / np.sqrt(HDIM))
MAXROW = 96
VW = 32
MLP = 4 * EMB
EXPERTS, EH = 6, 2 * EMB
ECH = EXPERTS * EH // P
ACH = MLP // P
CHUNKS = ACH + ECH
NVEC = CHUNKS + 5
BT = 4
BLOCKS = TILES // BT
OW = HDIM + 1


def head_at(n):
    r, i, j = n // 8, n // 4 % 2, n % 4
    return 8 * r + 2 * j + i


def need(eng, sem, value):
    if not isinstance(value, int) or value > 0:
        eng.wait_ge(sem, value)


def settle(eng, sem):
    eng.sem_inc(sem, 1)


def build(nc, a, out):
    with ExitStack() as ctx:
        def sb(name, shape, dt=F32):
            return ctx.enter_context(nc.sbuf_tensor(name, shape, dt))

        def ps(name, shape):
            return ctx.enter_context(nc.psum_tensor(name, shape, F32))

        def sem(name):
            return ctx.enter_context(nc.semaphore(name))

        parts_dram = nc.dram_tensor("parts_dram", (2, 2, 2, HDIM, HEADS, SEQ), F32).ap()

        x_keep = sb("x_keep", [P, TILES, EMB])
        ident = sb("ident", [P, P])
        ones = sb("ones", [P, P])
        wq, wk, wv, wo = (sb(n, [P, EMB]) for n in ("wq", "wk", "wv", "wo"))
        vec_rows = sb("vec_rows", [NVEC, P])
        vec_cols = sb("vec_cols", [P, NVEC])
        b1c, cols, lnc = vec_cols, vec_cols[:, CHUNKS:CHUNKS + 3], vec_cols[:, CHUNKS + 3:CHUNKS + 5]
        bvb = sb("bvb", [P, TPB, EMB])
        c_row = sb("c_row", [BATCH, EMB])
        c_exp = sb("c_exp", [BATCH, EMB])
        c_sig = sb("c_sig", [BATCH, EMB])
        c_silu = sb("c_silu", [BATCH, EMB])
        c_t = sb("c_t", [P, BATCH])
        wmod = sb("wmod", [P, 6 * EMB])
        mod_t = sb("mod_t", [P, 3, BATCH])
        gate_bo = sb("gate_bo", [P, BATCH])
        tmp_t = sb("tmp_t", [P, 2, BATCH])

        gen = sb("gen", [P, NG, P])
        gen_abs = sb("gen_abs", [P, NG, P])
        gen_t = sb("gen_t", [P, NG, P])
        rot = sb("rot", [P, NG, P])
        rot_t = sb("rot_t", [P, NG, P])
        ident4 = sb("ident4", [P, NG, P])
        nrm = sb("nrm", [P, NG])
        gscale = sb("gscale", [P, NG])
        todo = sb("todo", [P, NG])

        q_stack = sb("q_stack", [P, 2, HEADS, SEQ], F32R)
        k_stack = sb("k_stack", [P, 2, HEADS, SEQ], F32R)
        prob = sb("prob", [P, 8, TPB * SEQ])
        v_blocks = sb("v_blocks", [P, 2, TPB, HEADS, VW])
        v_tok = sb("v_tok", [P, TPB, EMB])
        stats = sb("stats", [P, TPB, 6])
        mv = sb("mv", [P, TPB, 2])
        rstd = sb("rstd", [P, TPB])
        var_eps = sb("var_eps", [P, TPB])
        neg_half = sb("neg_half", [P, TPB])
        xhat = sb("xhat", [P, TPB, EMB])
        h_t = sb("h_t", [P, SEQ])
        qk = sb("qk", [P, 2, SEQ])
        qk_parts = sb("qk_parts", [P, 2, 2, SEQ], F32R)
        row_max = sb("row_max", [P, 2, TPB, HEADS])
        max_parts = sb("max_parts", [P, 2, TPB, 2, 8], F32R)
        max_rows = sb("max_rows", [16, 2, SEQ])
        o_raw = sb("o_raw", [P, 2, SEQ])
        o_rsum = sb("o_rsum", [P, 2, 16])
        o_tok = sb("o_tok", [P, TPB, EMB])
        o_t = sb("o_t", [P, SEQ])
        y_t = sb("y_t", [P, SEQ])

        aw1 = sb("aw1", [P, MLP])
        aw2 = sb("aw2", [P, MLP // P, EMB])
        ew1 = sb("ew1", [P, EXPERTS, EH])
        ew2 = sb("ew2", [P, ECH, EMB])
        ew2_t = sb("ew2_t", [P, ECH, P])
        ew2_rot = sb("ew2_rot", [P, ECH, EMB])
        rot_all = sb("rot_all", [P, 3, P])
        eb2 = sb("eb2", [EXPERTS, EMB])
        eb2_t = sb("eb2_t", [P, EXPERTS])
        eb2_rot = sb("eb2_rot", [EXPERTS, EMB])
        ab2b = sb("ab2b", [P, EMB])
        gcwb = sb("gcwb", [P, 2, EMB])
        gate_w = sb("gate_w", [P, EXPERTS])
        gate_bb = sb("gate_bb", [P, EXPERTS])
        gcb = sb("gcb", [P, 1])
        gcb_half = sb("gcb_half", [P, 1])
        tri = sb("tri", [P, EXPERTS, EXPERTS])
        mod_rows = sb("mod_rows", [BATCH, 3, EMB])
        mod_tmp = sb("mod_tmp", [BATCH, 2, EMB])
        mod_b = sb("mod_b", [P, 2, 2, 3, EMB])
        st2 = sb("st2", [P, 2, BT, 6])
        mv2 = sb("mv2", [P, 2, BT, 2])
        ve2 = sb("ve2", [P, 2, BT])
        rs2 = sb("rs2", [P, 2, BT])
        nh4 = sb("nh4", [P, BT])
        h2 = sb("h2", [P, 2, BT, EMB])
        xn_tok = sb("xn_tok", [P, BT, EMB])
        xn_t = sb("xn_t", [P, 2, BT * P])
        lg = sb("lg", [P, BT, EXPERTS])
        cmp_gt = sb("cmp_gt", [P, BT, EXPERTS, EXPERTS])
        cmp_eq = sb("cmp_eq", [P, BT, EXPERTS, EXPERTS])
        rank = sb("rank", [P, BT, EXPERTS])
        sel = sb("sel", [P, 2, BT, EXPERTS])
        pick = sb("pick", [P, BT, EXPERTS])
        top = sb("top", [P, 3, BT])
        th = sb("th", [P, BT])
        w_gate = sb("w_gate", [P, 2, BT, EXPERTS])
        w_t = sb("w_t", [EXPERTS, BT * P])
        hid = prob[:, 0:4, :]
        acc = sb("acc", [P, 2, BT, EMB])
        abel = prob[:, 4:6, :].rearrange("p r (t e) -> p r t e", t=BT)
        zpart = sb("zpart", [P, 2, BT])
        zsum = sb("zsum", [P, BT])
        gth = sb("gth", [P, BT])
        gmix = sb("gmix", [P, BT])
        diff = sb("diff", [P, BT, EMB])
        y_out = prob[:, 6:8, :].rearrange("p r (t e) -> p r t e", t=BT)

        smax_bank = [ps(f"smax{i}", [P, 512]) for i in range(2)]
        st_bank = [ps(f"st{i}", [P, 512]) for i in range(2)]
        pv_bank = [ps(f"pv{i}", [P, 512]) for i in range(2)]
        mx = ps("mx", [P, 512])
        my = ps("my", [P, 512])

        s_w = sem("s_w")
        s_x = [sem(f"s_x{i}") for i in range(3)]
        s_gen = sem("s_gen")
        s_const = sem("s_const")
        s_stackzero = sem("s_stackzero")
        c1, c2, c3, c4 = sem("c_exp_ok"), sem("c_dve"), sem("c_t_pe"), sem("c_t_ok")
        mod_pe, mod_ok, mod_dve = sem("mod_pe"), sem("mod_ok"), sem("mod_dve")
        g_abs, g_sum, g_dve, g_tpe, g_tok, g_mm, g_acc = (
            sem(n) for n in ("g_abs", "g_sum", "g_dve", "g_tpe", "g_tok", "g_mm", "g_acc"))
        smax_done, st_done, pv_done = sem("smax_done"), sem("st_done"), sem("pv_done")
        xt_done, qk_done, v_done, mt_done, ot1_done, ot2_done, y_done, yt_done = (
            sem(n) for n in ("xt_done", "qk_done", "v_done", "mt_done", "ot1_done", "ot2_done", "y_done", "yt_done"))
        sqt_done, sq_done = sem("sqt_done"), sem("sq_done")
        red_done, max_split, max_row_ok, v_ok, o_norm, x1_ok, stat_ok, rot_ok = (
            sem(n) for n in ("red_done", "max_split", "max_row_ok", "v_ok", "o_norm", "x1_ok", "stat_ok", "rot_ok"))
        d_bn, d_mhi, d_rs, d_sq = sem("d_bn"), sem("d_mhi"), sem("d_rs"), sem("d_sq")
        exp_done, h_ok, qk_ok, oraw_ok, ot_ok, y_ok, rott_ok = (
            sem(n) for n in ("exp_done", "h_ok", "qk_ok", "oraw_ok", "ot_ok", "y_ok", "rott_ok"))
        vb_ok, split_ok, xhat_ok = sem("vb_ok"), sem("split_ok"), sem("xhat_ok")
        p_hi, p_var, p_rs, vb_zero = sem("p_hi"), sem("p_var"), sem("p_rs"), sem("vb_zero")
        parts_out = sem("parts_out")
        stack_in = [sem(f"stack_in{r}") for r in range(2)]
        max_in = [sem(f"max_in{r}") for r in range(2)]
        d_settled, p_settled = sem("d_settled"), sem("p_settled")

        f_w, f_const, mr_pe, mr_dve, mr_out = sem("f_w"), sem("f_const"), sem("mr_pe"), sem("mr_dve"), sem("mr_out")
        e2t_done, e2t_ok, rt_done, rt_ok, rp_done, rp_ok, er_done, er_ok = (
            sem(n) for n in ("e2t_done", "e2t_ok", "rt_done", "rt_ok", "rp_done", "rp_ok", "er_done", "er_ok"))
        modb_in = [sem(f"modb_in{i}") for i in range(2)]
        n_bn, n_mv, n_var, n_rs, n_hat, n_mul, h2_ok, xn_ok, fd = (
            sem(n) for n in ("n_bn", "n_mv", "n_var", "n_rs", "n_hat", "n_mul", "h2_ok", "xn_ok", "fd"))
        fxt_done, xnt_ok, lg_done, d_ok, th_ok, w_ok, wt_done, wt_ok, ai_done, acc0_ok = (
            sem(n) for n in ("fxt_done", "xnt_ok", "lg_done", "d_ok", "th_ok", "w_ok", "wt_done", "wt_ok", "ai_done", "acc0_ok"))
        m1_done, gelu_ok, m2_done, acc_ok, abel_ok, z_ok, tz, zth_ok, diff_ok, mix_ok, res1, res2, y_fin = (
            sem(n) for n in ("m1_done", "gelu_ok", "m2_done", "acc_ok", "abel_ok", "z_ok", "tz", "zth_ok", "diff_ok", "mix_ok", "res1", "res2", "y_fin"))
        y_stored = [sem(f"y_stored{i}") for i in range(2)]
        mod_dram = nc.dram_tensor("mod_dram", (BATCH, 3, EMB), F32).ap()

        block = ctx.enter_context(nc.Block())

        def blocks(eng, step):
            step(-1, -1, 1)
            step(0, 0, 0)
            with eng.Fori(0, (BLOCKS - 4) // 2) as i:
                step(i * 2 + 1, 1, 1)
                step(i * 2 + 2, 1, 0)
            for q in range(BLOCKS - 3, BLOCKS + 1):
                step(q, q, q % 2)

        def iterations(eng, step):
            for b in range(-3, 1):
                step(b, b, b % 2)
            with eng.Fori(0, (BATCH - 4) // 2) as i:
                step(i * 2 + 1, 1, 1)
                step(i * 2 + 2, 1, 0)
            for b in range(BATCH - 3, BATCH + 1):
                step(b, b, b % 2)

        NF = 10
        NW = 15

        @block.sync
        def _(sp):
            sp.dma_start(x_keep[:, 0:2, :], a["x"][0:2].rearrange("t p e -> p t e")).then_inc(s_x[0], 16)
            sp.dma_start(c_row[:], a["c"]).then_inc(s_w, 16)
            sp.dma_start(wmod[:], a["wmod"]).then_inc(s_w, 16)
            for t, n in ((wq, "wq"), (wk, "wk"), (wv, "wv"), (wo, "wo")):
                sp.dma_start(t[:], a[n]).then_inc(s_w, 16)
            sp.dma_start(vec_rows[0:ACH, :], a["ab1"].rearrange("(c k) -> c k", k=P)).then_inc(s_w, 16)
            sp.dma_start(vec_rows[ACH:CHUNKS, :], a["eb1"].rearrange("e (c k) -> (e c) k", k=P)).then_inc(s_w, 16)
            for i, n in enumerate(("bq", "bk", "bo", "ln_g", "ln_b")):
                sp.dma_start(vec_rows[CHUNKS + i:CHUNKS + i + 1, :], a[n].rearrange("(o e) -> o e", o=1)).then_inc(s_w, 16)
            for t in range(TPB):
                sp.dma_start(bvb[:, t, :], a["bv"].rearrange("(o e) -> o e", o=1).to_broadcast([P, EMB])).then_inc(s_w, 16)
            sp.dma_start(x_keep[:, 2:8, :], a["x"][2:8].rearrange("t p e -> p t e")).then_inc(s_x[1], 16)
            sp.dma_start(gen[:], a["gens"].rearrange("g i j -> i g j")).then_inc(s_gen, 16)
            fl = [(aw1[:], a["aw1"]), (aw2[:], a["aw2"].rearrange("(c k) n -> k c n", k=P)),
                  (ew1[:], a["ew1"].rearrange("e d h -> d e h")), (ew2[:], a["ew2"].rearrange("e (c k) d -> k (e c) d", k=P)),
                  (eb2[:], a["eb2"]),
                  (ab2b[:], a["ab2"].rearrange("(o e) -> o e", o=1).to_broadcast([P, EMB])),
                  (gcwb[:].rearrange("p a e -> p (a e)"), a["gc_w"].rearrange("e o -> o e").to_broadcast([P, 2 * EMB])),
                  (gate_w[:], a["gate_w"]),
                  (gate_bb[:], a["gate_b"].rearrange("(o e) -> o e", o=1).to_broadcast([P, EXPERTS])),
                  (gcb[:], a["gc_b"].rearrange("(o e) -> o e", o=1).to_broadcast([P, 1]))]
            for dst, src in fl:
                sp.dma_start(dst, src).then_inc(f_w, 16)
            assert len(fl) == NF
            sp.dma_start(x_keep[:, 8:TILES, :], a["x"][8:TILES].rearrange("t p e -> p t e")).then_inc(s_x[2], 16)

            def max_dma(b, p, r):
                need(sp, max_row_ok, 2 * b + r + 1)
                for part in range(2):
                    sp.dma_start(q_stack[MAXROW + part:MAXROW + part + 1, p, 8 * r:8 * r + 8, :].bitcast(F32),
                                 max_rows[8 * part:8 * part + 8, r, :]).then_inc(max_in[r], 16)

            def stack_dma(b2, p, r):
                hs = slice(8 * r, 8 * r + 8)

                def load(stack, row, qk_i, p0, np_):
                    sp.dma_start(
                        stack[row:row + HDIM * np_, p, hs, :].bitcast(F32),
                        parts_dram[p, qk_i, p0:p0 + np_, :, hs, :].rearrange("a d h t -> (a d) h t")).then_inc(stack_in[r], 16)
                load(k_stack, 0, 1, 0, 2)
                load(k_stack, 2 * HDIM, 1, 0, 2)
                load(q_stack, 0, 0, 0, 2)
                load(q_stack, 2 * HDIM, 0, 1, 1)
                load(q_stack, 3 * HDIM, 0, 0, 1)

            def step(b, f, p):
                if 0 <= f < BATCH:
                    max_dma(b, p, 1)
                if 0 <= f + 2 < BATCH:
                    b2 = b + 2
                    need(sp, split_ok, b2 + 1)
                    need(sp, stack_in[1], 80 * b + 80)
                    for part in range(2):
                        for i in range(2):
                            sp.dma_start(parts_dram[p, i, part].rearrange("d h t -> h d t"),
                                         qk_parts[:, part, i, :].bitcast(F32)).then_inc(parts_out, 16)
                    sp.wait_ge(parts_out, 64 * b2 + 64)
                    if f == -2:
                        sp.wait_ge(s_stackzero, 3)
                    need(sp, st_done, 16 * b + 8)
                    stack_dma(b2, p, 0)
                if 0 <= f + 1 < BATCH:
                    max_dma(b + 1, 1 - p, 0)
                if 0 <= f + 2 < BATCH:
                    need(sp, st_done, 16 * b + 16)
                    stack_dma(b + 2, p, 1)

            iterations(sp, step)

            def ffn(q, f, p):
                if 0 <= f - 1 < BLOCKS:
                    sp.wait_ge(y_fin, q)
                    sp.dma_start(out[bass.ds(BT * (q - 1), BT)].rearrange("t p e -> p t e"), y_out[:, 1 - p]).then_inc(y_stored[1 - p], 16)
                if 0 <= f + 1 < BLOCKS:
                    q1 = q + 1
                    if f == -1:
                        sp.wait_ge(mr_dve, 6)
                        sp.dma_start(mod_dram, mod_rows[:]).then_inc(mr_out, 16)
                        sp.wait_ge(mr_out, 16)
                    need(sp, y_fin, q)
                    for i in range(2):
                        sp.dma_start(mod_b[:, 1 - p, i], mod_dram[bass.ds(2 * q1 + i, 1)].to_broadcast([P, 3, EMB])).then_inc(modb_in[1 - p], 16)
            for i in range(2):
                sp.sem_inc(y_stored[i], 16)
            blocks(sp, ffn)
            for i in range(2):
                sp.wait_ge(y_stored[i], 16 * BLOCKS // 2 + 16)

        @block.gpsimd
        def _(pool):
            pool.memset(ident[:], 0.0).then_inc(s_const, 1)
            pool.memset(ones[:], 1.0).then_inc(s_const, 1)
            pool.memset(neg_half[:], -0.5).then_inc(s_const, 1)
            pool.wait_ge(s_const, 3)
            pool.affine_select(out=ident[:], in_=ident[:], compare_op=ALU.not_equal, fill=1.0, base=0,
                               pattern=[[-1, P]], channel_multiplier=1).then_inc(s_const, 1)
            pool.wait_ge(s_const, 4)
            for g in range(NG):
                pool.tensor_copy(ident4[:, g, :], ident[:]).then_inc(s_const, 1)
            pool.memset(nh4[:], -0.5).then_inc(f_const, 1)
            pool.memset(tri[:], 1.0).then_inc(f_const, 1)
            pool.wait_ge(f_const, 2)
            pool.affine_select(out=tri[:], in_=tri[:], compare_op=ALU.is_gt, fill=0.0, base=0,
                               pattern=[[1, EXPERTS], [-1, EXPERTS]], channel_multiplier=0).then_inc(f_const, 1)
            pool.wait_ge(f_w, 16 * NF)
            pool.tensor_scalar(gcb_half[:], gcb[:], 0.5, None, ALU.mult).then_inc(f_const, 1)

            def step(b, f, p):
                if f == -2:
                    pool.memset(q_stack[:].bitcast(F32), 0.0).then_inc(s_stackzero, 1)
                if 0 <= f + 1 < BATCH:
                    b1, q = b + 1, 1 - p
                    if f == -1:
                        pool.memset(v_blocks[:], 0.0).then_inc(vb_zero, 1)
                        pool.wait_ge(vb_zero, 1)
                        for i in range(2):
                            for buf in range(2):
                                for t in range(TPB):
                                    v = v_blocks[:, buf, t].rearrange("k (m i) w -> k m i w", i=2)
                                    pool.memset(v[:, :, i, OW * i + HDIM:OW * i + OW], 1.0)
                    need(pool, v_ok, b1 + 1)
                    need(pool, pv_done, 4 * b)
                    settle(pool, p_settled)
                    for t in range(TPB):
                        dst = bass.AP(tensor=v_blocks, offset=v_blocks[:, q, t, 0, 0:1].offset,
                                      ap=[v_blocks[:].ap[0], [2 * VW, 8], [VW + OW, 2], [1, HDIM]])
                        last = pool.tensor_copy(dst, v_tok[:, t, :].rearrange("k (m i d) -> k m i d", i=2, d=HDIM))
                    last.then_inc(vb_ok, 1)
                if 0 <= f + 2 < BATCH:
                    b2 = b + 2
                    need(pool, qk_ok, b2 + 1)
                    need(pool, parts_out, 64 * b2)
                    settle(pool, p_settled)
                    pool.tensor_copy(qk_parts[:, 0], qk[:]).then_inc(p_hi, 1)
                    pool.wait_ge(p_hi, b2 + 1)
                    pool.tensor_tensor(qk_parts[:, 1], qk[:], qk_parts[:, 0].bitcast(F32), ALU.subtract).then_inc(split_ok, 1)
                if 0 <= f + 3 < BATCH:
                    b3 = b + 3
                    pool.wait_ge(stat_ok, b3 + 1)
                    settle(pool, p_settled)
                    pool.tensor_scalar(var_eps[:], mv[:, :, 1], EPS, None, ALU.add).then_inc(p_var, 1)
                    pool.wait_ge(p_var, b3 + 1)
                    pool.tensor_tensor(rstd[:], var_eps[:], neg_half[:], ALU.pow).then_inc(p_rs, 1)
                    pool.wait_ge(p_rs, b3 + 1)

            iterations(pool, step)

            def rstd_of(k, q1):
                pool.wait_ge(n_mv, 2 * q1 + k + 1)
                settle(pool, p_settled)
                pool.tensor_scalar(ve2[:, k], mv2[:, k, :, 1], EPS, None, ALU.add).then_inc(n_var, 1)
                pool.wait_ge(n_var, 2 * q1 + k + 1)
                pool.tensor_tensor(rs2[:, k], ve2[:, k], nh4[:], ALU.pow).then_inc(n_rs, 1)

            def ffn(q, f, p):
                if 0 <= f - 1 < BLOCKS:
                    q0, r = q - 1, 1 - p
                    pool.wait_ge(acc_ok, EXPERTS * q)
                    pool.wait_ge(abel_ok, q)
                    need(pool, mix_ok, q0)
                    pool.tensor_tensor(diff[:], acc[:, r], abel[:, r], ALU.subtract).then_inc(diff_ok, 1)
                    pool.wait_ge(mix_ok, q)
                    pool.tensor_tensor(y_out[:, r], y_out[:, r], h2[:, r], ALU.add).then_inc(res1, 1)
                    pool.wait_ge(res1, q)
                    y4 = y_out[:, r].rearrange("p (b t) e -> p b t e", b=2)
                    pool.tensor_tensor(y4, y4, mod_b[:, r, :, 2:3, :].to_broadcast([P, 2, BT // 2, EMB]), ALU.mult).then_inc(res2, 1)
                    pool.wait_ge(res2, q)
                    pool.tensor_tensor(y_out[:, r], y_out[:, r], x_keep[:, bass.ds(BT * q0, BT), :], ALU.add).then_inc(y_fin, 1)
                if 0 <= f + 1 < BLOCKS:
                    q1, r = q + 1, 1 - p
                    rstd_of(0, q1)
                    pool.wait_ge(modb_in[r], 16 * (q1 - r) + 32)
                    pool.wait_ge(n_hat, q1 + 1)
                    h4 = h2[:, r].rearrange("p (b t) e -> p b t e", b=2)

                    def over(j):
                        return mod_b[:, r, :, j:j + 1, :].to_broadcast([P, 2, BT // 2, EMB])
                    pool.tensor_tensor(h4, h4, over(1), ALU.mult).then_inc(n_mul, 1)
                    pool.wait_ge(n_mul, q1 + 1)
                    pool.tensor_tensor(h4, h4, over(0), ALU.add).then_inc(h2_ok, 1)
                    rstd_of(1, q1)

            blocks(pool, ffn)

        @block.scalar
        def _(act):
            act.wait_ge(s_w, 16 * NW)
            act.activation(c_exp[:], c_row[:], ACT.Exp, scale=-1.0).then_inc(c1, 1)
            act.wait_ge(c3, 1)
            act.activation(vec_cols[:], mx[:, 32:32 + NVEC], ACT.Identity)
            act.activation(c_t[:], mx[:, 0:BATCH], ACT.Identity).then_inc(c4, 1)
            act.wait_ge(s_gen, 16)
            act.activation(gen_abs[:], gen[:], ACT.Abs).then_inc(g_abs, 1)

            def step(b, f, p):
                live = 0 <= f < BATCH

                def expo(n):
                    need(act, st_done, 16 * b + n + 1)
                    need(act, pv_done, 4 * b + n // 4 - 1)
                    act.activation(prob[:, n % 8, :], st_bank[n % 2][:], ACT.Exp, scale=SCALE).then_inc(exp_done, 1)

                for n in range(HEADS):
                    if live:
                        expo(n)
                    if n == 0 and 0 <= f + 2 < BATCH:
                        act.wait_ge(xt_done, b + 3)
                        if f == -2:
                            act.wait_ge(mod_dve, 6)
                        act.activation(h_t[:], mx[:, 0:SEQ], ACT.Identity, scale=mod_t[:, 1, bass.ds(b + 2, 1)],
                                       bias=mod_t[:, 0, bass.ds(b + 2, 1)]).then_inc(h_ok, 1)
                    if n == 3 and 0 <= f + 2 < BATCH:
                        act.wait_ge(qk_done, b + 3)
                        need(act, split_ok, b + 2)
                        for i in range(2):
                            last = act.activation(qk[:, i, :], mx[:, SEQ * i:SEQ * (i + 1)], ACT.Identity, bias=cols[:, i:i + 1])
                        last.then_inc(qk_ok, 1)
                    if n == 2 and 0 <= f - 1 < BATCH:
                        act.wait_ge(pv_done, 4 * b)
                        act.activation(o_raw[:, 1, :], pv_bank[1][:, 0:SEQ], ACT.Identity).then_inc(oraw_ok, 1)
                    if n == 6 and 0 <= f - 1 < BATCH:
                        act.wait_ge(ot2_done, b)
                        act.activation(o_t[:], my[:, 0:SEQ], ACT.Identity).then_inc(ot_ok, 1)
                    if n == 7 and 0 <= f - 1 < BATCH:
                        act.wait_ge(y_done, b)
                        act.activation(y_t[:], mx[:, 0:SEQ], ACT.Identity, scale=mod_t[:, 2, bass.ds(b - 1, 1)],
                                       bias=gate_bo[:, bass.ds(b - 1, 1)]).then_inc(y_ok, 1)
                    if n == 10 and live:
                        act.wait_ge(pv_done, 4 * b + 2)
                        act.activation(o_raw[:, 0, :], pv_bank[0][:, 0:SEQ], ACT.Identity).then_inc(oraw_ok, 1)
                    if n == 13 and live:
                        act.wait_ge(sqt_done, b + 1)
                        act.activation(rot_t[:], mx[:].rearrange("p (g j) -> p g j", g=NG), ACT.Identity).then_inc(rott_ok, 1)

            act.wait_ge(g_tpe, 1)
            act.activation(gen_t[:], my[:].rearrange("p (g j) -> p g j", g=NG), ACT.Identity).then_inc(g_tok, 1)
            iterations(act, step)

            act.wait_ge(rt_done, 1)
            act.activation(rot_t[:], mx[:].rearrange("p (g j) -> p g j", g=NG), ACT.Identity).then_inc(rt_ok, 1)

            def ffn(q, f, p):
                def front(n):
                    q1 = q + 1
                    if n == 10:
                        act.wait_ge(fxt_done, q1 + 1)
                        act.activation(xn_t[:, 1 - p], mx[:], ACT.Identity, scale=lnc[:, 0:1], bias=lnc[:, 1:2]).then_inc(xnt_ok, 1)
                    if n == 13:
                        act.wait_ge(d_ok, q1 + 1)
                        act.activation(th[:], top[:, 2], ACT.Tanh, scale=0.5).then_inc(th_ok, 1)
                for c in range(CHUNKS):
                    if 0 <= f < BLOCKS:
                        need(act, m2_done, CHUNKS * q + c - 3)
                        act.wait_ge(m1_done, CHUNKS * q + c + 1)
                        act.activation(hid[:, c % 4, :], smax_bank[c % 2][:], ACT.Gelu, bias=b1c[:, c:c + 1]).then_inc(gelu_ok, 1)
                    if 0 <= f + 1 < BLOCKS:
                        front(c)
                    if c == 2 and 0 <= f - 1 < BLOCKS:
                        act.wait_ge(z_ok, q)
                        act.activation(gth[:], zsum[:], ACT.Tanh, scale=0.5, bias=gcb_half[:]).then_inc(zth_ok, 1)

            act.wait_ge(f_const, 4)
            blocks(act, ffn)

        @block.tensor
        def _(pe):
            pe.wait_ge(s_const, 8)
            pe.wait_ge(c2, 3)
            pe.wait_ge(s_w, 16 * NW)
            pe.transpose(mx[:, 32:32 + NVEC], vec_rows[:], ident[0:NVEC, 0:NVEC])
            pe.transpose(mx[:, 0:BATCH], c_silu[:], ident[0:BATCH, 0:BATCH]).then_inc(c3, 1)
            pe.wait_ge(c4, 1)
            pe.matmul(mx[0:BATCH, 128:128 + 3 * EMB], c_t[:], wmod[:, 3 * EMB:6 * EMB], start=True, stop=True).then_inc(mr_pe, 1)
            for j in range(3):
                last = pe.matmul(mx[:, 32 + BATCH * j:32 + BATCH * (j + 1)], wmod[:, EMB * j:EMB * (j + 1)], c_t[:], start=True, stop=True)
            last.then_inc(mod_pe, 1)
            pe.wait_ge(g_abs, 1)
            pe.matmul(my[:], ones[:], gen_abs[:].rearrange("p g j -> p (g j)"), start=True, stop=True).then_inc(g_sum, 1)
            pe.wait_ge(g_dve, 8)
            for g in range(NG):
                last = pe.transpose(my[:, P * g:P * (g + 1)], gen[:, g, :], ident[:])
            last.then_inc(g_tpe, 1)
            for k in range(TAYLOR):
                pe.wait_ge(g_tok, 1)
                if k:
                    pe.wait_ge(g_acc, k)
                for g in range(NG):
                    last = pe.matmul(my[:, P * g:P * (g + 1)], gen_t[:, g, :], (rot if k else ident4)[:, g, :], start=True, stop=True)
                last.then_inc(g_mm, 1)

            def pv(b, p, g):
                r, i = g // 2, g % 2
                if g == 0:
                    pe.wait_ge(vb_ok, b + 1)
                if i == 0:
                    need(pe, oraw_ok, 2 * b - 1 + r)
                pe.wait_ge(exp_done, 16 * b + 4 * g + 4)
                for t in range(TPB):
                    for j in range(4):
                        last = pe.matmul(pv_bank[r][VW * j:VW * (j + 1), 0:SEQ], v_blocks[:, p, t, 8 * r + 2 * j + i, :],
                                         prob[:, (4 * g + j) % 8, SEQ * t:SEQ * (t + 1)],
                                         start=(i == 0 and t == 0), stop=(i == 1 and t == TPB - 1))
                last.then_inc(pv_done, 1)

            def o_transposes(b, r, bank):
                pe.wait_ge(oraw_ok, 2 * b + r + 1)
                for t in range(TPB):
                    last = pe.transpose(bank[:, P * t:P * (t + 1)], o_raw[:, r, P * t:P * (t + 1)], ident[:])
                last.then_inc(ot1_done, 1)

            def max_transposes(b, p, r, bank):
                pe.wait_ge(max_split, 2 * b + r + 1)
                for t in range(TPB):
                    last = pe.transpose(bank[0:16, P * t:P * (t + 1)], max_parts[:, r, t].bitcast(F32).rearrange("p a h -> p (a h)"), ident[:])
                last.then_inc(mt_done, 1)

            def step(b, f, p):
                live, smax, pre, post = 0 <= f < BATCH, 0 <= f + 1 < BATCH, 0 <= f + 2 < BATCH, 0 <= f - 1 < BATCH
                for n in range(HEADS):
                    if smax:
                        if n % 8 == 0:
                            pe.wait_ge(stack_in[n // 8], 80 * (b + 2))
                        need(pe, red_done, 16 * (b + 1) + n - 1)
                        for t in range(TPB):
                            last = pe.matmul(smax_bank[n % 2][:, SEQ * t:SEQ * (t + 1)],
                                             q_stack[0:MAXROW, 1 - p, n, P * t:P * (t + 1)],
                                             k_stack[0:MAXROW, 1 - p, n, :], start=True, stop=True)
                        last.then_inc(smax_done, 1)
                    if live:
                        h = head_at(n)
                        if n % 8 == 0:
                            pe.wait_ge(max_in[n // 8], 32 * (b + 1))
                        need(pe, exp_done, 16 * b + n - 1)
                        for t in range(TPB):
                            last = pe.matmul(st_bank[n % 2][:, SEQ * t:SEQ * (t + 1)], k_stack[:, p, h, P * t:P * (t + 1)],
                                             q_stack[:, p, h, :], start=True, stop=True)
                        last.then_inc(st_done, 1)
                    if n == 0 and pre:
                        pe.wait_ge(xhat_ok, b + 3)
                        need(pe, rott_ok, b)
                        if f == -2:
                            pe.wait_ge(mod_ok, 1)
                        for t in range(TPB):
                            last = pe.transpose(mx[:, P * t:P * (t + 1)], xhat[:, t, :], ident[:])
                        last.then_inc(xt_done, 1)
                    if n == 1 and live:
                        need(pe, rot_ok, b)
                        max_transposes(b, p, 1, my)
                    if n == 1 and post:
                        pv(b - 1, 1 - p, 3)
                    if n == 2 and pre:
                        pe.wait_ge(h_ok, b + 3)
                        for i, w in enumerate((wq, wk)):
                            last = pe.matmul(mx[:, SEQ * i:SEQ * (i + 1)], w[:], h_t[:], start=True, stop=True)
                        last.then_inc(qk_done, 1)
                    if n == 3 and pre:
                        if f == -2:
                            pe.wait_ge(g_acc, TAYLOR)
                        if f == -1:
                            pe.wait_ge(v_ok, 1)
                        need(pe, max_row_ok, 2 * b + 2)
                        for t in range(TPB):
                            last = pe.matmul(my[:, EMB * t:EMB * (t + 1)], h_t[:, P * t:P * (t + 1)], wv[:], start=True, stop=True)
                        last.then_inc(v_done, 1)
                    if n == 4 and post:
                        need(pe, qk_ok, b + 3 if pre else BATCH)
                        need(pe, rott_ok, b)
                        o_transposes(b - 1, 1, mx)
                    if n == 5 and post:
                        pe.wait_ge(o_norm, 2 * b)
                        need(pe, v_ok, b + 3 if pre else BATCH)
                        need(pe, max_row_ok, 2 * b + 2 if live else 2 * BATCH)
                        need(pe, rot_ok, b)
                        for t in range(TPB):
                            last = pe.transpose(my[:, P * t:P * (t + 1)], o_tok[:, t, :], ident[:])
                        last.then_inc(ot2_done, 1)
                    if n == 5 and live:
                        pv(b, p, 0)
                    if n == 6 and post:
                        pe.wait_ge(ot_ok, b)
                        pe.matmul(mx[:, 0:SEQ], wo[:], o_t[:], start=True, stop=True).then_inc(y_done, 1)
                    if n == 7 and post:
                        pe.wait_ge(y_ok, b)
                        for t in range(TPB):
                            last = pe.transpose(my[:, P * t:P * (t + 1)], y_t[:, P * t:P * (t + 1)], ident[:])
                        last.then_inc(yt_done, 1)
                    if n == 9 and live:
                        pv(b, p, 1)
                    if n == 9 and smax:
                        need(pe, y_ok, b)
                        need(pe, qk_ok, b + 3 if pre else BATCH)
                        max_transposes(b + 1, 1 - p, 0, mx)
                    if n == 11 and live:
                        need(pe, x1_ok, b)
                        need(pe, v_ok, b + 3 if pre else BATCH)
                        need(pe, max_row_ok, 2 * b + 2)
                        o_transposes(b, 0, my)
                    if n == 12 and live:
                        need(pe, max_row_ok, 2 * b + 3 if smax else 2 * BATCH)
                        need(pe, y_ok, b)
                        if f == 0:
                            pe.wait_ge(g_acc, TAYLOR)
                        need(pe, rot_ok, b)
                        for g in range(NG):
                            last = pe.transpose(mx[:, P * g:P * (g + 1)], rot[:, g, :], ident[:])
                        last.then_inc(sqt_done, 1)
                    if n == 13 and live:
                        pv(b, p, 2)
                    if n == 14 and live:
                        pe.wait_ge(rott_ok, b + 1)
                        pe.wait_ge(o_norm, 2 * b + 1)
                        for g in range(NG):
                            last = pe.matmul(my[:, P * g:P * (g + 1)], rot_t[:, g, :], rot[:, g, :], start=True, stop=True)
                        last.then_inc(sq_done, 1)

            iterations(pe, step)

            pe.wait_ge(rot_ok, BATCH)
            pe.wait_ge(y_ok, BATCH)
            for g in range(NG):
                last = pe.transpose(mx[:, P * g:P * (g + 1)], rot[:, g, :], ident[:])
            last.then_inc(rt_done, 1)
            pe.wait_ge(f_w, 16 * NF)
            for k in range(ECH // 4):
                pe.wait_ge(x1_ok, BATCH)
                need(pe, e2t_ok, k)
                for c in range(4):
                    last = pe.transpose(my[:, P * c:P * (c + 1)], ew2[:, 4 * k + c, :], ident[:])
                last.then_inc(e2t_done, 1)
            pe.wait_ge(e2t_ok, 3)
            pe.transpose(my[:, 0:EXPERTS], eb2[:], ident[0:EXPERTS, 0:EXPERTS]).then_inc(e2t_done, 1)
            pe.wait_ge(rt_ok, 1)
            for k in range(NG - 1):
                need(pe, rp_ok, k)
                pe.matmul(mx[:, 0:P], rot_t[:, NG - 2 - k, :], rot[:, NG - 1, :] if k == 0 else rot_all[:, k - 1, :],
                          start=True, stop=True).then_inc(rp_done, 1)
            pe.wait_ge(rp_ok, NG - 1)
            pe.wait_ge(e2t_ok, 4)
            for k in range(ECH // 4):
                need(pe, er_ok, k)
                for c in range(4):
                    last = pe.matmul(mx[:, P * c:P * (c + 1)], ew2_t[:, 4 * k + c, :], rot_all[:, NG - 2, :], start=True, stop=True)
                last.then_inc(er_done, 1)
            pe.wait_ge(er_ok, 3)
            pe.matmul(mx[0:EXPERTS, 0:EMB], eb2_t[:], rot_all[:, NG - 2, :], start=True, stop=True).then_inc(er_done, 1)
            pe.wait_ge(er_ok, 4)

            def m2(q, p, c):
                pe.wait_ge(gelu_ok, CHUNKS * q + c + 1)
                if c < ACH:
                    bank, w, first, final = pv_bank[0], aw2[:, c, :], c == 0, c == ACH - 1
                    if first:
                        need(pe, abel_ok, q)
                else:
                    e = (c - ACH) // 2
                    bank, w, first, final = st_bank[e % 2], ew2_rot[:, c - ACH, :], c % 2 == 0, c % 2 == 1
                    if first:
                        need(pe, acc_ok, EXPERTS * q + e - 1)
                for t in range(BT):
                    last = pe.matmul(bank[:, EMB * t:EMB * (t + 1)], hid[:, c % 4, P * t:P * (t + 1)], w,
                                     start=first and t == 0, stop=final, skip_group_check=True)
                last.then_inc(m2_done, 1)

            def ffn(q, f, p):
                live, front, = 0 <= f < BLOCKS, 0 <= f + 1 < BLOCKS
                for c in range(CHUNKS):
                    if live:
                        if c == 0:
                            pe.wait_ge(xnt_ok, q + 1)
                        need(pe, gelu_ok, CHUNKS * q + c - 1)
                        w = aw1[:, P * c:P * (c + 1)] if c < ACH else ew1[:, (c - ACH) // 2, P * (c % 2):P * (c % 2 + 1)]
                        pe.matmul(smax_bank[c % 2][:], w, xn_t[:, p], start=True, stop=True).then_inc(m1_done, 1)
                    if c == 0:
                        if 0 <= f - 1 < BLOCKS:
                            m2(q - 1, 1 - p, CHUNKS - 1)
                    elif live:
                        m2(q, p, c - 1)
                    if front:
                        q1 = q + 1
                        if c == 10:
                            pe.wait_ge(xn_ok, q1 + 1)
                            need(pe, wt_ok, q1)
                            for t in range(BT):
                                last = pe.transpose(mx[:, P * t:P * (t + 1)], xn_tok[:, t, :], ident[:])
                            last.then_inc(fxt_done, 1)
                        if c == 12:
                            pe.wait_ge(xnt_ok, q1 + 1)
                            need(pe, acc0_ok, q1)
                            for t in range(BT):
                                last = pe.matmul(my[:, 8 * t:8 * t + EXPERTS], xn_t[:, 1 - p, P * t:P * (t + 1)], gate_w[:], start=True, stop=True)
                            last.then_inc(lg_done, 1)
                    if live and c == 1:
                        pe.wait_ge(w_ok, q + 1)
                        for t in range(BT):
                            last = pe.transpose(mx[0:EXPERTS, P * t:P * (t + 1)], w_gate[:, p, t, :], ident[:])
                        last.then_inc(wt_done, 1)
                    if live and c == 3:
                        pe.wait_ge(wt_ok, q + 1)
                        for t in range(BT):
                            last = pe.matmul(my[:, EMB * t:EMB * (t + 1)], w_t[:, P * t:P * (t + 1)], eb2_rot[:], start=True, stop=True)
                        last.then_inc(ai_done, 1)

            blocks(pe, ffn)

        @block.vector
        def _(dve):
            dve.wait_ge(c1, 1)
            dve.tensor_scalar(c_exp[:], c_exp[:], 1.0, None, ALU.add).then_inc(c2, 1)
            dve.wait_ge(c2, 1)
            dve.reciprocal(c_sig[:], c_exp[:]).then_inc(c2, 1)
            dve.wait_ge(c2, 2)
            dve.tensor_tensor(c_silu[:], c_row[:], c_sig[:], ALU.mult).then_inc(c2, 1)
            dve.wait_ge(mod_pe, 1)
            dve.wait_ge(mr_pe, 1)
            dve.tensor_copy(mod_t[:], mx[:, 32:32 + 3 * BATCH].rearrange("p (j b) -> p j b", j=3)).then_inc(mod_ok, 1)
            dve.wait_ge(mod_ok, 1)
            dve.tensor_scalar(tmp_t[:, 1, :], mod_t[:, 2, :], 0.0, None, ALU.is_ge).then_inc(mod_dve, 1)
            dve.wait_ge(mod_dve, 1)
            dve.tensor_scalar(tmp_t[:, 1, :], tmp_t[:, 1, :], 2.0, -1.0, ALU.mult, ALU.add).then_inc(mod_dve, 1)
            dve.wait_ge(mod_dve, 2)
            dve.tensor_tensor(tmp_t[:, 0, :], mod_t[:, 2, :], tmp_t[:, 1, :], ALU.mult).then_inc(mod_dve, 1)
            dve.wait_ge(mod_dve, 3)
            dve.scalar_tensor_tensor(out=mod_t[:, 2, :], in0=tmp_t[:, 0, :], scalar=0.25, in1=tmp_t[:, 1, :],
                                     op0=ALU.max, op1=ALU.mult).then_inc(mod_dve, 1)
            dve.tensor_scalar(mod_t[:, 1, :], mod_t[:, 1, :], 1.0, None, ALU.add).then_inc(mod_dve, 1)
            dve.wait_ge(mod_dve, 5)
            dve.wait_ge(c4, 1)
            dve.tensor_copy(mod_rows[:], mx[0:BATCH, 128:128 + 3 * EMB].rearrange("p (j e) -> p j e", j=3)).then_inc(mr_dve, 1)
            dve.wait_ge(mr_dve, 1)
            dve.tensor_scalar(mod_tmp[:, 1, :], mod_rows[:, 2, :], 0.0, None, ALU.is_ge).then_inc(mr_dve, 1)
            dve.wait_ge(mr_dve, 2)
            dve.tensor_scalar(mod_tmp[:, 1, :], mod_tmp[:, 1, :], 2.0, -1.0, ALU.mult, ALU.add).then_inc(mr_dve, 1)
            dve.wait_ge(mr_dve, 3)
            dve.tensor_tensor(mod_tmp[:, 0, :], mod_rows[:, 2, :], mod_tmp[:, 1, :], ALU.mult).then_inc(mr_dve, 1)
            dve.wait_ge(mr_dve, 4)
            dve.scalar_tensor_tensor(out=mod_rows[:, 2, :], in0=mod_tmp[:, 0, :], scalar=0.25, in1=mod_tmp[:, 1, :],
                                     op0=ALU.max, op1=ALU.mult).then_inc(mr_dve, 1)
            dve.tensor_scalar(mod_rows[:, 1, :], mod_rows[:, 1, :], 1.0, None, ALU.add).then_inc(mr_dve, 1)
            dve.tensor_scalar(gate_bo[:], mod_t[:, 2, :], cols[:, 2:3], None, ALU.mult).then_inc(mod_dve, 1)
            dve.memset(k_stack[:].bitcast(F32), 0.0).then_inc(s_stackzero, 1)
            dve.wait_ge(s_stackzero, 1)
            dve.memset(k_stack[MAXROW:MAXROW + 2].bitcast(F32), 1.0).then_inc(s_stackzero, 1)
            dve.wait_ge(g_sum, 1)
            dve.tensor_reduce(nrm[:], my[:].rearrange("p (g j) -> p g j", g=NG), AX_X, ALU.max).then_inc(g_dve, 1)
            dve.wait_ge(g_dve, 1)
            dve.tensor_scalar(nrm[:], nrm[:], 2.0, 2.0 ** -100, ALU.mult, ALU.max).then_inc(g_dve, 1)
            dve.wait_ge(g_dve, 2)
            dve.tensor_scalar(nrm[:].bitcast(U32), nrm[:].bitcast(U32), 0x7F800000, None, ALU.bitwise_and).then_inc(g_dve, 1)
            dve.wait_ge(g_dve, 3)
            dve.reciprocal(gscale[:], nrm[:]).then_inc(g_dve, 1)
            dve.wait_ge(g_dve, 4)
            dve.tensor_scalar(gscale[:], gscale[:], 1.0, 2.0 ** -SQUARINGS, ALU.min, ALU.max).then_inc(g_dve, 1)
            dve.wait_ge(g_dve, 5)
            for g in range(NG):
                last = dve.tensor_scalar(gen[:, g, :], gen[:, g, :], gscale[:, g:g + 1], None, ALU.mult)
            last.then_inc(g_dve, 3)
            dve.wait_ge(s_const, 8)
            for k in range(TAYLOR):
                dve.wait_ge(g_mm, k + 1)
                dve.scalar_tensor_tensor(out=rot[:].rearrange("p g j -> p (g j)"), in0=my[:], scalar=1.0 / (TAYLOR - k),
                                         in1=ident4[:].rearrange("p g j -> p (g j)"), op0=ALU.mult, op1=ALU.add).then_inc(g_acc, 1)

            def split_max(b, p, r):
                hs = slice(8 * r, 8 * r + 8)
                dve.wait_ge(red_done, 16 * b + 8 * r + 8)
                need(dve, mt_done, 2 * b - 1 + r)
                dve.tensor_scalar(max_parts[:, r, :, 0, :], row_max[:, p, :, hs], -1.0, None, ALU.mult).then_inc(d_mhi, 1)
                dve.wait_ge(d_mhi, 2 * b + r + 1)
                dve.scalar_tensor_tensor(out=max_parts[:, r, :, 1, :], in0=row_max[:, p, :, hs], scalar=-1.0,
                                         in1=max_parts[:, r, :, 0, :].bitcast(F32), op0=ALU.mult, op1=ALU.subtract).then_inc(max_split, 1)

            def max_row(b, r, bank):
                dve.wait_ge(mt_done, 2 * b + r + 1)
                need(dve, max_in[r], 32 * b)
                dve.tensor_copy(max_rows[:, r, :], bank[0:16, 0:SEQ]).then_inc(max_row_ok, 1)

            def normalise(b, r, bank):
                dve.wait_ge(ot1_done, 2 * b + r + 1)
                o = bank[:, 0:SEQ].rearrange("p (m w) -> p m w", w=VW)[:, :, 0:2 * OW].rearrange("p m (i d) -> p m i d", i=2)
                dve.reciprocal(o_rsum[:, r, :].rearrange("p (m i) -> p m i", i=2), o[:, :, :, HDIM]).then_inc(d_rs, 1)
                dve.wait_ge(d_rs, 2 * b + r + 1)
                need(dve, ot2_done, b)
                dve.tensor_tensor(o_tok[:, :, 64 * r:64 * r + 64].rearrange("p t (j i d) -> p t j i d", i=2, d=HDIM),
                                  o[:, :, :, 0:HDIM].rearrange("p (t j) i d -> p t j i d", t=TPB),
                                  o_rsum[:, r, :].rearrange("p (t j i o) -> p t j i o", t=TPB, i=2, o=1).to_broadcast([P, TPB, 4, 2, HDIM]),
                                  ALU.mult).then_inc(o_norm, 1)

            def step(b, f, p):
                live, smax, pre, post = 0 <= f < BATCH, 0 <= f + 1 < BATCH, 0 <= f + 2 < BATCH, 0 <= f - 1 < BATCH
                if live:
                    split_max(b, p, 1)
                for n in range(HEADS):
                    if smax:
                        dve.wait_ge(smax_done, 16 * (b + 1) + n + 1)
                        dve.tensor_reduce(row_max[:, 1 - p, :, n], smax_bank[n % 2][:].rearrange("p (t k) -> p t k", t=TPB),
                                          AX_X, ALU.max).then_inc(red_done, 1)
                    if n == 1 and live:
                        max_row(b, 1, my)
                    if n == 4 and pre:
                        dve.wait_ge(v_done, b + 3)
                        need(dve, vb_ok, b + 2)
                        dve.tensor_tensor(v_tok[:], my[:, 0:SEQ].rearrange("p (t e) -> p t e", t=TPB), bvb[:], ALU.add).then_inc(v_ok, 1)
                    if n == 5 and post:
                        normalise(b - 1, 1, mx)
                    if n == 8 and post:
                        dve.wait_ge(yt_done, b)
                        xs = x_keep[:, bass.ds(TPB * (b - 1), TPB), :]
                        dve.tensor_tensor(xs, my[:, 0:SEQ].rearrange("p (t e) -> p t e", t=TPB), xs, ALU.add).then_inc(x1_ok, 1)
                    if n == 8 and smax:
                        split_max(b + 1, 1 - p, 0)
                    if n == 10 and smax:
                        max_row(b + 1, 0, mx)
                    if n == 12 and live:
                        normalise(b, 0, my)
                    if n == 13 and 0 <= f + 3 < BATCH:
                        b3 = b + 3
                        if f in (-3, -2, 0):
                            dve.wait_ge(s_x[(-3, -2, 0).index(f)], 16)
                        need(dve, xhat_ok, b3)
                        for t in range(TPB):
                            last = dve.bn_stats(stats[:, t, :], x_keep[:, bass.ds(TPB * b3 + t, 1), :].rearrange("p o e -> p (o e)"))
                        last.then_inc(d_bn, 1)
                        dve.wait_ge(d_bn, b3 + 1)
                        settle(dve, d_settled)
                        for t in range(TPB):
                            last = dve.bn_aggr(mv[:, t, :], stats[:, t, :])
                        last.then_inc(stat_ok, 1)
                    if n == 15 and 0 <= f + 3 < BATCH:
                        b3 = b + 3
                        dve.wait_ge(p_rs, b3 + 1)
                        need(dve, xt_done, b3)
                        for t in range(TPB):
                            last = dve.tensor_scalar(xhat[:, t, :], x_keep[:, bass.ds(TPB * b3 + t, 1), :].rearrange("p o e -> p (o e)"),
                                                     mv[:, t, 0:1], rstd[:, t:t + 1], ALU.subtract, ALU.mult)
                        last.then_inc(xhat_ok, 1)
                    if n == 14 and live:
                        dve.tensor_scalar(todo[:], gscale[:], 0.75, None, ALU.is_lt).then_inc(d_sq, 1)
                        dve.wait_ge(d_sq, 2 * b + 1)
                        dve.scalar_tensor_tensor(out=gscale[:], in0=todo[:], scalar=1.0, in1=gscale[:], op0=ALU.add, op1=ALU.mult).then_inc(d_sq, 1)
                    if n == 15 and live:
                        dve.wait_ge(sq_done, b + 1)
                        dve.wait_ge(d_sq, 2 * b + 2)
                        settle(dve, d_settled)
                        dve.copy_predicated(out=rot[:], mask=todo[:].bitcast(U32).rearrange("p (g o) -> p g o", o=1).to_broadcast([P, NG, P]),
                                            data=my[:].rearrange("p (g j) -> p g j", g=NG)).then_inc(rot_ok, 1)

            iterations(dve, step)

            for k in range(ECH // 4):
                dve.wait_ge(e2t_done, k + 1)
                dve.tensor_copy(ew2_t[:, 4 * k:4 * k + 4, :], my[:].rearrange("p (c j) -> p c j", c=4)).then_inc(e2t_ok, 1)
            dve.wait_ge(e2t_done, 4)
            dve.tensor_copy(eb2_t[:], my[:, 0:EXPERTS]).then_inc(e2t_ok, 1)
            for k in range(NG - 1):
                dve.wait_ge(rp_done, k + 1)
                dve.tensor_copy(rot_all[:, k, :], mx[:, 0:P]).then_inc(rp_ok, 1)
            for k in range(ECH // 4):
                dve.wait_ge(er_done, k + 1)
                dve.tensor_copy(ew2_rot[:, 4 * k:4 * k + 4, :], mx[:].rearrange("p (c j) -> p c j", c=4)).then_inc(er_ok, 1)
            dve.wait_ge(er_done, 4)
            dve.tensor_copy(eb2_rot[:], mx[0:EXPERTS, 0:EMB]).then_inc(er_ok, 1)

            def norm(k, q1, src, dst, ready):
                for t in range(BT):
                    last = dve.bn_stats(st2[:, k, t, :], src(t))
                last.then_inc(n_bn, 1)
                dve.wait_ge(n_bn, 2 * q1 + k + 1)
                settle(dve, d_settled)
                for t in range(BT):
                    last = dve.bn_aggr(mv2[:, k, t, :], st2[:, k, t, :])
                last.then_inc(n_mv, 1)
                dve.wait_ge(n_rs, 2 * q1 + k + 1)
                for t in range(BT):
                    last = dve.tensor_scalar(dst(t), src(t), mv2[:, k, t, 0:1], rs2[:, k, t:t + 1], ALU.subtract, ALU.mult)
                last.then_inc(ready, 1)

            FD = 11

            def ffn(q, f, p):
                def front(c):
                    q1, r = q + 1, 1 - p
                    if c == 6:
                        need(dve, y_fin, q)
                        norm(0, q1, lambda t: x_keep[:, bass.ds(BT * q1 + t, 1), :].rearrange("p o e -> p (o e)"),
                             lambda t: h2[:, r, t, :], n_hat)
                    if c == 8:
                        dve.wait_ge(h2_ok, q1 + 1)
                        need(dve, fxt_done, q1)
                        norm(1, q1, lambda t: h2[:, r, t, :], lambda t: xn_tok[:, t, :], xn_ok)
                    if c == 12:
                        n = [FD * q1]

                        def then(ins):
                            ins.then_inc(fd, 1)
                            n[0] = n[0] + 1
                            dve.wait_ge(fd, n[0])
                        dve.wait_ge(lg_done, q1 + 1)
                        then(dve.tensor_tensor(lg[:], my[:, 0:8 * BT].rearrange("p (t e) -> p t e", t=BT)[:, :, 0:EXPERTS],
                                               gate_bb[:].rearrange("p (o e) -> p o e", o=1).to_broadcast([P, BT, EXPERTS]), ALU.add))
                        other = lg[:].rearrange("p t (o e) -> p t o e", o=1).to_broadcast([P, BT, EXPERTS, EXPERTS])
                        own = lg[:].rearrange("p t (e o) -> p t e o", o=1).to_broadcast([P, BT, EXPERTS, EXPERTS])
                        dve.tensor_tensor(cmp_gt[:], other, own, ALU.is_gt)
                        then(dve.tensor_tensor(cmp_eq[:], other, own, ALU.is_equal))
                        then(dve.tensor_tensor(cmp_eq[:], cmp_eq[:], tri[:].rearrange("p (o e) g -> p o e g", o=1).to_broadcast([P, BT, EXPERTS, EXPERTS]), ALU.mult))
                        then(dve.tensor_tensor(cmp_gt[:], cmp_gt[:], cmp_eq[:], ALU.add))
                        then(dve.tensor_reduce(rank[:], cmp_gt[:], AX_X, ALU.add))
                        dve.tensor_scalar(sel[:, 0], rank[:], 0.0, None, ALU.is_equal)
                        then(dve.tensor_scalar(sel[:, 1], rank[:], 1.0, None, ALU.is_equal))
                        then(dve.tensor_tensor(pick[:], lg[:], sel[:, 1], ALU.mult))
                        dve.tensor_reduce(top[:, 1], pick[:], AX_X, ALU.add)
                        then(dve.tensor_reduce(top[:, 0], lg[:], AX_X, ALU.max))
                        dve.tensor_tensor(top[:, 2], top[:, 0], top[:, 1], ALU.subtract).then_inc(d_ok, 1)
                    if c == 14:
                        dve.wait_ge(th_ok, q1 + 1)
                        dve.tensor_tensor(pick[:], sel[:, 0], sel[:, 1], ALU.subtract).then_inc(fd, 1)
                        dve.wait_ge(fd, FD * q1 + 9)
                        dve.tensor_tensor(pick[:], pick[:], th[:].rearrange("p (t o) -> p t o", o=1).to_broadcast([P, BT, EXPERTS]), ALU.mult)
                        dve.tensor_tensor(rank[:], sel[:, 0], sel[:, 1], ALU.add).then_inc(fd, 1)
                        dve.wait_ge(fd, FD * q1 + 10)
                        dve.tensor_tensor(rank[:], pick[:], rank[:], ALU.add).then_inc(fd, 1)
                        dve.wait_ge(fd, FD * q1 + 11)
                        dve.tensor_scalar(w_gate[:, r], rank[:], 0.5, None, ALU.mult).then_inc(w_ok, 1)

                def add_expert(qq, pp, e):
                    dve.wait_ge(m2_done, CHUNKS * qq + ACH + 2 * e + 2)
                    need(dve, acc_ok, EXPERTS * qq + e)
                    if e == 0:
                        dve.wait_ge(acc0_ok, qq + 1)
                    for t in range(BT):
                        last = dve.scalar_tensor_tensor(out=acc[:, pp, t, :], in0=st_bank[e % 2][:, EMB * t:EMB * (t + 1)],
                                                        scalar=w_gate[:, pp, t, e:e + 1], in1=acc[:, pp, t, :], op0=ALU.mult, op1=ALU.add)
                    last.then_inc(acc_ok, 1)

                for c in range(CHUNKS):
                    if c == 1 and 0 <= f - 1 < BLOCKS:
                        add_expert(q - 1, 1 - p, EXPERTS - 1)
                        dve.wait_ge(acc_ok, EXPERTS * q)
                        for t in range(BT):
                            for i, v in enumerate((abel, acc)):
                                last = dve.tensor_tensor_reduce((gen_abs, gen_t)[i][:, t, :], v[:, 1 - p, t, :], gcwb[:, i, :], 1.0, 0.0, ALU.mult, ALU.add, zpart[:, i, t:t + 1])
                        last.then_inc(tz, 1)
                        dve.wait_ge(tz, 2 * q - 1)
                        dve.tensor_tensor(zsum[:], zpart[:, 0], zpart[:, 1], ALU.add).then_inc(z_ok, 1)
                    if c == 3 and 0 <= f - 1 < BLOCKS:
                        dve.wait_ge(zth_ok, q)
                        dve.tensor_scalar(gmix[:], gth[:], 0.5, 0.5, ALU.mult, ALU.add).then_inc(tz, 1)
                        dve.wait_ge(tz, 2 * q)
                        dve.wait_ge(diff_ok, q)
                        dve.wait_ge(y_stored[1 - p], 8 * (q - 1 - (1 - p)) + 16)
                        for t in range(BT):
                            last = dve.scalar_tensor_tensor(out=y_out[:, 1 - p, t, :], in0=diff[:, t, :], scalar=gmix[:, t:t + 1],
                                                            in1=abel[:, 1 - p, t, :], op0=ALU.mult, op1=ALU.add)
                        last.then_inc(mix_ok, 1)
                    if 0 <= f < BLOCKS:
                        if c == 2:
                            dve.wait_ge(wt_done, q + 1)
                            dve.tensor_copy(w_t[:], mx[0:EXPERTS, :]).then_inc(wt_ok, 1)
                        if c == 4:
                            dve.wait_ge(ai_done, q + 1)
                            dve.tensor_copy(acc[:, p], my[:].rearrange("p (t e) -> p t e", t=BT)).then_inc(acc0_ok, 1)
                        if c == 5:
                            dve.wait_ge(m2_done, CHUNKS * q + ACH)
                            dve.tensor_tensor(abel[:, p], pv_bank[0][:].rearrange("p (t e) -> p t e", t=BT),
                                              ab2b[:].rearrange("p (o e) -> p o e", o=1).to_broadcast([P, BT, EMB]), ALU.add).then_inc(abel_ok, 1)
                        if c >= 7 and c % 2 == 1:
                            add_expert(q, p, (c - 7) // 2)
                    if 0 <= f + 1 < BLOCKS:
                        front(c)

            dve.wait_ge(f_const, 4)
            blocks(dve, ffn)


_NAMES = {
    "x": "L0_attn_hidden_states", "wq": "L0_attn_wq", "bq": "L0_attn_bq", "wk": "L0_attn_wk", "bk": "L0_attn_bk",
    "wv": "L0_attn_wv", "bv": "L0_attn_bv", "wo": "L0_attn_wo", "bo": "L0_attn_bo", "ln_g": "L0_ffn_ln_g",
    "ln_b": "L0_ffn_ln_b", "aw1": "L0_ffn_aw1", "ab1": "L0_ffn_ab1", "aw2": "L0_ffn_aw2", "ab2": "L0_ffn_ab2",
    "gate_w": "L0_ffn_gate_w", "gate_b": "L0_ffn_gate_b", "ew1": "L0_ffn_ew1", "eb1": "L0_ffn_eb1",
    "ew2": "L0_ffn_ew2", "eb2": "L0_ffn_eb2", "gens": "L0_ffn_gens", "gc_w": "L0_ffn_gc_w", "gc_b": "L0_ffn_gc_b",
    "c": "L0_c", "wmod": "L0_wmod",
}


def kernel(**inputs):
    import concourse.bacc as bacc
    from concourse.bass_utils import run_bass_kernel_spmd

    nc = bacc.Bacc("TRN2", target_bir_lowering=False, num_devices=1)
    arrays, aps = {}, {}
    for short, name in _NAMES.items():
        arr = np.ascontiguousarray(inputs[name])
        if short == "x":
            arr = arr.reshape(TILES, P, EMB)
        arrays[f"in_{short}"] = arr
        aps[short] = nc.dram_tensor(f"in_{short}", arr.shape, mybir.dt.from_np(arr.dtype), kind="ExternalInput").ap()
    out = nc.dram_tensor("out_0", (TILES, P, EMB), F32, kind="ExternalOutput").ap()
    build(nc, aps, out)
    r = run_bass_kernel_spmd(nc, [arrays], core_ids=[0])
    return np.asarray(r.results[0]["out_0"]).reshape(BATCH, SEQ, EMB)
```

```python
from contextlib import ExitStack

import numpy as np

import concourse.bass as bass
from concourse import mybir

F32 = mybir.dt.float32
F32R = mybir.dt.float32r
U32 = mybir.dt.uint32
ALU = mybir.AluOpType
ACT = mybir.ActivationFunctionType
AX_X = mybir.AxisListType.X

P = 128
BATCH, SEQ, EMB = 16, 256, 128
HEADS = 16
HDIM = EMB // HEADS
TILES = BATCH * SEQ // P
TPB = SEQ // P
NG = 4
SQUARINGS = 16
TAYLOR = 10
EPS = 1e-5
SCALE = float(1.0 / np.sqrt(HDIM))
MAXROW = 96
VW = 32
MLP = 4 * EMB
EXPERTS, EH = 6, 2 * EMB
ECH = EXPERTS * EH // P
ACH = MLP // P
CHUNKS = ACH + ECH
NVEC = CHUNKS + 5
NB = 5 * EMB + EXPERTS + 1
BT = 4
BLOCKS = TILES // BT
OW = HDIM + 1


def head_at(n):
    r, i, j = n // 8, n // 4 % 2, n % 4
    return 8 * r + 2 * j + i


def need(eng, sem, value):
    if not isinstance(value, int) or value > 0:
        eng.wait_ge(sem, value)


def settle(eng, sem):
    eng.sem_inc(sem, 1)


def build(nc, a, out):
    with ExitStack() as ctx:
        def sb(name, shape, dt=F32):
            return ctx.enter_context(nc.sbuf_tensor(name, shape, dt))

        def ps(name, shape):
            return ctx.enter_context(nc.psum_tensor(name, shape, F32))

        def sem(name):
            return ctx.enter_context(nc.semaphore(name))

        parts_dram = nc.dram_tensor("parts_dram", (2, 2, 2, HDIM, HEADS, SEQ), F32).ap()

        x_keep = sb("x_keep", [P, TILES, EMB])
        ident = sb("ident", [P, P])
        ones = sb("ones", [P, P])
        w_attn = sb("w_attn", [P, 10, EMB])
        wq, wk, wv, wo = (w_attn[:, i, :] for i in range(4))
        wmod = w_attn[:, 4:10, :].rearrange("p j e -> p (j e)")
        w_ffn = sb("w_ffn", [P, 2 * CHUNKS * P + EXPERTS])
        w1 = w_ffn[:, 0:CHUNKS * P]
        aw2 = w_ffn[:, CHUNKS * P:(CHUNKS + ACH) * P].rearrange("p (c n) -> p c n", c=ACH)
        ew2 = w_ffn[:, (CHUNKS + ACH) * P:2 * CHUNKS * P].rearrange("p (c n) -> p c n", c=ECH)
        gate_w = w_ffn[:, 2 * CHUNKS * P:2 * CHUNKS * P + EXPERTS]
        bcast = sb("bcast", [P, NB])
        ab2b = bcast[:, 2 * EMB:3 * EMB]
        gcwb = bcast[:, 3 * EMB:5 * EMB].rearrange("p (a e) -> p a e", a=2)
        gate_bb = bcast[:, 5 * EMB:5 * EMB + EXPERTS]
        gcb = bcast[:, 5 * EMB + EXPERTS:NB]
        bvb = bcast[:, 0:2 * EMB].rearrange("p (t e) -> p t e", t=TPB)
        vec_rows = sb("vec_rows", [NVEC, P])
        vec_cols = sb("vec_cols", [P, NVEC])
        b1c, cols, lnc = vec_cols, vec_cols[:, CHUNKS:CHUNKS + 3], vec_cols[:, CHUNKS + 3:CHUNKS + 5]
        c_row = sb("c_row", [BATCH, EMB])
        c_exp = sb("c_exp", [BATCH, EMB])
        c_sig = sb("c_sig", [BATCH, EMB])
        c_silu = sb("c_silu", [BATCH, EMB])
        c_t = sb("c_t", [P, BATCH])
        mod_t = sb("mod_t", [P, 3, BATCH])
        gate_bo = sb("gate_bo", [P, BATCH])
        tmp_t = sb("tmp_t", [P, 2, BATCH])

        gen = sb("gen", [P, NG, P])
        gen_abs = sb("gen_abs", [P, NG, P])
        gen_t = sb("gen_t", [P, NG, P])
        rot = sb("rot", [P, NG, P])
        rot_t = sb("rot_t", [P, NG, P])
        ident4 = sb("ident4", [P, NG, P])
        nrm = sb("nrm", [P, NG])
        gscale = sb("gscale", [P, NG])
        todo = sb("todo", [P, NG])

        q_stack = sb("q_stack", [P, 2, HEADS, SEQ], F32R)
        k_stack = sb("k_stack", [P, 2, HEADS, SEQ], F32R)
        prob = sb("prob", [P, 8, TPB * SEQ])
        v_blocks = sb("v_blocks", [P, 2, TPB, HEADS, VW])
        v_tok = sb("v_tok", [P, TPB, EMB])
        stats = sb("stats", [P, TPB, 6])
        mv = sb("mv", [P, TPB, 2])
        rstd = sb("rstd", [P, TPB])
        var_eps = sb("var_eps", [P, TPB])
        neg_half = sb("neg_half", [P, TPB])
        xhat = sb("xhat", [P, TPB, EMB])
        h_t = sb("h_t", [P, SEQ])
        qk = sb("qk", [P, 2, SEQ])
        qk_parts = sb("qk_parts", [P, 2, 2, SEQ], F32R)
        row_max = sb("row_max", [P, 2, TPB, HEADS])
        max_parts = sb("max_parts", [P, 2, TPB, 2, 8], F32R)
        max_rows = sb("max_rows", [16, 2, SEQ])
        o_raw = sb("o_raw", [P, 2, SEQ])
        o_rsum = sb("o_rsum", [P, 2, 16])
        o_tok = sb("o_tok", [P, TPB, EMB])
        o_t = sb("o_t", [P, SEQ])
        y_t = sb("y_t", [P, SEQ])

        ew2_t = sb("ew2_t", [P, ECH, P])
        ew2_rot = sb("ew2_rot", [P, ECH, EMB])
        rot_all = sb("rot_all", [P, 3, P])
        eb2 = sb("eb2", [EXPERTS, EMB])
        eb2_t = sb("eb2_t", [P, EXPERTS])
        eb2_rot = sb("eb2_rot", [EXPERTS, EMB])
        gcb_half = sb("gcb_half", [P, 1])
        tri = sb("tri", [P, EXPERTS, EXPERTS])
        mod_rows = sb("mod_rows", [BATCH, 3, EMB])
        mod_tmp = sb("mod_tmp", [BATCH, 2, EMB])
        mod_b = sb("mod_b", [P, 2, 2, 3, EMB])
        st2 = sb("st2", [P, 2, BT, 6])
        mv2 = sb("mv2", [P, 2, BT, 2])
        ve2 = sb("ve2", [P, 2, BT])
        rs2 = sb("rs2", [P, 2, BT])
        nh4 = sb("nh4", [P, BT])
        h2 = sb("h2", [P, 2, BT, EMB])
        xn_tok = sb("xn_tok", [P, BT, EMB])
        xn_t = sb("xn_t", [P, BT * P])
        w1_parts = q_stack[:, 0].rearrange("p h t -> p (h t)").rearrange("p (a m) -> p a m", a=2)
        xn_parts = k_stack[:, 0].rearrange("p h t -> p (h t)")[:, 0:4 * BT * P].rearrange("p (r a m) -> p r a m", r=2, a=2)
        lg = sb("lg", [P, BT, EXPERTS])
        cmp_gt = sb("cmp_gt", [P, BT, EXPERTS, EXPERTS])
        cmp_eq = sb("cmp_eq", [P, BT, EXPERTS, EXPERTS])
        rank = sb("rank", [P, BT, EXPERTS])
        sel = sb("sel", [P, 2, BT, EXPERTS])
        pick = sb("pick", [P, BT, EXPERTS])
        top = sb("top", [P, 3, BT])
        th = sb("th", [P, BT])
        w_gate = sb("w_gate", [P, 2, BT, EXPERTS])
        w_t = sb("w_t", [EXPERTS, BT * P])
        hid = prob[:, 0:4, :]
        acc = sb("acc", [P, 2, BT, EMB])
        abel = prob[:, 4:6, :].rearrange("p r (t e) -> p r t e", t=BT)
        zpart = sb("zpart", [P, 2, BT])
        zsum = sb("zsum", [P, BT])
        gth = sb("gth", [P, BT])
        gmix = sb("gmix", [P, BT])
        diff = sb("diff", [P, BT, EMB])
        y_out = prob[:, 6:8, :].rearrange("p r (t e) -> p r t e", t=BT)

        smax_bank = [ps(f"smax{i}", [P, 512]) for i in range(2)]
        st_bank = [ps(f"st{i}", [P, 512]) for i in range(2)]
        pv_bank = [ps(f"pv{i}", [P, 512]) for i in range(2)]
        mx = ps("mx", [P, 512])
        my = ps("my", [P, 512])

        s_c, s_wa, s_vec, s_bc, s_gen, f_w, s_eb2 = (sem(n) for n in ("s_c", "s_wa", "s_vec", "s_bc", "s_gen", "f_w", "s_eb2"))
        s_x = [sem(f"s_x{i}") for i in range(3)]
        s_const = sem("s_const")
        s_stackzero = sem("s_stackzero")
        c1, c2, c3, c4 = sem("c_exp_ok"), sem("c_dve"), sem("c_t_pe"), sem("c_t_ok")
        mod_pe, mod_ok, mod_dve = sem("mod_pe"), sem("mod_ok"), sem("mod_dve")
        g_abs, g_sum, g_dve, g_tpe, g_tok, g_mm, g_acc = (
            sem(n) for n in ("g_abs", "g_sum", "g_dve", "g_tpe", "g_tok", "g_mm", "g_acc"))
        smax_done, st_done, pv_done = sem("smax_done"), sem("st_done"), sem("pv_done")
        xt_done, qk_done, v_done, mt_done, ot1_done, ot2_done, y_done, yt_done = (
            sem(n) for n in ("xt_done", "qk_done", "v_done", "mt_done", "ot1_done", "ot2_done", "y_done", "yt_done"))
        sqt_done, sq_done = sem("sqt_done"), sem("sq_done")
        red_done, max_split, max_row_ok, v_ok, o_norm, x1_ok, stat_ok, rot_ok = (
            sem(n) for n in ("red_done", "max_split", "max_row_ok", "v_ok", "o_norm", "x1_ok", "stat_ok", "rot_ok"))
        d_bn, d_mhi, d_rs, d_sq = sem("d_bn"), sem("d_mhi"), sem("d_rs"), sem("d_sq")
        exp_done, h_ok, qk_ok, oraw_ok, ot_ok, y_ok, rott_ok = (
            sem(n) for n in ("exp_done", "h_ok", "qk_ok", "oraw_ok", "ot_ok", "y_ok", "rott_ok"))
        vb_ok, split_ok, xhat_ok = sem("vb_ok"), sem("split_ok"), sem("xhat_ok")
        p_hi, p_var, p_rs, vb_zero = sem("p_hi"), sem("p_var"), sem("p_rs"), sem("vb_zero")
        parts_out = sem("parts_out")
        stack_in = [sem(f"stack_in{r}") for r in range(2)]
        max_in = [sem(f"max_in{r}") for r in range(2)]
        d_settled, p_settled = sem("d_settled"), sem("p_settled")

        f_const, mr_dve, mr_out, w1_hi, w1_ok, xs_ok, f_hi = (
            sem(n) for n in ("f_const", "mr_dve", "mr_out", "w1_hi", "w1_ok", "xs_ok", "f_hi"))
        e2t_done, e2t_ok, rt_done, rt_ok, rp_done, rp_ok, er_done, er_ok = (
            sem(n) for n in ("e2t_done", "e2t_ok", "rt_done", "rt_ok", "rp_done", "rp_ok", "er_done", "er_ok"))
        modb_in = [sem(f"modb_in{i}") for i in range(2)]
        n_bn, n_mv, n_var, n_rs, n_hat, n_mul, h2_ok, xn_ok, fd = (
            sem(n) for n in ("n_bn", "n_mv", "n_var", "n_rs", "n_hat", "n_mul", "h2_ok", "xn_ok", "fd"))
        fxt_done, xnt_ok, lg_done, d_ok, th_ok, w_ok, wt_done, wt_ok, ai_done, acc0_ok = (
            sem(n) for n in ("fxt_done", "xnt_ok", "lg_done", "d_ok", "th_ok", "w_ok", "wt_done", "wt_ok", "ai_done", "acc0_ok"))
        m1_done, gelu_ok, m2_done, acc_ok, abel_ok, z_ok, tz, zth_ok, diff_ok, mix_ok, res1, res2, y_fin = (
            sem(n) for n in ("m1_done", "gelu_ok", "m2_done", "acc_ok", "abel_ok", "z_ok", "tz", "zth_ok", "diff_ok", "mix_ok", "res1", "res2", "y_fin"))
        y_stored = [sem(f"y_stored{i}") for i in range(2)]
        mod_dram = nc.dram_tensor("mod_dram", (BATCH, 3, EMB), F32).ap()

        block = ctx.enter_context(nc.Block())

        def blocks(eng, step):
            step(0, 0, 0)
            with eng.Fori(0, (BLOCKS - 2) // 2) as i:
                step(i * 2 + 1, 1, 1)
                step(i * 2 + 2, 2, 0)
            step(BLOCKS - 1, BLOCKS - 1, 1)
            step(BLOCKS, BLOCKS, 0)

        def iterations(eng, step, between):
            step(-3, -3, 1)
            step(-2, -2, 0)
            between()
            step(-1, -1, 1)
            step(0, 0, 0)
            with eng.Fori(0, (BATCH - 4) // 2) as i:
                step(i * 2 + 1, 1, 1)
                step(i * 2 + 2, 1, 0)
            for b in range(BATCH - 3, BATCH):
                step(b, b, b % 2)

        def squared(b):
            return b + 1 if not isinstance(b, int) or b < BATCH - 2 else SQUARINGS

        @block.sync
        def _(sp):
            sp.dma_start(x_keep[:, 0:2, :], a["x"][0:2].rearrange("t p e -> p t e")).then_inc(s_x[0], 16)
            sp.dma_start(c_row[:], a["c"]).then_inc(s_c, 16)
            sp.dma_start(vec_rows[:], a["vec_rows"]).then_inc(s_vec, 16)
            sp.dma_start(w_attn[:].rearrange("p j e -> p (j e)"), a["w_attn"]).then_inc(s_wa, 16)
            sp.dma_start(bcast[:], a["bcast"].to_broadcast([P, NB])).then_inc(s_bc, 16)
            sp.dma_start(x_keep[:, 2:8, :], a["x"][2:8].rearrange("t p e -> p t e")).then_inc(s_x[1], 16)
            sp.dma_start(gen[:], a["gens"].rearrange("g i j -> i g j")).then_inc(s_gen, 16)
            sp.dma_start(x_keep[:, 8:TILES, :], a["x"][8:TILES].rearrange("t p e -> p t e")).then_inc(s_x[2], 16)
            sp.dma_start(w_ffn[:], a["w_ffn"]).then_inc(f_w, 16)
            sp.dma_start(eb2[:], a["eb2"]).then_inc(s_eb2, 16)
            sp.wait_ge(mr_dve, 6)
            sp.dma_start(mod_dram, mod_rows[:]).then_inc(mr_out, 16)

            def max_dma(b, p, r):
                need(sp, max_row_ok, 2 * b + r + 1)
                for part in range(2):
                    sp.dma_start(q_stack[MAXROW + part:MAXROW + part + 1, p, 8 * r:8 * r + 8, :].bitcast(F32),
                                 max_rows[8 * part:8 * part + 8, r, :]).then_inc(max_in[r], 16)

            def stack_dma(b2, p, r):
                hs = slice(8 * r, 8 * r + 8)

                def load(stack, row, qk_i, p0, np_):
                    sp.dma_start(
                        stack[row:row + HDIM * np_, p, hs, :].bitcast(F32),
                        parts_dram[p, qk_i, p0:p0 + np_, :, hs, :].rearrange("a d h t -> (a d) h t")).then_inc(stack_in[r], 16)
                load(k_stack, 0, 1, 0, 2)
                load(k_stack, 2 * HDIM, 1, 0, 2)
                load(q_stack, 0, 0, 0, 2)
                load(q_stack, 2 * HDIM, 0, 1, 1)
                load(q_stack, 3 * HDIM, 0, 0, 1)

            def step(b, f, p):
                if f == BATCH - 3:
                    sp.wait_ge(mr_out, 16)
                    load_modulation(0, 0)
                if 0 <= f < BATCH:
                    max_dma(b, p, 1)
                if 0 <= f + 2 < BATCH:
                    b2 = b + 2
                    need(sp, split_ok, b2 + 1)
                    need(sp, stack_in[1], 80 * b + 80)
                    for part in range(2):
                        for i in range(2):
                            sp.dma_start(parts_dram[p, i, part].rearrange("d h t -> h d t"),
                                         qk_parts[:, part, i, :].bitcast(F32)).then_inc(parts_out, 16)
                    sp.wait_ge(parts_out, 64 * b2 + 64)
                    if f == -2:
                        sp.wait_ge(s_stackzero, 3)
                    need(sp, st_done, 16 * b + 8)
                    stack_dma(b2, p, 0)
                if 0 <= f + 1 < BATCH:
                    max_dma(b + 1, 1 - p, 0)
                if 0 <= f + 2 < BATCH:
                    need(sp, st_done, 16 * b + 16)
                    stack_dma(b + 2, p, 1)

            def load_modulation(q1, r):
                for i in range(2):
                    sp.dma_start(mod_b[:, r, i], mod_dram[bass.ds(2 * q1 + i, 1)].to_broadcast([P, 3, EMB])).then_inc(modb_in[r], 16)

            iterations(sp, step, lambda: None)
            for i in range(2):
                sp.sem_inc(y_stored[i], 16)

            def ffn(q, f, p):
                if 0 <= f - 1 < BLOCKS:
                    sp.wait_ge(y_fin, q)
                    sp.dma_start(out[bass.ds(BT * (q - 1), BT)].rearrange("t p e -> p t e"), y_out[:, 1 - p]).then_inc(y_stored[1 - p], 16)
                if 0 <= f + 1 < BLOCKS:
                    load_modulation(q + 1, 1 - p)
            blocks(sp, ffn)
            for i in range(2):
                sp.wait_ge(y_stored[i], 16 * BLOCKS // 2 + 16)

        @block.gpsimd
        def _(pool):
            pool.memset(ident[:], 0.0).then_inc(s_const, 1)
            pool.memset(ones[:], 1.0).then_inc(s_const, 1)
            pool.memset(neg_half[:], -0.5).then_inc(s_const, 1)
            pool.wait_ge(s_const, 3)
            pool.affine_select(out=ident[:], in_=ident[:], compare_op=ALU.not_equal, fill=1.0, base=0,
                               pattern=[[-1, P]], channel_multiplier=1).then_inc(s_const, 1)
            pool.wait_ge(s_const, 4)
            for g in range(NG):
                pool.tensor_copy(ident4[:, g, :], ident[:]).then_inc(s_const, 1)
            pool.memset(nh4[:], -0.5).then_inc(f_const, 1)
            pool.memset(tri[:], 1.0).then_inc(f_const, 1)
            pool.wait_ge(f_const, 2)
            pool.affine_select(out=tri[:], in_=tri[:], compare_op=ALU.is_gt, fill=0.0, base=0,
                               pattern=[[1, EXPERTS], [-1, EXPERTS]], channel_multiplier=0).then_inc(f_const, 1)
            pool.memset(q_stack[:].bitcast(F32), 0.0).then_inc(s_stackzero, 1)
            pool.wait_ge(s_bc, 16)
            pool.tensor_scalar(gcb_half[:], gcb[:], 0.5, None, ALU.mult).then_inc(f_const, 1)

            def step(b, f, p):
                if 0 <= f + 1 < BATCH:
                    b1, q = b + 1, 1 - p
                    if f == -1:
                        pool.memset(v_blocks[:], 0.0).then_inc(vb_zero, 1)
                        pool.wait_ge(vb_zero, 1)
                        for i in range(2):
                            for buf in range(2):
                                for t in range(TPB):
                                    v = v_blocks[:, buf, t].rearrange("k (m i) w -> k m i w", i=2)
                                    pool.memset(v[:, :, i, OW * i + HDIM:OW * i + OW], 1.0)
                    need(pool, v_ok, b1 + 1)
                    need(pool, pv_done, 4 * b)
                    settle(pool, p_settled)
                    for t in range(TPB):
                        dst = bass.AP(tensor=v_blocks, offset=v_blocks[:, q, t, 0, 0:1].offset,
                                      ap=[v_blocks[:].ap[0], [2 * VW, 8], [VW + OW, 2], [1, HDIM]])
                        last = pool.tensor_copy(dst, v_tok[:, t, :].rearrange("k (m i d) -> k m i d", i=2, d=HDIM))
                    last.then_inc(vb_ok, 1)
                if 0 <= f + 2 < BATCH:
                    b2 = b + 2
                    need(pool, qk_ok, b2 + 1)
                    need(pool, parts_out, 64 * b2)
                    settle(pool, p_settled)
                    pool.tensor_copy(qk_parts[:, 0], qk[:]).then_inc(p_hi, 1)
                    pool.wait_ge(p_hi, b2 + 1)
                    pool.tensor_tensor(qk_parts[:, 1], qk[:], qk_parts[:, 0].bitcast(F32), ALU.subtract).then_inc(split_ok, 1)
                if 0 <= f + 3 < BATCH:
                    b3 = b + 3
                    pool.wait_ge(stat_ok, b3 + 1)
                    settle(pool, p_settled)
                    pool.tensor_scalar(var_eps[:], mv[:, :, 1], EPS, None, ALU.add).then_inc(p_var, 1)
                    pool.wait_ge(p_var, b3 + 1)
                    pool.tensor_tensor(rstd[:], var_eps[:], neg_half[:], ALU.pow).then_inc(p_rs, 1)
                    pool.wait_ge(p_rs, b3 + 1)

            def rstd_of(k, q1):
                pool.wait_ge(n_mv, 2 * q1 + k + 1)
                settle(pool, p_settled)
                pool.tensor_scalar(ve2[:, k], mv2[:, k, :, 1], EPS, None, ALU.add).then_inc(n_var, 1)
                pool.wait_ge(n_var, 2 * q1 + k + 1)
                pool.tensor_tensor(rs2[:, k], ve2[:, k], nh4[:], ALU.pow).then_inc(n_rs, 1)

            def front(q1, r):
                rstd_of(0, q1)
                pool.wait_ge(modb_in[r], 16 * (q1 - r) + 32)
                pool.wait_ge(n_hat, q1 + 1)
                h4 = h2[:, r].rearrange("p (b t) e -> p b t e", b=2)

                def over(j):
                    return mod_b[:, r, :, j:j + 1, :].to_broadcast([P, 2, BT // 2, EMB])
                pool.tensor_tensor(h4, h4, over(1), ALU.mult).then_inc(n_mul, 1)
                pool.wait_ge(n_mul, q1 + 1)
                pool.tensor_tensor(h4, h4, over(0), ALU.add).then_inc(h2_ok, 1)
                rstd_of(1, q1)

            iterations(pool, step, lambda: None)
            front(0, 0)

            def ffn(q, f, p):
                if 0 <= f - 1 < BLOCKS:
                    q0, r = q - 1, 1 - p
                    pool.wait_ge(acc_ok, EXPERTS * q)
                    pool.wait_ge(abel_ok, q)
                    need(pool, mix_ok, q0)
                    pool.tensor_tensor(diff[:], acc[:, r], abel[:, r], ALU.subtract).then_inc(diff_ok, 1)
                    pool.wait_ge(mix_ok, q)
                    pool.tensor_tensor(y_out[:, r], y_out[:, r], h2[:, r], ALU.add).then_inc(res1, 1)
                    pool.wait_ge(res1, q)
                    y4 = y_out[:, r].rearrange("p (b t) e -> p b t e", b=2)
                    pool.tensor_tensor(y4, y4, mod_b[:, r, :, 2:3, :].to_broadcast([P, 2, BT // 2, EMB]), ALU.mult).then_inc(res2, 1)
                    pool.wait_ge(res2, q)
                    pool.tensor_tensor(y_out[:, r], y_out[:, r], x_keep[:, bass.ds(BT * q0, BT), :], ALU.add).then_inc(y_fin, 1)
                if 0 <= f + 1 < BLOCKS:
                    front(q + 1, 1 - p)

            blocks(pool, ffn)

        @block.scalar
        def _(act):
            act.wait_ge(s_c, 16)
            act.activation(c_exp[:], c_row[:], ACT.Exp, scale=-1.0).then_inc(c1, 1)
            act.wait_ge(c3, 1)
            act.activation(vec_cols[:], mx[:, 32:32 + NVEC], ACT.Identity)
            act.activation(c_t[:], mx[:, 0:BATCH], ACT.Identity).then_inc(c4, 1)

            def o_evac(b, r):
                act.wait_ge(pv_done, 4 * b + 2 * r + 2)
                act.activation(o_raw[:, r, :], pv_bank[r][:, 0:SEQ], ACT.Identity).then_inc(oraw_ok, 1)

            def o_turn(b):
                act.wait_ge(ot2_done, b + 1)
                act.activation(o_t[:], my[:, 0:SEQ], ACT.Identity).then_inc(ot_ok, 1)

            def y_gate(b):
                act.wait_ge(y_done, b + 1)
                act.activation(y_t[:], mx[:, 0:SEQ], ACT.Identity, scale=mod_t[:, 2, bass.ds(b, 1)],
                               bias=gate_bo[:, bass.ds(b, 1)]).then_inc(y_ok, 1)

            def turn_rot(m):
                act.wait_ge(sqt_done, m)
                act.activation(rot_t[:], mx[:].rearrange("p (g j) -> p g j", g=NG), ACT.Identity).then_inc(rott_ok, 1)

            def xn_evac(q1, bank):
                act.wait_ge(fxt_done, q1 + 1)
                act.activation(xn_t[:], bank[:], ACT.Identity, scale=lnc[:, 0:1], bias=lnc[:, 1:2]).then_inc(xnt_ok, 1)

            def gate_tanh(q1):
                act.wait_ge(d_ok, q1 + 1)
                act.activation(th[:], top[:, 2], ACT.Tanh, scale=0.5).then_inc(th_ok, 1)

            def step(b, f, p):
                live, pre, post = 0 <= f < BATCH, 0 <= f + 2 < BATCH, 0 <= f - 1 < BATCH
                for n in range(HEADS):
                    if live:
                        act.wait_ge(st_done, 16 * b + n + 1)
                        need(act, pv_done, 4 * b + n // 4 - 1)
                        act.activation(prob[:, n % 8, :], st_bank[n % 2][:], ACT.Exp, scale=SCALE).then_inc(exp_done, 1)
                    if n == 0 and pre:
                        act.wait_ge(xt_done, b + 3)
                        if f == -2:
                            act.wait_ge(mod_dve, 5)
                        act.activation(h_t[:], mx[:, 0:SEQ], ACT.Identity, scale=mod_t[:, 1, bass.ds(b + 2, 1)],
                                       bias=mod_t[:, 0, bass.ds(b + 2, 1)]).then_inc(h_ok, 1)
                    if n == 2 and post:
                        o_evac(b - 1, 1)
                    if n == 3 and pre:
                        act.wait_ge(qk_done, b + 3)
                        need(act, split_ok, b + 2)
                        for i in range(2):
                            last = act.activation(qk[:, i, :], mx[:, SEQ * i:SEQ * (i + 1)], ACT.Identity, bias=cols[:, i:i + 1])
                        last.then_inc(qk_ok, 1)
                    if n == 7 and post:
                        o_turn(b - 1)
                    if n == 9 and post:
                        y_gate(b - 1)
                    if n == 10 and live:
                        o_evac(b, 0)
                    if f == BATCH - 2 and n == 1:
                        turn_rot(SQUARINGS - 1)
                    if n == 14 and live and f < BATCH - 1:
                        turn_rot(squared(b))
                    if f == -1 and n in (8, 10, 12):
                        k = (n - 8) // 2
                        act.wait_ge(e2t_done, k + 1)
                        act.activation(ew2_t[:, 4 * k:4 * k + 4, :], pv_bank[0][:].rearrange("p (c j) -> p c j", c=4), ACT.Identity).then_inc(e2t_ok, 1)
                    if f == -1 and n == 14:
                        act.wait_ge(e2t_done, 4)
                        act.activation(eb2_t[:], pv_bank[0][:, 0:EXPERTS], ACT.Identity).then_inc(e2t_ok, 1)
                    if f == BATCH - 1:
                        if n == 3:
                            act.wait_ge(rt_done, 1)
                            act.activation(rot_t[:], smax_bank[1][:].rearrange("p (g j) -> p g j", g=NG), ACT.Identity).then_inc(rt_ok, 1)
                        if n == 4:
                            xn_evac(0, smax_bank[0])
                        if n == 11:
                            gate_tanh(0)

            def between():
                act.wait_ge(s_gen, 16)
                act.activation(gen_abs[:], gen[:], ACT.Abs).then_inc(g_abs, 1)
                act.wait_ge(g_tpe, 1)
                act.activation(gen_t[:], pv_bank[1][:].rearrange("p (g j) -> p g j", g=NG), ACT.Identity).then_inc(g_tok, 1)

            iterations(act, step, between)

            def ffn(q, f, p):
                for c in range(CHUNKS):
                    if 0 <= f < BLOCKS:
                        need(act, m2_done, CHUNKS * q + c - 3)
                        act.wait_ge(m1_done, CHUNKS * q + c + 1)
                        act.activation(hid[:, c % 4, :], smax_bank[c % 2][:], ACT.Gelu, bias=b1c[:, c:c + 1]).then_inc(gelu_ok, 1)
                    if 0 <= f + 1 < BLOCKS:
                        if c == 10:
                            xn_evac(q + 1, mx)
                        if c == 14:
                            gate_tanh(q + 1)
                    if c == 2 and 0 <= f - 1 < BLOCKS:
                        act.wait_ge(z_ok, q)
                        act.activation(gth[:], zsum[:], ACT.Tanh, scale=0.5, bias=gcb_half[:]).then_inc(zth_ok, 1)
                    if f == 0:
                        if c == 0:
                            o_evac(BATCH - 1, 1)
                        if c == 3:
                            o_turn(BATCH - 1)
                        if c == 5:
                            y_gate(BATCH - 1)

            act.wait_ge(f_const, 4)
            blocks(act, ffn)

        @block.tensor
        def _(pe):
            pe.wait_ge(s_const, 4)
            pe.wait_ge(s_vec, 16)
            pe.transpose(mx[:, 32:32 + NVEC], vec_rows[:], ident[0:NVEC, 0:NVEC])
            pe.wait_ge(c2, 3)
            pe.transpose(mx[:, 0:BATCH], c_silu[:], ident[0:BATCH, 0:BATCH]).then_inc(c3, 1)
            pe.wait_ge(c4, 1)
            pe.wait_ge(s_wa, 16)
            pe.matmul(mx[0:BATCH, 128:128 + 3 * EMB], c_t[:], wmod[:, 3 * EMB:6 * EMB], start=True, stop=True)
            for j in range(3):
                last = pe.matmul(mx[:, 32 + BATCH * j:32 + BATCH * (j + 1)], wmod[:, EMB * j:EMB * (j + 1)], c_t[:], start=True, stop=True)
            last.then_inc(mod_pe, 1)

            def pv(b, p, g):
                r, i = g // 2, g % 2
                if g == 0:
                    pe.wait_ge(vb_ok, b + 1)
                if i == 0:
                    need(pe, oraw_ok, 2 * b - 1 + r)
                pe.wait_ge(exp_done, 16 * b + 4 * g + 4)
                for t in range(TPB):
                    for j in range(4):
                        last = pe.matmul(pv_bank[r][VW * j:VW * (j + 1), 0:SEQ], v_blocks[:, p, t, 8 * r + 2 * j + i, :],
                                         prob[:, (4 * g + j) % 8, SEQ * t:SEQ * (t + 1)],
                                         start=(i == 0 and t == 0), stop=(i == 1 and t == TPB - 1))
                last.then_inc(pv_done, 1)

            def o_transposes(b, r, bank):
                pe.wait_ge(oraw_ok, 2 * b + r + 1)
                for t in range(TPB):
                    last = pe.transpose(bank[:, P * t:P * (t + 1)], o_raw[:, r, P * t:P * (t + 1)], ident[:])
                last.then_inc(ot1_done, 1)

            def o_back(b):
                pe.wait_ge(o_norm, 2 * b + 2)
                for t in range(TPB):
                    last = pe.transpose(my[:, P * t:P * (t + 1)], o_tok[:, t, :], ident[:])
                last.then_inc(ot2_done, 1)

            def project(b):
                pe.wait_ge(ot_ok, b + 1)
                pe.matmul(mx[:, 0:SEQ], wo, o_t[:], start=True, stop=True).then_inc(y_done, 1)

            def y_transposes(b):
                pe.wait_ge(y_ok, b + 1)
                for t in range(TPB):
                    last = pe.transpose(my[:, P * t:P * (t + 1)], y_t[:, P * t:P * (t + 1)], ident[:])
                last.then_inc(yt_done, 1)

            def max_transposes(b, r, bank):
                pe.wait_ge(max_split, 2 * b + r + 1)
                for t in range(TPB):
                    last = pe.transpose(bank[0:16, P * t:P * (t + 1)], max_parts[:, r, t].bitcast(F32).rearrange("p a h -> p (a h)"), ident[:])
                last.then_inc(mt_done, 1)

            def square_turn(m):
                need(pe, rot_ok, m - 1)
                for g in range(NG):
                    last = pe.transpose(mx[:, P * g:P * (g + 1)], rot[:, g, :], ident[:])
                last.then_inc(sqt_done, 1)

            def square(m):
                pe.wait_ge(rott_ok, m)
                for g in range(NG):
                    last = pe.matmul(my[:, P * g:P * (g + 1)], rot_t[:, g, :], rot[:, g, :], start=True, stop=True)
                last.then_inc(sq_done, 1)

            def horner(k):
                if k:
                    pe.wait_ge(g_acc, k)
                for g in range(NG):
                    last = pe.matmul(pv_bank[1][:, P * g:P * (g + 1)], gen_t[:, g, :], (rot if k else ident4)[:, g, :], start=True, stop=True)
                last.then_inc(g_mm, 1)

            def turn_block(q1, bank):
                pe.wait_ge(xn_ok, q1 + 1)
                for t in range(BT):
                    last = pe.transpose(bank[:, P * t:P * (t + 1)], xn_tok[:, t, :], ident[:])
                last.then_inc(fxt_done, 1)

            def logits(q1, bank):
                pe.wait_ge(xnt_ok, q1 + 1)
                for t in range(BT):
                    last = pe.matmul(bank[:, 8 * t:8 * t + EXPERTS], xn_t[:, P * t:P * (t + 1)], gate_w, start=True, stop=True)
                last.then_inc(lg_done, 1)

            def rotate_product(k):
                if k == 0:
                    pe.wait_ge(rt_ok, 1)
                need(pe, rp_ok, k)
                pe.matmul(smax_bank[1][:, 0:P], rot_t[:, NG - 2 - k, :], rot[:, NG - 1, :] if k == 0 else rot_all[:, k - 1, :],
                          start=True, stop=True).then_inc(rp_done, 1)

            def rotate_weights(k):
                if k < 3:
                    for c in range(4):
                        last = pe.matmul(st_bank[k % 2][:, P * c:P * (c + 1)], ew2_t[:, 4 * k + c, :], rot_all[:, NG - 2, :], start=True, stop=True)
                else:
                    last = pe.matmul(st_bank[1][0:EXPERTS, 0:EMB], eb2_t[:], rot_all[:, NG - 2, :], start=True, stop=True)
                last.then_inc(er_done, 1)

            def step(b, f, p):
                live, smax, pre, post = 0 <= f < BATCH, 0 <= f + 1 < BATCH, 0 <= f + 2 < BATCH, 0 <= f - 1 < BATCH
                for n in range(HEADS):
                    if smax:
                        if n % 8 == 0:
                            pe.wait_ge(stack_in[n // 8], 80 * (b + 2))
                        need(pe, red_done, 16 * (b + 1) + n - 1)
                        for t in range(TPB):
                            last = pe.matmul(smax_bank[n % 2][:, SEQ * t:SEQ * (t + 1)],
                                             q_stack[0:MAXROW, 1 - p, n, P * t:P * (t + 1)],
                                             k_stack[0:MAXROW, 1 - p, n, :], start=True, stop=True)
                        last.then_inc(smax_done, 1)
                    if live:
                        h = head_at(n)
                        if n % 8 == 0:
                            pe.wait_ge(max_in[n // 8], 32 * (b + 1))
                        need(pe, exp_done, 16 * b + n - 1)
                        for t in range(TPB):
                            last = pe.matmul(st_bank[n % 2][:, SEQ * t:SEQ * (t + 1)], k_stack[:, p, h, P * t:P * (t + 1)],
                                             q_stack[:, p, h, :], start=True, stop=True)
                        last.then_inc(st_done, 1)
                    if n == 0 and pre:
                        pe.wait_ge(xhat_ok, b + 3)
                        need(pe, rott_ok, b)
                        if f == -2:
                            pe.wait_ge(mod_ok, 2)
                        if f == -1:
                            pe.wait_ge(qk_ok, 1)
                        if f == 0:
                            pe.wait_ge(max_row_ok, 1)
                        for t in range(TPB):
                            last = pe.transpose(mx[:, P * t:P * (t + 1)], xhat[:, t, :], ident[:])
                        last.then_inc(xt_done, 1)
                    if n == 1 and live:
                        need(pe, rot_ok, b if f < BATCH - 1 else SQUARINGS)
                        if f == 0:
                            pe.wait_ge(v_ok, 2)
                        max_transposes(b, 1, my)
                    if n == 1 and post:
                        pv(b - 1, 1 - p, 3)
                    if n == 2 and pre:
                        pe.wait_ge(h_ok, b + 3)
                        for i, w in enumerate((wq, wk)):
                            last = pe.matmul(mx[:, SEQ * i:SEQ * (i + 1)], w, h_t[:], start=True, stop=True)
                        last.then_inc(qk_done, 1)
                    if n == 3 and pre:
                        need(pe, max_row_ok, 2 * b + 2)
                        if f == -1:
                            pe.wait_ge(v_ok, 1)
                        for t in range(TPB):
                            last = pe.matmul(my[:, EMB * t:EMB * (t + 1)], h_t[:, P * t:P * (t + 1)], wv, start=True, stop=True)
                        last.then_inc(v_done, 1)
                    if n == 4 and post:
                        if pre:
                            pe.wait_ge(qk_ok, b + 3)
                        else:
                            pe.wait_ge(rott_ok, SQUARINGS - 1 if f == BATCH - 2 else SQUARINGS)
                        o_transposes(b - 1, 1, mx)
                    if n == 5 and live:
                        if f == 0:
                            pe.wait_ge(e2t_ok, 4)
                        pv(b, p, 0)
                    if n == 6 and post:
                        if pre:
                            pe.wait_ge(v_ok, b + 3)
                        elif f == BATCH - 2:
                            pe.wait_ge(rot_ok, SQUARINGS - 1)
                        else:
                            pe.wait_ge(max_row_ok, 2 * b + 2)
                        o_back(b - 1)
                    if n == 8 and post:
                        project(b - 1)
                    if n == 9 and live:
                        pv(b, p, 1)
                    if n == 10 and post:
                        y_transposes(b - 1)
                    if n == 11 and smax:
                        if post:
                            pe.wait_ge(y_ok, b)
                        else:
                            pe.wait_ge(qk_ok, b + 3)
                        max_transposes(b + 1, 0, mx)
                    if n == 12 and live:
                        if post:
                            pe.wait_ge(x1_ok, b)
                        else:
                            pe.wait_ge(v_ok, 3)
                        o_transposes(b, 0, my)
                    if n == 13 and live:
                        if f == 0:
                            pe.wait_ge(g_acc, TAYLOR)
                        pv(b, p, 2)
                        if f < BATCH - 1:
                            pe.wait_ge(max_row_ok, 2 * b + 3)
                            square_turn(squared(b))
                    if n == 15 and live and f < BATCH - 1:
                        pe.wait_ge(o_norm, 2 * b + 1)
                        square(squared(b))
                    if f == -1:
                        if 2 <= n < 8:
                            horner(n + 2)
                        if n == 8:
                            pe.wait_ge(f_w, 16)
                        if n in (8, 10, 12):
                            k = (n - 8) // 2
                            need(pe, e2t_ok, k)
                            for c in range(4):
                                last = pe.transpose(pv_bank[0][:, P * c:P * (c + 1)], ew2[:, 4 * k + c, :], ident[:])
                            last.then_inc(e2t_done, 1)
                        if n == 14:
                            pe.wait_ge(e2t_ok, 3)
                            pe.wait_ge(s_eb2, 16)
                            pe.transpose(pv_bank[0][:, 0:EXPERTS], eb2[:], ident[0:EXPERTS, 0:EXPERTS]).then_inc(e2t_done, 1)
                    if f == BATCH - 2:
                        if n == 0:
                            need(pe, rott_ok, squared(b - 1))
                            square_turn(SQUARINGS - 1)
                        if n == 3:
                            pe.wait_ge(max_row_ok, 2 * b + 2)
                            square(SQUARINGS - 1)
                    if f == BATCH - 1:
                        if n == 2:
                            pe.wait_ge(red_done, 16 * BATCH)
                            pe.wait_ge(rot_ok, SQUARINGS)
                            for g in range(NG):
                                last = pe.transpose(smax_bank[1][:, P * g:P * (g + 1)], rot[:, g, :], ident[:])
                            last.then_inc(rt_done, 1)
                        if n == 3:
                            turn_block(0, smax_bank[0])
                        if n == 6:
                            logits(0, smax_bank[0])
                        if n in (5, 8, 11):
                            rotate_product((n - 5) // 3)

            def between():
                pe.wait_ge(g_abs, 1)
                pe.matmul(pv_bank[0][:], ones[:], gen_abs[:].rearrange("p g j -> p (g j)"), start=True, stop=True).then_inc(g_sum, 1)
                pe.wait_ge(g_dve, 8)
                for g in range(NG):
                    last = pe.transpose(pv_bank[1][:, P * g:P * (g + 1)], gen[:, g, :], ident[:])
                last.then_inc(g_tpe, 1)
                pe.wait_ge(g_tok, 1)
                pe.wait_ge(s_const, 8)
                for k in range(4):
                    horner(k)

            iterations(pe, step, between)

            def m2(q, p, c):
                pe.wait_ge(gelu_ok, CHUNKS * q + c + 1)
                if c < ACH:
                    bank, w, first, final = pv_bank[0], aw2[:, c, :], c == 0, c == ACH - 1
                    if first:
                        need(pe, abel_ok, q)
                else:
                    e = (c - ACH) // 2
                    bank, w, first, final = st_bank[e % 2], ew2_rot[:, c - ACH, :], c % 2 == 0, c % 2 == 1
                    if first:
                        need(pe, acc_ok, EXPERTS * q + e - 1)
                for t in range(BT):
                    last = pe.matmul(bank[:, EMB * t:EMB * (t + 1)], hid[:, c % 4, P * t:P * (t + 1)], w,
                                     start=first and t == 0, stop=final, skip_group_check=True)
                last.then_inc(m2_done, 1)

            def ffn(q, f, p):
                live, front = 0 <= f < BLOCKS, 0 <= f + 1 < BLOCKS
                for c in range(CHUNKS):
                    if live:
                        if c == 0:
                            pe.wait_ge(xs_ok, q + 1)
                            if f == 0:
                                pe.wait_ge(w1_ok, 1)
                                pe.wait_ge(fd, 1)
                                pe.wait_ge(rp_ok, NG - 1)
                        need(pe, gelu_ok, CHUNKS * q + c - 1)
                        for i, (wi, xi) in enumerate(((0, 0), (1, 0), (0, 1))):
                            last = pe.matmul(smax_bank[c % 2][:], w1_parts[:, wi, P * c:P * (c + 1)], xn_parts[:, p, xi, :],
                                             start=i == 0, stop=i == 2)
                        last.then_inc(m1_done, 1)
                    if c == 0:
                        if 0 <= f - 1 < BLOCKS:
                            m2(q - 1, 1 - p, CHUNKS - 1)
                    elif live:
                        m2(q, p, c - 1)
                    if f == 0:
                        if c == 0:
                            pv(BATCH - 1, 1, 3)
                            pe.wait_ge(exp_done, 16 * BATCH)
                            rotate_weights(0)
                            rotate_weights(1)
                        if c == 1:
                            pe.wait_ge(y_ok, BATCH - 1)
                            o_transposes(BATCH - 1, 1, mx)
                            pe.wait_ge(er_ok, 2)
                            rotate_weights(2)
                            rotate_weights(3)
                        if c == 3:
                            o_back(BATCH - 1)
                        if c == 4:
                            pe.wait_ge(er_ok, 4)
                            pe.wait_ge(ot_ok, BATCH)
                        if c == 5:
                            project(BATCH - 1)
                        if c == 7:
                            pe.wait_ge(acc0_ok, 1)
                            y_transposes(BATCH - 1)
                        if c == 10:
                            pe.wait_ge(y_ok, BATCH)
                        if c == 12:
                            pe.wait_ge(x1_ok, BATCH)
                    if live and c == 2:
                        pe.wait_ge(w_ok, q + 1)
                        if f == 0:
                            pe.wait_ge(o_norm, 2 * BATCH)
                        for t in range(BT):
                            last = pe.transpose(mx[0:EXPERTS, P * t:P * (t + 1)], w_gate[:, p, t, :], ident[:])
                        last.then_inc(wt_done, 1)
                    if live and c == 4:
                        pe.wait_ge(wt_ok, q + 1)
                        for t in range(BT):
                            last = pe.matmul(my[:, EMB * t:EMB * (t + 1)], w_t[:, P * t:P * (t + 1)], eb2_rot[:], start=True, stop=True)
                        last.then_inc(ai_done, 1)
                    if front and c == 10:
                        turn_block(q + 1, mx)
                    if front and c == 12:
                        pe.wait_ge(acc0_ok, q + 1)
                        logits(q + 1, my)

            blocks(pe, ffn)

        @block.vector
        def _(dve):
            dve.memset(k_stack[:].bitcast(F32), 0.0).then_inc(s_stackzero, 1)
            dve.wait_ge(c1, 1)
            dve.tensor_scalar(c_exp[:], c_exp[:], 1.0, None, ALU.add).then_inc(c2, 1)
            dve.wait_ge(c2, 1)
            dve.reciprocal(c_sig[:], c_exp[:]).then_inc(c2, 1)
            dve.wait_ge(c2, 2)
            dve.tensor_tensor(c_silu[:], c_row[:], c_sig[:], ALU.mult).then_inc(c2, 1)

            def modulations():
                dve.wait_ge(mod_pe, 1)
                dve.tensor_copy(mod_t[:], mx[:, 32:32 + 3 * BATCH].rearrange("p (j b) -> p j b", j=3)).then_inc(mod_ok, 1)
                dve.tensor_copy(mod_rows[:], mx[0:BATCH, 128:128 + 3 * EMB].rearrange("p (j e) -> p j e", j=3)).then_inc(mod_ok, 1)
                dve.wait_ge(mod_ok, 2)
                dve.tensor_scalar(mod_t[:, 1, :], mod_t[:, 1, :], 1.0, None, ALU.add).then_inc(mod_dve, 1)
                for g, tmp, done in ((mod_t[:, 2, :], tmp_t, mod_dve), (mod_rows[:, 2, :], mod_tmp, mr_dve)):
                    first = 1 if done is mod_dve else 0
                    dve.tensor_scalar(tmp[:, 1, :], g, 0.0, None, ALU.is_ge).then_inc(done, 1)
                    dve.wait_ge(done, first + 1)
                    dve.tensor_scalar(tmp[:, 1, :], tmp[:, 1, :], 2.0, -1.0, ALU.mult, ALU.add).then_inc(done, 1)
                    dve.wait_ge(done, first + 2)
                    dve.tensor_tensor(tmp[:, 0, :], g, tmp[:, 1, :], ALU.mult).then_inc(done, 1)
                    dve.wait_ge(done, first + 3)
                    dve.scalar_tensor_tensor(out=g, in0=tmp[:, 0, :], scalar=0.25, in1=tmp[:, 1, :],
                                             op0=ALU.max, op1=ALU.mult).then_inc(done, 1)
                dve.tensor_scalar(mod_rows[:, 1, :], mod_rows[:, 1, :], 1.0, None, ALU.add).then_inc(mr_dve, 2)
                dve.wait_ge(mod_dve, 5)
                dve.wait_ge(c4, 1)
                dve.tensor_scalar(gate_bo[:], mod_t[:, 2, :], cols[:, 2:3], None, ALU.mult).then_inc(mod_dve, 1)
                dve.wait_ge(s_stackzero, 2)
                dve.memset(k_stack[MAXROW:MAXROW + 2].bitcast(F32), 1.0).then_inc(s_stackzero, 1)

            def series(k):
                dve.wait_ge(g_mm, k + 1)
                dve.scalar_tensor_tensor(out=rot[:].rearrange("p g j -> p (g j)"), in0=pv_bank[1][:], scalar=1.0 / (TAYLOR - k),
                                         in1=ident4[:].rearrange("p g j -> p (g j)"), op0=ALU.mult, op1=ALU.add).then_inc(g_acc, 1)

            def between():
                dve.wait_ge(g_sum, 1)
                dve.tensor_reduce(nrm[:], pv_bank[0][:].rearrange("p (g j) -> p g j", g=NG), AX_X, ALU.max).then_inc(g_dve, 1)
                dve.wait_ge(g_dve, 1)
                dve.tensor_scalar(nrm[:], nrm[:], 2.0, 2.0 ** -100, ALU.mult, ALU.max).then_inc(g_dve, 1)
                dve.wait_ge(g_dve, 2)
                dve.tensor_scalar(nrm[:].bitcast(U32), nrm[:].bitcast(U32), 0x7F800000, None, ALU.bitwise_and).then_inc(g_dve, 1)
                dve.wait_ge(g_dve, 3)
                dve.reciprocal(gscale[:], nrm[:]).then_inc(g_dve, 1)
                dve.wait_ge(g_dve, 4)
                dve.tensor_scalar(gscale[:], gscale[:], 1.0, 2.0 ** -SQUARINGS, ALU.min, ALU.max).then_inc(g_dve, 1)
                dve.wait_ge(g_dve, 5)
                for g in range(NG):
                    last = dve.tensor_scalar(gen[:, g, :], gen[:, g, :], gscale[:, g:g + 1], None, ALU.mult)
                last.then_inc(g_dve, 3)
                dve.wait_ge(s_const, 8)
                for k in range(4):
                    series(k)

            def split_max(b, p, r):
                hs = slice(8 * r, 8 * r + 8)
                dve.wait_ge(red_done, 16 * b + 8 * r + 8)
                need(dve, mt_done, 2 * b - 1 + r)
                dve.tensor_scalar(max_parts[:, r, :, 0, :], row_max[:, p, :, hs], -1.0, None, ALU.mult).then_inc(d_mhi, 1)
                dve.wait_ge(d_mhi, 2 * b + r + 1)
                dve.scalar_tensor_tensor(out=max_parts[:, r, :, 1, :], in0=row_max[:, p, :, hs], scalar=-1.0,
                                         in1=max_parts[:, r, :, 0, :].bitcast(F32), op0=ALU.mult, op1=ALU.subtract).then_inc(max_split, 1)

            def max_row(b, r, bank):
                dve.wait_ge(mt_done, 2 * b + r + 1)
                need(dve, max_in[r], 32 * b)
                dve.tensor_copy(max_rows[:, r, :], bank[0:16, 0:SEQ]).then_inc(max_row_ok, 1)

            def normalise(b, r, bank):
                dve.wait_ge(ot1_done, 2 * b + r + 1)
                o = bank[:, 0:SEQ].rearrange("p (m w) -> p m w", w=VW)[:, :, 0:2 * OW].rearrange("p m (i d) -> p m i d", i=2)
                dve.reciprocal(o_rsum[:, r, :].rearrange("p (m i) -> p m i", i=2), o[:, :, :, HDIM]).then_inc(d_rs, 1)
                dve.wait_ge(d_rs, 2 * b + r + 1)
                need(dve, ot2_done, b)
                dve.tensor_tensor(o_tok[:, :, 64 * r:64 * r + 64].rearrange("p t (j i d) -> p t j i d", i=2, d=HDIM),
                                  o[:, :, :, 0:HDIM].rearrange("p (t j) i d -> p t j i d", t=TPB),
                                  o_rsum[:, r, :].rearrange("p (t j i o) -> p t j i o", t=TPB, i=2, o=1).to_broadcast([P, TPB, 4, 2, HDIM]),
                                  ALU.mult).then_inc(o_norm, 1)

            def add_attention(b):
                dve.wait_ge(yt_done, b + 1)
                xs = x_keep[:, bass.ds(TPB * b, TPB), :]
                dve.tensor_tensor(xs, my[:, 0:SEQ].rearrange("p (t e) -> p t e", t=TPB), xs, ALU.add).then_inc(x1_ok, 1)

            def squaring_due(m):
                need(dve, rot_ok, m - 1)
                dve.tensor_scalar(todo[:], gscale[:], 0.75, None, ALU.is_lt).then_inc(d_sq, 1)
                dve.wait_ge(d_sq, 2 * m - 1)
                dve.scalar_tensor_tensor(out=gscale[:], in0=todo[:], scalar=1.0, in1=gscale[:], op0=ALU.add, op1=ALU.mult).then_inc(d_sq, 1)

            def take_square(m):
                dve.wait_ge(sq_done, m)
                dve.wait_ge(d_sq, 2 * m)
                settle(dve, d_settled)
                dve.copy_predicated(out=rot[:], mask=todo[:].bitcast(U32).rearrange("p (g o) -> p g o", o=1).to_broadcast([P, NG, P]),
                                    data=my[:].rearrange("p (g j) -> p g j", g=NG)).then_inc(rot_ok, 1)

            def tile(t):
                return x_keep[:, bass.ds(t, 1), :].rearrange("p o e -> p (o e)")

            def norm(k, q1, src, dst, ready):
                for t in range(BT):
                    last = dve.bn_stats(st2[:, k, t, :], src(t))
                last.then_inc(n_bn, 1)
                dve.wait_ge(n_bn, 2 * q1 + k + 1)
                settle(dve, d_settled)
                for t in range(BT):
                    last = dve.bn_aggr(mv2[:, k, t, :], st2[:, k, t, :])
                last.then_inc(n_mv, 1)
                dve.wait_ge(n_rs, 2 * q1 + k + 1)
                for t in range(BT):
                    last = dve.tensor_scalar(dst(t), src(t), mv2[:, k, t, 0:1], rs2[:, k, t:t + 1], ALU.subtract, ALU.mult)
                last.then_inc(ready, 1)

            def norm_x(q1, r):
                norm(0, q1, lambda t: tile(BT * q1 + t), lambda t: h2[:, r, t, :], n_hat)

            def norm_h(q1, r):
                dve.wait_ge(h2_ok, q1 + 1)
                need(dve, fxt_done, q1)
                norm(1, q1, lambda t: h2[:, r, t, :], lambda t: xn_tok[:, t, :], xn_ok)

            def split_xn(q1, r):
                dve.wait_ge(xnt_ok, q1 + 1)
                dve.tensor_copy(xn_parts[:, r, 0, :], xn_t[:]).then_inc(f_hi, 1)
                dve.wait_ge(f_hi, q1 + 1)
                dve.tensor_tensor(xn_parts[:, r, 1, :], xn_t[:], xn_parts[:, r, 0, :].bitcast(F32), ALU.subtract).then_inc(xs_ok, 1)

            FD = 11

            def rank_experts(q1, bank):
                n = [FD * q1]

                def then(ins):
                    ins.then_inc(fd, 1)
                    n[0] = n[0] + 1
                    dve.wait_ge(fd, n[0])
                dve.wait_ge(lg_done, q1 + 1)
                then(dve.tensor_tensor(lg[:], bank[:, 0:8 * BT].rearrange("p (t e) -> p t e", t=BT)[:, :, 0:EXPERTS],
                                       gate_bb.rearrange("p (o e) -> p o e", o=1).to_broadcast([P, BT, EXPERTS]), ALU.add))
                other = lg[:].rearrange("p t (o e) -> p t o e", o=1).to_broadcast([P, BT, EXPERTS, EXPERTS])
                own = lg[:].rearrange("p t (e o) -> p t e o", o=1).to_broadcast([P, BT, EXPERTS, EXPERTS])
                dve.tensor_tensor(cmp_gt[:], other, own, ALU.is_gt)
                then(dve.tensor_tensor(cmp_eq[:], other, own, ALU.is_equal))
                then(dve.tensor_tensor(cmp_eq[:], cmp_eq[:], tri[:].rearrange("p (o e) g -> p o e g", o=1).to_broadcast([P, BT, EXPERTS, EXPERTS]), ALU.mult))
                then(dve.tensor_tensor(cmp_gt[:], cmp_gt[:], cmp_eq[:], ALU.add))
                then(dve.tensor_reduce(rank[:], cmp_gt[:], AX_X, ALU.add))
                dve.tensor_scalar(sel[:, 0], rank[:], 0.0, None, ALU.is_equal)
                then(dve.tensor_scalar(sel[:, 1], rank[:], 1.0, None, ALU.is_equal))
                then(dve.tensor_tensor(pick[:], lg[:], sel[:, 1], ALU.mult))
                dve.tensor_reduce(top[:, 1], pick[:], AX_X, ALU.add)
                then(dve.tensor_reduce(top[:, 0], lg[:], AX_X, ALU.max))
                dve.tensor_tensor(top[:, 2], top[:, 0], top[:, 1], ALU.subtract).then_inc(d_ok, 1)

            def weigh_experts(q1, r):
                dve.wait_ge(th_ok, q1 + 1)
                dve.tensor_tensor(pick[:], sel[:, 0], sel[:, 1], ALU.subtract).then_inc(fd, 1)
                dve.wait_ge(fd, FD * q1 + 9)
                dve.tensor_tensor(pick[:], pick[:], th[:].rearrange("p (t o) -> p t o", o=1).to_broadcast([P, BT, EXPERTS]), ALU.mult)
                dve.tensor_tensor(rank[:], sel[:, 0], sel[:, 1], ALU.add).then_inc(fd, 1)
                dve.wait_ge(fd, FD * q1 + 10)
                dve.tensor_tensor(rank[:], pick[:], rank[:], ALU.add).then_inc(fd, 1)
                dve.wait_ge(fd, FD * q1 + 11)
                dve.tensor_scalar(w_gate[:, r], rank[:], 0.5, None, ALU.mult).then_inc(w_ok, 1)

            def step(b, f, p):
                live, smax, pre, post = 0 <= f < BATCH, 0 <= f + 1 < BATCH, 0 <= f + 2 < BATCH, 0 <= f - 1 < BATCH
                if live:
                    split_max(b, p, 1)
                for n in range(HEADS):
                    if smax:
                        dve.wait_ge(smax_done, 16 * (b + 1) + n + 1)
                        dve.tensor_reduce(row_max[:, 1 - p, :, n], smax_bank[n % 2][:].rearrange("p (t k) -> p t k", t=TPB),
                                          AX_X, ALU.max).then_inc(red_done, 1)
                    if n == 0 and post:
                        take_square(squared(b - 1))
                    if n == 2 and live:
                        max_row(b, 1, my)
                    if n == 4 and pre:
                        dve.wait_ge(v_done, b + 3)
                        need(dve, vb_ok, b + 2)
                        if f == -2:
                            dve.wait_ge(s_bc, 16)
                        dve.tensor_tensor(v_tok[:], my[:, 0:SEQ].rearrange("p (t e) -> p t e", t=TPB), bvb, ALU.add).then_inc(v_ok, 1)
                    if n == 5 and post:
                        normalise(b - 1, 1, mx)
                    if n == 8 and smax:
                        split_max(b + 1, 1 - p, 0)
                    if n == 9 and 0 <= f + 3 < BATCH:
                        b3 = b + 3
                        if f in (-3, -2, 0):
                            dve.wait_ge(s_x[(-3, -2, 0).index(f)], 16)
                        need(dve, xhat_ok, b3)
                        for t in range(TPB):
                            last = dve.bn_stats(stats[:, t, :], tile(TPB * b3 + t))
                        last.then_inc(d_bn, 1)
                        dve.wait_ge(d_bn, b3 + 1)
                        settle(dve, d_settled)
                        for t in range(TPB):
                            last = dve.bn_aggr(mv[:, t, :], stats[:, t, :])
                        last.then_inc(stat_ok, 1)
                    if n == 11 and post:
                        add_attention(b - 1)
                    if n == 12 and smax:
                        max_row(b + 1, 0, mx)
                    if n == 13 and live:
                        normalise(b, 0, my)
                    if n == 14 and 0 <= f + 3 < BATCH:
                        b3 = b + 3
                        dve.wait_ge(p_rs, b3 + 1)
                        need(dve, xt_done, b3)
                        for t in range(TPB):
                            last = dve.tensor_scalar(xhat[:, t, :], tile(TPB * b3 + t), mv[:, t, 0:1], rstd[:, t:t + 1], ALU.subtract, ALU.mult)
                        last.then_inc(xhat_ok, 1)
                    if n == 14 and live and f < BATCH - 1:
                        squaring_due(squared(b))
                    if f == -1 and 2 <= n < 8:
                        series(n + 2)
                    if f == BATCH - 2:
                        if n == 1:
                            squaring_due(SQUARINGS - 1)
                        if n == 4:
                            take_square(SQUARINGS - 1)
                        if n == 6:
                            norm_x(0, 0)
                        if n == 12:
                            norm_h(0, 0)
                    if f == BATCH - 1:
                        if n == 3:
                            dve.wait_ge(st_done, 16 * (BATCH - 1))
                            dve.tensor_copy(w1_parts[:, 0, :], w1).then_inc(w1_hi, 1)
                            dve.wait_ge(w1_hi, 1)
                            dve.tensor_tensor(w1_parts[:, 1, :], w1, w1_parts[:, 0, :].bitcast(F32), ALU.subtract).then_inc(w1_ok, 1)
                        if n == 5:
                            split_xn(0, 0)
                        if n in (6, 9, 12):
                            k = (n - 6) // 3
                            dve.wait_ge(rp_done, k + 1)
                            dve.tensor_copy(rot_all[:, k, :], smax_bank[1][:, 0:P]).then_inc(rp_ok, 1)
                        if n == 7:
                            rank_experts(0, smax_bank[0])
                        if n == 14:
                            weigh_experts(0, 0)
                if f == -3:
                    modulations()

            iterations(dve, step, between)

            def add_expert(q, p, e):
                dve.wait_ge(m2_done, CHUNKS * q + ACH + 2 * e + 2)
                need(dve, acc_ok, EXPERTS * q + e)
                if e == 0:
                    dve.wait_ge(acc0_ok, q + 1)
                for t in range(BT):
                    last = dve.scalar_tensor_tensor(out=acc[:, p, t, :], in0=st_bank[e % 2][:, EMB * t:EMB * (t + 1)],
                                                    scalar=w_gate[:, p, t, e:e + 1], in1=acc[:, p, t, :], op0=ALU.mult, op1=ALU.add)
                last.then_inc(acc_ok, 1)

            def ffn(q, f, p):
                for c in range(CHUNKS):
                    if c == 1 and 0 <= f - 1 < BLOCKS:
                        add_expert(q - 1, 1 - p, EXPERTS - 1)
                        dve.wait_ge(acc_ok, EXPERTS * q)
                        for t in range(BT):
                            for i, v in enumerate((abel, acc)):
                                last = dve.tensor_tensor_reduce((gen_abs, gen_t)[i][:, t, :], v[:, 1 - p, t, :], gcwb[:, i, :], 1.0, 0.0, ALU.mult, ALU.add, zpart[:, i, t:t + 1])
                        last.then_inc(tz, 1)
                        dve.wait_ge(tz, 2 * q - 1)
                        dve.tensor_tensor(zsum[:], zpart[:, 0], zpart[:, 1], ALU.add).then_inc(z_ok, 1)
                    if f == 0:
                        if c in (0, 1):
                            for k in (2 * c, 2 * c + 1):
                                dve.wait_ge(er_done, k + 1)
                                if k < 3:
                                    dve.tensor_copy(ew2_rot[:, 4 * k:4 * k + 4, :], st_bank[k % 2][:].rearrange("p (c j) -> p c j", c=4)).then_inc(er_ok, 1)
                                else:
                                    dve.tensor_copy(eb2_rot[:], st_bank[1][0:EXPERTS, 0:EMB]).then_inc(er_ok, 1)
                            if c == 0:
                                normalise(BATCH - 1, 1, mx)
                        if c == 8:
                            add_attention(BATCH - 1)
                    if 0 <= f < BLOCKS:
                        if c == 2:
                            dve.wait_ge(wt_done, q + 1)
                            dve.tensor_copy(w_t[:], mx[0:EXPERTS, :]).then_inc(wt_ok, 1)
                    if c == 3 and 0 <= f - 1 < BLOCKS:
                        dve.wait_ge(zth_ok, q)
                        dve.tensor_scalar(gmix[:], gth[:], 0.5, 0.5, ALU.mult, ALU.add).then_inc(tz, 1)
                        dve.wait_ge(tz, 2 * q)
                        dve.wait_ge(diff_ok, q)
                        dve.wait_ge(y_stored[1 - p], 8 * (q - 1 - (1 - p)) + 16)
                        for t in range(BT):
                            last = dve.scalar_tensor_tensor(out=y_out[:, 1 - p, t, :], in0=diff[:, t, :], scalar=gmix[:, t:t + 1],
                                                            in1=abel[:, 1 - p, t, :], op0=ALU.mult, op1=ALU.add)
                        last.then_inc(mix_ok, 1)
                    if 0 <= f < BLOCKS:
                        if c == 4:
                            dve.wait_ge(ai_done, q + 1)
                            dve.tensor_copy(acc[:, p], my[:].rearrange("p (t e) -> p t e", t=BT)).then_inc(acc0_ok, 1)
                        if c == 5:
                            dve.wait_ge(m2_done, CHUNKS * q + ACH)
                            dve.tensor_tensor(abel[:, p], pv_bank[0][:].rearrange("p (t e) -> p t e", t=BT),
                                              ab2b.rearrange("p (o e) -> p o e", o=1).to_broadcast([P, BT, EMB]), ALU.add).then_inc(abel_ok, 1)
                        if c >= 7 and c % 2 == 1:
                            add_expert(q, p, (c - 7) // 2)
                    if 0 <= f + 1 < BLOCKS:
                        if c == 6:
                            need(dve, y_fin, q)
                            norm_x(q + 1, 1 - p)
                        if c == 8:
                            norm_h(q + 1, 1 - p)
                        if c == 10:
                            split_xn(q + 1, 1 - p)
                        if c == 12:
                            rank_experts(q + 1, my)
                        if c == 15:
                            weigh_experts(q + 1, 1 - p)

            dve.wait_ge(f_const, 4)
            blocks(dve, ffn)


def kernel(**inputs):
    import concourse.bacc as bacc
    from concourse.bass_utils import run_bass_kernel_spmd

    def of(name):
        return np.asarray(inputs[name])

    attn, ffn = "L0_attn_", "L0_ffn_"
    by_row = of(ffn + "ew1").transpose(1, 0, 2).reshape(EMB, EXPERTS * EH)
    down = [of(ffn + "aw2"), of(ffn + "ew2").reshape(EXPERTS * EH, EMB)]
    down = np.concatenate(down, axis=0).reshape(CHUNKS, P, EMB).transpose(1, 0, 2).reshape(P, CHUNKS * EMB)
    arrays = {
        "x": of(attn + "hidden_states").reshape(TILES, P, EMB),
        "c": of("L0_c"),
        "w_attn": np.concatenate([of(attn + "wq"), of(attn + "wk"), of(attn + "wv"), of(attn + "wo"), of("L0_wmod")], axis=1),
        "vec_rows": np.concatenate([of(ffn + "ab1").reshape(ACH, P), of(ffn + "eb1").reshape(ECH, P)]
                                   + [of(n).reshape(1, P) for n in (attn + "bq", attn + "bk", attn + "bo", ffn + "ln_g", ffn + "ln_b")], axis=0),
        "bcast": np.concatenate([of(attn + "bv"), of(attn + "bv"), of(ffn + "ab2"), of(ffn + "gc_w").reshape(2 * EMB),
                                 of(ffn + "gate_b"), of(ffn + "gc_b")]).reshape(1, NB),
        "gens": of(ffn + "gens"),
        "w_ffn": np.concatenate([of(ffn + "aw1"), by_row, down, of(ffn + "gate_w")], axis=1),
        "eb2": of(ffn + "eb2"),
    }
    arrays = {f"in_{n}": np.ascontiguousarray(v) for n, v in arrays.items()}
    nc = bacc.Bacc("TRN2", target_bir_lowering=False, num_devices=1)
    aps = {n[3:]: nc.dram_tensor(n, v.shape, mybir.dt.from_np(v.dtype), kind="ExternalInput").ap() for n, v in arrays.items()}
    out = nc.dram_tensor("out_0", (TILES, P, EMB), F32, kind="ExternalOutput").ap()
    build(nc, aps, out)
    r = run_bass_kernel_spmd(nc, [arrays], core_ids=[0])
    return np.asarray(r.results[0]["out_0"]).reshape(BATCH, SEQ, EMB)
```

```python
from contextlib import ExitStack

import numpy as np

import concourse.bass as bass
from concourse import mybir

F32 = mybir.dt.float32
F32R = mybir.dt.float32r
U32 = mybir.dt.uint32
ALU = mybir.AluOpType
ACT = mybir.ActivationFunctionType
AX_X = mybir.AxisListType.X

P = 128
BATCH, SEQ, EMB = 16, 256, 128
HEADS = 16
HDIM = EMB // HEADS
TILES = BATCH * SEQ // P
TPB = SEQ // P
NG = 4
SQUARINGS = 16
TAYLOR = 10
EPS = 1e-5
SCALE = float(1.0 / np.sqrt(HDIM))
MAXROW = 96
VW = 32
MLP = 4 * EMB
EXPERTS, EH = 6, 2 * EMB
ECH = EXPERTS * EH // P
ACH = MLP // P
CHUNKS = ACH + ECH
NVEC = CHUNKS + 4
NB = 6 * EMB + EXPERTS + 1
BT = 4
BLOCKS = TILES // BT
OW = HDIM + 1


SLOT = dict(
    x_turn=0, qk=2, v=4, max_turn1=1, pv3=1, o_turn1=4, o_back=7, project=9, max_turn0=13, o_turn0=13, pv0=6,
    pv1=10, pv2=15, square_turn=12, square=15,
    x_modulate=0, qk_bias=2, o_evac1=1, o_back_evac=7, o_evac0=10, square_turn_evac=14,
    square_take=1, max_row1=1, v_bias=4, normalise1=5, max_split0=10, stats=9, residual=10, max_row0=13,
    normalise0=15, xhat=14, square_due=14,
)
CHUNK = dict(
    gates_turn=3, biases=4, xn_turn=12, logits=13,
    gate_tanh=0, mix_tanh=3, xn_evac=12,
    weigh=1, gates_evac=3, mix=3, biases_evac=7, dense_logit=6, x_stats=0, x_hat=6, h_stats=9, h_hat=11,
    xn_split=13, rank=14,
)


def head_at(n):
    r, i, j = n // 8, n // 4 % 2, n % 4
    return 8 * r + 2 * j + i


def need(eng, sem, value):
    if not isinstance(value, int) or value > 0:
        eng.wait_ge(sem, value)


def settle(eng, sem):
    eng.sem_inc(sem, 1)


def build(nc, a, out):
    with ExitStack() as ctx:
        def sb(name, shape, dt=F32):
            return ctx.enter_context(nc.sbuf_tensor(name, shape, dt))

        def ps(name, shape):
            return ctx.enter_context(nc.psum_tensor(name, shape, F32))

        def sem(name):
            return ctx.enter_context(nc.semaphore(name))

        mod_dram = nc.dram_tensor("mod_dram", (BATCH, 5, EMB), F32).ap()

        x_keep = sb("x_keep", [P, TILES, EMB])
        ident = sb("ident", [P, P])
        ones = sb("ones", [P, P])
        w_attn = sb("w_attn", [P, 10, EMB])
        wq, wk, wv, wo = (w_attn[:, i, :] for i in range(4))
        wmod = w_attn[:, 4:10, :].rearrange("p j e -> p (j e)")
        w_ffn = sb("w_ffn", [P, 2 * CHUNKS * P + EXPERTS])
        w1 = w_ffn[:, 0:CHUNKS * P]
        aw2 = w_ffn[:, CHUNKS * P:(CHUNKS + ACH) * P].rearrange("p (c n) -> p c n", c=ACH)
        ew2 = w_ffn[:, (CHUNKS + ACH) * P:2 * CHUNKS * P].rearrange("p (c n) -> p c n", c=ECH)
        gate_w = w_ffn[:, 2 * CHUNKS * P:2 * CHUNKS * P + EXPERTS]
        bcast = sb("bcast", [P, NB])
        ab2b = bcast[:, 2 * EMB:3 * EMB]
        gcwb = bcast[:, 3 * EMB:5 * EMB].rearrange("p (a e) -> p a e", a=2)
        bob = bcast[:, 5 * EMB:6 * EMB]
        gate_bb = bcast[:, 6 * EMB:6 * EMB + EXPERTS]
        gcb = bcast[:, 6 * EMB + EXPERTS:NB]
        bvb = bcast[:, 0:2 * EMB].rearrange("p (t e) -> p t e", t=TPB)
        vec_rows = sb("vec_rows", [NVEC, P])
        vec_cols = sb("vec_cols", [P, NVEC])
        b1c, cols, lnc = vec_cols, vec_cols[:, CHUNKS:CHUNKS + 2], vec_cols[:, CHUNKS + 2:CHUNKS + 4]
        c_row = sb("c_row", [BATCH, EMB])
        c_exp = sb("c_exp", [BATCH, EMB])
        c_sig = sb("c_sig", [BATCH, EMB])
        c_silu = sb("c_silu", [BATCH, EMB])
        c_t = sb("c_t", [P, BATCH])
        mod_t = sb("mod_t", [P, 2, BATCH])
        gate_b = sb("gate_b", [P, 2, 2, EMB])
        wo_gated = sb("wo_gated", [P, 2, EMB])

        gen = sb("gen", [P, NG, P])
        gen_abs = sb("gen_abs", [P, NG, P])
        gen_t = sb("gen_t", [P, NG, P])
        rot = sb("rot", [P, NG, P])
        rot_t = sb("rot_t", [P, NG, P])
        ident4 = sb("ident4", [P, NG, P])
        nrm = sb("nrm", [P, NG])
        gscale = sb("gscale", [P, NG])
        todo = sb("todo", [P, NG])

        stacks = sb("stacks", [P, 2, 2, HEADS, SEQ], F32R)
        q_stack, k_stack = stacks[:, 0], stacks[:, 1]
        prob = sb("prob", [P, 8, TPB * SEQ])
        v_blocks = sb("v_blocks", [P, 2, TPB, HEADS, VW])
        v_tok = sb("v_tok", [P, TPB, EMB])
        stats = sb("stats", [P, TPB, 6])
        mv = sb("mv", [P, TPB, 2])
        rstd = sb("rstd", [P, TPB])
        var_eps = sb("var_eps", [P, TPB])
        neg_half = sb("neg_half", [P, TPB])
        xhat = sb("xhat", [P, TPB, EMB])
        h_t = sb("h_t", [P, SEQ])
        qk = sb("qk", [P, 2, SEQ])
        qk_parts = sb("qk_parts", [P, 4, SEQ], F32R)
        row_max = sb("row_max", [P, 2, HEADS, TPB])
        max_parts = sb("max_parts", [P, 2, 2, 8 * TPB], F32R)
        max_rows = sb("max_rows", [2 * 8 * TPB, 2, P])
        o_raw = sb("o_raw", [P, 2, SEQ])
        o_rsum = sb("o_rsum", [P, 2, 16])
        o_tok = sb("o_tok", [P, TPB, EMB])
        o_t = sb("o_t", [P, SEQ])

        ew2_t = sb("ew2_t", [P, ECH, P])
        ew2_rot = sb("ew2_rot", [P, ECH, EMB])
        rot_all = sb("rot_all", [P, 3, P])
        eb2 = sb("eb2", [EXPERTS, EMB])
        eb2_t = sb("eb2_t", [P, 4, 32])
        eb2_rot = gen_abs
        eb2_parts = sb("eb2_parts", [P, BT, EMB], F32R)
        diag = sb("diag", [P, BT, EMB])
        gate_parts = sb("gate_parts", [P, 4, 32], F32R)
        gcb_half = sb("gcb_half", [P, 1])
        tri = sb("tri", [P, EXPERTS, EXPERTS])
        mod_rows = sb("mod_rows", [BATCH, 5, EMB])
        mod_tmp = sb("mod_tmp", [BATCH, 2, 2, EMB])
        mod_b = sb("mod_b", [P, 2, 2, 3, EMB])
        st2 = sb("st2", [P, 2, BT, 6])
        mv2 = sb("mv2", [P, 2, BT, 2])
        ve2 = sb("ve2", [P, 2, BT])
        rs2 = sb("rs2", [P, 2, BT])
        nh4 = sb("nh4", [P, BT])
        h2 = sb("h2", [P, 2, BT, EMB])
        xn_tok = sb("xn_tok", [P, BT, EMB])
        xn_t = sb("xn_t", [P, BT * P])
        w1_parts = q_stack[:, 0].rearrange("p h t -> p (h t)").rearrange("p (a m) -> p a m", a=2)
        xn_parts = k_stack[:, 0].rearrange("p h t -> p (h t)")[:, 0:4 * BT * P].rearrange("p (r a m) -> p r a m", r=2, a=2)
        lg = sb("lg", [P, BT, EXPERTS])
        cmp_gt = sb("cmp_gt", [P, BT, EXPERTS, EXPERTS])
        cmp_eq = sb("cmp_eq", [P, BT, EXPERTS, EXPERTS])
        rank = sb("rank", [P, BT, EXPERTS])
        sel = sb("sel", [P, 2, BT, EXPERTS])
        pick = sb("pick", [P, BT, EXPERTS])
        top = sb("top", [P, 3, BT])
        th = sb("th", [P, BT])
        w_gate = sb("w_gate", [P, 2, BT, EXPERTS])
        w_t = sb("w_t", [P, P], F32R)
        hid = prob[:, 0:4, :]
        acc = sb("acc", [P, 2, BT, EMB])
        abel = prob[:, 4:6, :].rearrange("p r (t e) -> p r t e", t=BT)
        zpart = sb("zpart", [P, 2, BT])
        zsum = sb("zsum", [P, BT])
        gth = sb("gth", [P, BT])
        gmix = sb("gmix", [P, BT])
        diff = rot
        y_out = prob[:, 6:8, :].rearrange("p r (t e) -> p r t e", t=BT)

        smax_bank = [ps(f"smax{i}", [P, 512]) for i in range(2)]
        st_bank = [ps(f"st{i}", [P, 512]) for i in range(2)]
        pv_bank = [ps(f"pv{i}", [P, 512]) for i in range(2)]
        mx = ps("mx", [P, 512])
        my = ps("my", [P, 512])

        c_in, w_attn_in, vec_in, bcast_in, gen_in, w_ffn_in = (
            sem(n) for n in ("c_in", "w_attn_in", "vec_in", "bcast_in", "gen_in", "w_ffn_in"))
        eb2_in = sem("eb2_in")
        const_ok, ffn_const, diag_steps, parts_zero, v_blocks_clear = (
            sem(n) for n in ("const_ok", "ffn_const", "diag_steps", "parts_zero", "v_blocks_clear"))
        c_exp_ok, c_steps, c_turned, c_t_ok, mod_pe, mod_ok = (
            sem(n) for n in ("c_exp_ok", "c_steps", "c_turned", "c_t_ok", "mod_pe", "mod_ok"))
        mod_dve, mod_rows_steps, mod_rows_stored = (
            sem(n) for n in ("mod_dve", "mod_rows_steps", "mod_rows_stored"))
        gen_abs_ok, gen_sums_done, gen_steps, gen_turned, gen_t_ok, series_done = (
            sem(n) for n in ("gen_abs_ok", "gen_sums_done", "gen_steps", "gen_turned", "gen_t_ok", "series_done"))
        series_ok, rot_turned_sq, rot_t_sq_ok, square_done, square_steps, rot_ok = (
            sem(n) for n in ("series_ok", "rot_turned_sq", "rot_t_sq_ok", "square_done", "square_steps", "rot_ok"))
        bn_ok, stat_ok, var_ok, rstd_ok, xhat_ok, x_turned = (
            sem(n) for n in ("bn_ok", "stat_ok", "var_ok", "rstd_ok", "xhat_ok", "x_turned"))
        h_ok, qk_done, qk_ok, qk_high_ok, split_ok, v_done = (
            sem(n) for n in ("h_ok", "qk_done", "qk_ok", "qk_high_ok", "split_ok", "v_done"))
        v_ok, v_blocks_ok = (
            sem(n) for n in ("v_ok", "v_blocks_ok"))
        scores_done, row_max_ok, max_high_ok, max_split, max_turned, max_row_ok = (
            sem(n) for n in ("scores_done", "row_max_ok", "max_high_ok", "max_split", "max_turned", "max_row_ok"))
        scores_t_done, exp_done, pv_done, oraw_ok, o_turned, o_rsum_ok = (
            sem(n) for n in ("scores_t_done", "exp_done", "pv_done", "oraw_ok", "o_turned", "o_rsum_ok"))
        o_norm, o_back_done, ot_ok, gated_ok, y_done, residual_ok = (
            sem(n) for n in ("o_norm", "o_back_done", "ot_ok", "gated_ok", "y_done", "residual_ok"))
        ew2_turned, ew2_t_ok, rot_turned, rot_t_ok, rot_product_done, rot_product_ok = (
            sem(n) for n in ("ew2_turned", "ew2_t_ok", "rot_turned", "rot_t_ok", "rot_product_done", "rot_product_ok"))
        ew2_rot_done, ew2_rot_ok, eb2_steps = (
            sem(n) for n in ("ew2_rot_done", "ew2_rot_ok", "eb2_steps"))
        ffn_bn_ok, ffn_stat_ok, ffn_var_ok, ffn_rstd_ok, x_hat_ok, x_scaled = (
            sem(n) for n in ("ffn_bn_ok", "ffn_stat_ok", "ffn_var_ok", "ffn_rstd_ok", "x_hat_ok", "x_scaled"))
        h2_ok, xn_ok, xn_turned, xn_t_ok, xn_high_ok, xn_parts_ok = (
            sem(n) for n in ("h2_ok", "xn_ok", "xn_turned", "xn_t_ok", "xn_high_ok", "xn_parts_ok"))
        logits_done, rank_steps, top_ok, gate_tanh_ok, w_ok, wt_done = (
            sem(n) for n in ("logits_done", "rank_steps", "top_ok", "gate_tanh_ok", "w_ok", "wt_done"))
        wt_ok, biases_done, acc0_ok = (
            sem(n) for n in ("wt_ok", "biases_done", "acc0_ok"))
        w1_hi, w1_ok, layer1_done, gelu_ok, layer2_done, acc_ok = (
            sem(n) for n in ("w1_hi", "w1_ok", "layer1_done", "gelu_ok", "layer2_done", "acc_ok"))
        abel_ok, dense_logit_ok, mix_steps, mix_logit_ok, mix_tanh_ok, diff1 = (
            sem(n) for n in ("abel_ok", "dense_logit_ok", "mix_steps", "mix_logit_ok", "mix_tanh_ok", "diff1"))
        diff_ok, base1, base2, base_ok, y_fin = (
            sem(n) for n in ("diff_ok", "base1", "base2", "base_ok", "y_fin"))
        x_in = [sem(f"x_in{i}") for i in range(3)]
        stack_init = [sem(f"stack_init{i}") for i in range(2)]
        stack_in = [sem(f"stack_in{r}") for r in range(2)]
        max_in = [sem(f"max_in{r}") for r in range(2)]
        d_settled, p_settled = sem("d_settled"), sem("p_settled")
        mod_b_in = [sem(f"mod_b_in{i}") for i in range(2)]
        y_stored = [sem(f"y_stored{i}") for i in range(2)]
        gate_in = [sem(f"gate_in{i}") for i in range(2)]

        block = ctx.enter_context(nc.Block())

        def blocks(eng, step):
            step(0, 0, 0)
            with eng.Fori(0, (BLOCKS - 2) // 2) as i:
                step(i * 2 + 1, 1, 1)
                step(i * 2 + 2, 2, 0)
            step(BLOCKS - 1, BLOCKS - 1, 1)
            step(BLOCKS, BLOCKS, 0)

        def iterations(eng, step, between):
            step(-3, -3, 1)
            step(-2, -2, 0)
            between()
            step(-1, -1, 1)
            step(0, 0, 0)
            with eng.Fori(0, (BATCH - 4) // 2) as i:
                step(i * 2 + 1, 1, 1)
                step(i * 2 + 2, 1, 0)
            for b in range(BATCH - 3, BATCH):
                step(b, b, b % 2)

        def squared(b):
            return b + 1

        def split_qk(eng, b):
            high, low = qk_parts[:, 0:4:2, :], qk_parts[:, 1:4:2, :]
            eng.tensor_copy(high, qk[:]).then_inc(qk_high_ok, 1)
            eng.wait_ge(qk_high_ok, b + 1)
            eng.tensor_tensor(low, qk[:], high.bitcast(F32), ALU.subtract).then_inc(split_ok, 1)

        SERIES_AT = [(-1, n) for n in (4, 7, 10, 13)] + [(0, n) for n in (0, 2, 4, 6, 8, 10)]

        @block.sync
        def _(sp):
            sp.dma_start(x_keep[:, 0:2, :], a["x"][0:2].rearrange("t p e -> p t e")).then_inc(x_in[0], 16)
            sp.dma_start(c_row[:], a["c"]).then_inc(c_in, 16)
            sp.dma_start(vec_rows[:], a["vec_rows"]).then_inc(vec_in, 16)
            sp.dma_start(gen[:], a["gens"].rearrange("g i j -> i g j")).then_inc(gen_in, 16)
            sp.dma_start(w_attn[:].rearrange("p j e -> p (j e)"), a["w_attn"]).then_inc(w_attn_in, 16)
            sp.dma_start(bcast[:], a["bcast"].to_broadcast([P, NB])).then_inc(bcast_in, 16)
            sp.dma_start(x_keep[:, 2:8, :], a["x"][2:8].rearrange("t p e -> p t e")).then_inc(x_in[1], 16)
            sp.dma_start(x_keep[:, 8:TILES, :], a["x"][8:TILES].rearrange("t p e -> p t e")).then_inc(x_in[2], 16)
            sp.dma_start(w_ffn[:], a["w_ffn"]).then_inc(w_ffn_in, 16)
            sp.dma_start(eb2[:], a["eb2"]).then_inc(eb2_in, 16)
            sp.wait_ge(mod_rows_steps, 7)
            sp.dma_start(mod_dram, mod_rows[:]).then_inc(mod_rows_stored, 16)

            def max_dma(b, p, r):
                need(sp, max_row_ok, 2 * b + r + 1)
                sp.dma_start(q_stack[MAXROW:MAXROW + 2, p, 8 * r:8 * r + 8, :].bitcast(F32).rearrange("a h (t q) -> a (h t) q", t=TPB),
                             max_rows[:, r, :]).then_inc(max_in[r], 16)

            def stack_dma(b2, p, r):
                for row, q_part, k_part in ((0, 0, 0), (1, 1, 1), (2, 1, 0), (3, 0, 1)):
                    for stack, part in ((k_stack, 2 + k_part), (q_stack, q_part)):
                        sp.dma_start(stack[HDIM * row:HDIM * (row + 1), p, 8 * r:8 * r + 8, :].bitcast(F32),
                                     qk_parts[64 * r:64 * r + 64, part, :].bitcast(F32)).then_inc(stack_in[r], 16)

            def step(b, f, p):
                if f == BATCH - 3:
                    load_modulation(0, 0)
                if 0 <= f < BATCH:
                    max_dma(b, p, 1)
                    if f == 0:
                        sp.wait_ge(mod_rows_stored, 16)
                    need(sp, gated_ok, b)
                    sp.dma_start(gate_b[:, p], mod_dram[bass.ds(b, 1), 3:5, :].to_broadcast([P, 2, EMB])).then_inc(gate_in[p], 16)
                if 0 <= f + 2 < BATCH:
                    b2 = b + 2
                    need(sp, split_ok, b2 + 1)
                    if f < 0:
                        sp.wait_ge(stack_init[p], 3 if p == 0 else 2)
                    need(sp, scores_t_done, 16 * b + 8)
                    stack_dma(b2, p, 0)
                if 0 <= f + 1 < BATCH:
                    max_dma(b + 1, 1 - p, 0)
                if 0 <= f + 2 < BATCH:
                    need(sp, scores_t_done, 16 * b + 16)
                    stack_dma(b + 2, p, 1)

            def load_modulation(q1, r):
                for i in range(2):
                    sp.dma_start(mod_b[:, r, i], mod_dram[bass.ds(2 * q1 + i, 1), 0:3, :].to_broadcast([P, 3, EMB])).then_inc(mod_b_in[r], 16)

            iterations(sp, step, lambda: None)
            for i in range(2):
                sp.sem_inc(y_stored[i], 16)

            def ffn(q, f, p):
                if 0 <= f - 1 < BLOCKS:
                    sp.wait_ge(y_fin, q)
                    sp.dma_start(out[bass.ds(BT * (q - 1), BT)].rearrange("t p e -> p t e"), y_out[:, 1 - p]).then_inc(y_stored[1 - p], 16)
                if 0 <= f + 1 < BLOCKS:
                    load_modulation(q + 1, 1 - p)
            blocks(sp, ffn)
            for i in range(2):
                sp.wait_ge(y_stored[i], 16 * BLOCKS // 2 + 16)

        @block.gpsimd
        def _(pool):
            pool.memset(ident[:], 0.0).then_inc(const_ok, 1)
            pool.memset(ones[:], 1.0).then_inc(const_ok, 1)
            pool.memset(neg_half[:], -0.5).then_inc(const_ok, 1)
            pool.wait_ge(const_ok, 3)
            pool.affine_select(out=ident[:], in_=ident[:], compare_op=ALU.not_equal, fill=1.0, base=0,
                               pattern=[[-1, P]], channel_multiplier=1).then_inc(const_ok, 1)
            pool.wait_ge(const_ok, 4)
            for g in range(NG):
                pool.tensor_copy(ident4[:, g, :], ident[:]).then_inc(const_ok, 1)
            pool.memset(nh4[:], -0.5).then_inc(ffn_const, 1)
            pool.memset(tri[:], 1.0).then_inc(ffn_const, 1)
            pool.wait_ge(ffn_const, 2)
            pool.affine_select(out=tri[:], in_=tri[:], compare_op=ALU.is_gt, fill=0.0, base=0,
                               pattern=[[1, EXPERTS], [-1, EXPERTS]], channel_multiplier=0).then_inc(ffn_const, 1)
            pool.memset(q_stack[:, 0].bitcast(F32), 0.0).then_inc(stack_init[0], 1)

            def rstd_of(k, q1):
                pool.wait_ge(ffn_stat_ok, 2 * q1 + k + 1)
                settle(pool, p_settled)
                pool.tensor_scalar(ve2[:, k], mv2[:, k, :, 1], EPS, None, ALU.add).then_inc(ffn_var_ok, 1)
                pool.wait_ge(ffn_var_ok, 2 * q1 + k + 1)
                pool.tensor_tensor(rs2[:, k], ve2[:, k], nh4[:], ALU.pow).then_inc(ffn_rstd_ok, 1)

            def over(r, j):
                return mod_b[:, r, :, j:j + 1, :].to_broadcast([P, 2, BT // 2, EMB])

            def by_batch(v):
                return v.rearrange("p (b t) e -> p b t e", b=2)

            def front(q1, r):
                pool.wait_ge(mod_b_in[r], 16 * (q1 - r) + 32)
                pool.wait_ge(x_hat_ok, q1 + 1)
                h4 = by_batch(h2[:, r])
                pool.tensor_tensor(h4, h4, over(r, 1), ALU.mult).then_inc(x_scaled, 1)
                pool.wait_ge(x_scaled, q1 + 1)
                pool.tensor_tensor(h4, h4, over(r, 0), ALU.add).then_inc(h2_ok, 1)
                rstd_of(1, q1)

            def step(b, f, p):
                if 0 <= f + 1 < BATCH:
                    b1, q = b + 1, 1 - p
                    if f == -1:
                        pool.wait_ge(v_blocks_clear, 1)
                        for i in range(2):
                            for buf in range(2):
                                for t in range(TPB):
                                    v = v_blocks[:, buf, t].rearrange("k (m i) w -> k m i w", i=2)
                                    pool.memset(v[:, :, i, OW * i + HDIM:OW * i + OW], 1.0)
                    need(pool, v_ok, b1 + 1)
                    need(pool, pv_done, 4 * b)
                    settle(pool, p_settled)
                    for t in range(TPB):
                        dst = bass.AP(tensor=v_blocks, offset=v_blocks[:, q, t, 0, 0:1].offset,
                                      ap=[v_blocks[:].ap[0], [2 * VW, 8], [VW + OW, 2], [1, HDIM]])
                        last = pool.tensor_copy(dst, v_tok[:, t, :].rearrange("k (m i d) -> k m i d", i=2, d=HDIM))
                    last.then_inc(v_blocks_ok, 1)
                if 0 <= f + 2 < BATCH:
                    b2 = b + 2
                    need(pool, qk_ok, b2 + 1)
                    need(pool, stack_in[0], 128 * b2)
                    need(pool, stack_in[1], 128 * b2)
                    settle(pool, p_settled)
                    if f > -2:
                        split_qk(pool, b2)
                if 0 <= f + 3 < BATCH:
                    b3 = b + 3
                    pool.wait_ge(stat_ok, b3 + 1)
                    settle(pool, p_settled)
                    pool.tensor_scalar(var_eps[:], mv[:, :, 1], EPS, None, ALU.add).then_inc(var_ok, 1)
                    pool.wait_ge(var_ok, b3 + 1)
                    pool.tensor_tensor(rstd[:], var_eps[:], neg_half[:], ALU.pow).then_inc(rstd_ok, 1)
                    pool.wait_ge(rstd_ok, b3 + 1)
                if f == -3:
                    pool.memset(q_stack[:, 1].bitcast(F32), 0.0).then_inc(stack_init[1], 1)
                    pool.memset(v_blocks[:], 0.0).then_inc(v_blocks_clear, 1)
                    pool.memset(eb2_t[:], 0.0).then_inc(parts_zero, 1)
                    pool.memset(gate_parts[:].bitcast(F32), 0.0).then_inc(parts_zero, 1)
                    pool.memset(diag[:], 1.0).then_inc(ffn_const, 1)
                    pool.memset(k_stack[:, 1].bitcast(F32), 1.0).then_inc(stack_init[1], 1)
                    pool.wait_ge(bcast_in, 16)
                    pool.tensor_scalar(gcb_half[:], gcb[:], 0.5, None, ALU.mult).then_inc(ffn_const, 1)

                if f == -1:
                    pool.wait_ge(ffn_const, 5)
                    for bound, sign in ((0, 1), (EXPERTS - 1, -1)):
                        for i in range(4):
                            rows = diag[32 * i:32 * (i + 1)]
                            pool.affine_select(out=rows, in_=rows, compare_op=ALU.is_ge, fill=0.0, base=bound,
                                               pattern=[[-sign * EXPERTS, BT], [0, EMB]], channel_multiplier=sign).then_inc(diag_steps, 1)
                        pool.wait_ge(diag_steps, 4 if sign == 1 else 8)

                if f == BATCH - 3:
                    rstd_of(0, 0)
                if f == BATCH - 2:
                    front(0, 0)
                if 0 <= f < BATCH:
                    pool.wait_ge(gate_in[p], 8 * (b - p) + 16)
                    need(pool, y_done, b)
                    settle(pool, p_settled)
                    pool.tensor_tensor(wo_gated[:, p], wo, gate_b[:, p, 0], ALU.mult)
                    xs = x_keep[:, bass.ds(TPB * b, TPB), :]
                    pool.tensor_tensor(xs, xs, gate_b[:, p, 1:2, :].to_broadcast([P, TPB, EMB]), ALU.add).then_inc(gated_ok, 1)

            iterations(pool, step, lambda: None)

            def ffn(q, f, p):
                if 0 <= f + 1 < BLOCKS:
                    rstd_of(0, q + 1)
                if 0 <= f - 1 < BLOCKS:
                    pool.wait_ge(acc_ok, EXPERTS * q)
                    need(pool, y_fin, q - 1)
                    pool.tensor_tensor(diff[:], acc[:, 1 - p], abel[:, 1 - p], ALU.subtract).then_inc(diff1, 1)
                    pool.wait_ge(diff1, q)
                    pool.tensor_tensor(by_batch(diff[:]), by_batch(diff[:]), over(1 - p, 2), ALU.mult).then_inc(diff_ok, 1)
                if 0 <= f + 1 < BLOCKS:
                    front(q + 1, 1 - p)
                if 0 <= f < BLOCKS:
                    pool.wait_ge(abel_ok, q + 1)
                    pool.wait_ge(y_stored[p], 8 * (q - p) + 16)
                    settle(pool, p_settled)
                    y = y_out[:, p]
                    pool.tensor_tensor(y, abel[:, p], h2[:, p], ALU.add).then_inc(base1, 1)
                    pool.wait_ge(base1, q + 1)
                    pool.tensor_tensor(by_batch(y), by_batch(y), over(p, 2), ALU.mult).then_inc(base2, 1)
                    pool.wait_ge(base2, q + 1)
                    pool.tensor_tensor(y, y, x_keep[:, bass.ds(BT * q, BT), :], ALU.add).then_inc(base_ok, 1)

            blocks(pool, ffn)

        @block.scalar
        def _(act):
            act.wait_ge(c_in, 16)
            act.activation(c_exp[:], c_row[:], ACT.Exp, scale=-1.0).then_inc(c_exp_ok, 1)
            act.wait_ge(gen_in, 16)
            act.activation(gen_abs[:], gen[:], ACT.Abs).then_inc(gen_abs_ok, 1)
            act.wait_ge(c_turned, 1)
            act.activation(vec_cols[:], mx[:, 32:32 + NVEC], ACT.Identity)
            act.activation(c_t[:], mx[:, 0:BATCH], ACT.Identity).then_inc(c_t_ok, 1)

            def o_evac(b, r):
                act.wait_ge(pv_done, 4 * b + 2 * r + 2)
                act.activation(o_raw[:, r, :], pv_bank[r][:, 0:SEQ], ACT.Identity).then_inc(oraw_ok, 1)

            def o_turn(b):
                act.wait_ge(o_back_done, b + 1)
                act.activation(o_t[:], my[:, 0:SEQ], ACT.Identity).then_inc(ot_ok, 1)

            def turn_rot(m, bank=pv_bank[0]):
                act.wait_ge(rot_turned_sq, m)
                act.activation(rot_t[:], bank[:].rearrange("p (g j) -> p g j", g=NG), ACT.Identity).then_inc(rot_t_sq_ok, 1)

            def xn_evac(q1, bank):
                act.wait_ge(xn_turned, q1 + 1)
                act.activation(xn_t[:], bank[:], ACT.Identity, scale=lnc[:, 0:1], bias=lnc[:, 1:2]).then_inc(xn_t_ok, 1)

            def gate_tanh(q1):
                act.wait_ge(top_ok, q1 + 1)
                act.activation(th[:], top[:, 2], ACT.Tanh, scale=0.5).then_inc(gate_tanh_ok, 1)

            def step(b, f, p):
                live, pre, post = 0 <= f < BATCH, 0 <= f + 2 < BATCH, 0 <= f - 1 < BATCH
                for n in range(HEADS):
                    if live:
                        act.wait_ge(scores_t_done, 16 * b + n + 1)
                        need(act, pv_done, 4 * b + n // 4 - 1)
                        act.activation(prob[:, n % 8, :], st_bank[n % 2][:], ACT.Exp, scale=SCALE).then_inc(exp_done, 1)
                    if n == SLOT["x_modulate"] and pre:
                        act.wait_ge(x_turned, b + 3)
                        if f == -2:
                            act.wait_ge(mod_dve, 1)
                        act.activation(h_t[:], mx[:, 0:SEQ], ACT.Identity, scale=mod_t[:, 1, bass.ds(b + 2, 1)],
                                       bias=mod_t[:, 0, bass.ds(b + 2, 1)]).then_inc(h_ok, 1)
                    if n == SLOT["o_evac1"] and post:
                        o_evac(b - 1, 1)
                    if n == SLOT["qk_bias"] and pre:
                        act.wait_ge(qk_done, b + 3)
                        need(act, split_ok, b + 2)
                        for i in range(2):
                            last = act.activation(qk[:, i, :], mx[:, SEQ * i:SEQ * (i + 1)], ACT.Identity, bias=cols[:, i:i + 1])
                        last.then_inc(qk_ok, 1)
                    if n == SLOT["o_back_evac"] and post:
                        o_turn(b - 1)
                    if n == SLOT["o_evac0"] and live:
                        o_evac(b, 0)
                    if f == BATCH - 1 and n == 2:
                        turn_rot(SQUARINGS, smax_bank[1])
                    if n == SLOT["square_turn_evac"] and live and f < BATCH - 1:
                        turn_rot(squared(b))
                    if f == -1 and n == 1:
                        act.wait_ge(gen_turned, 1)
                        act.activation(gen_t[:], pv_bank[1][:].rearrange("p (g j) -> p g j", g=NG), ACT.Identity).then_inc(gen_t_ok, 1)
                    if f == -1 and n in (8, 10, 12):
                        k = (n - 8) // 2
                        act.wait_ge(ew2_turned, k + 1)
                        act.activation(ew2_t[:, 4 * k:4 * k + 4, :], pv_bank[0][:].rearrange("p (c j) -> p c j", c=4), ACT.Identity).then_inc(ew2_t_ok, 1)
                    if f == -1 and n == 14:
                        act.wait_ge(ew2_turned, 4)
                        act.wait_ge(parts_zero, 1)
                        for i in range(4):
                            last = act.activation(eb2_t[:, i, 0:BT * EXPERTS].rearrange("p (t e) -> p t e", e=EXPERTS),
                                                  pv_bank[0][:, 0:EXPERTS].rearrange("p (o e) -> p o e", o=1).to_broadcast([P, BT, EXPERTS]), ACT.Identity)
                        last.then_inc(ew2_t_ok, 1)
                    if f == BATCH - 1:
                        if n == 8:
                            act.wait_ge(rot_turned, 1)
                            act.activation(rot_t[:], smax_bank[1][:].rearrange("p (g j) -> p g j", g=NG), ACT.Identity).then_inc(rot_t_ok, 1)
                        if n == 2:
                            xn_evac(0, smax_bank[0])

            iterations(act, step, lambda: None)

            def ffn(q, f, p):
                for c in range(CHUNKS):
                    if 0 <= f < BLOCKS:
                        need(act, layer2_done, CHUNKS * q + c - 3)
                        act.wait_ge(layer1_done, CHUNKS * q + c + 1)
                        act.activation(hid[:, c % 4, :], smax_bank[c % 2][:], ACT.Gelu, bias=b1c[:, c:c + 1]).then_inc(gelu_ok, 1)
                    if 0 <= f + 1 < BLOCKS and c == CHUNK["xn_evac"]:
                        xn_evac(q + 1, mx)
                    if 0 <= f < BLOCKS and c == CHUNK["gate_tanh"]:
                        gate_tanh(q)
                    if c == CHUNK["mix_tanh"] and 0 <= f - 1 < BLOCKS:
                        act.wait_ge(mix_logit_ok, q)
                        act.activation(gth[:], zsum[:], ACT.Tanh, scale=0.5, bias=gcb_half[:]).then_inc(mix_tanh_ok, 1)
                    if f == 0:
                        if c == 0:
                            o_evac(BATCH - 1, 1)
                        if c == 3:
                            o_turn(BATCH - 1)

            act.wait_ge(ffn_const, 5)
            blocks(act, ffn)

        @block.tensor
        def _(pe):
            pe.wait_ge(const_ok, 4)
            pe.wait_ge(vec_in, 16)
            pe.transpose(mx[:, 32:32 + NVEC], vec_rows[:], ident[0:NVEC, 0:NVEC])
            pe.wait_ge(c_steps, 3)
            pe.transpose(mx[:, 0:BATCH], c_silu[:], ident[0:BATCH, 0:BATCH]).then_inc(c_turned, 1)
            pe.wait_ge(c_t_ok, 1)
            pe.wait_ge(w_attn_in, 16)
            pe.matmul(mx[0:BATCH, 128:128 + 3 * EMB], c_t[:], wmod[:, 3 * EMB:6 * EMB], start=True, stop=True)
            pe.matmul(my[0:BATCH, 0:EMB], c_t[:], wmod[:, 2 * EMB:3 * EMB], start=True, stop=True)
            for j in range(2):
                last = pe.matmul(mx[:, 32 + BATCH * j:32 + BATCH * (j + 1)], wmod[:, EMB * j:EMB * (j + 1)], c_t[:], start=True, stop=True)
            last.then_inc(mod_pe, 1)

            def pv(b, p, g):
                r, i = g // 2, g % 2
                if g == 0:
                    pe.wait_ge(v_blocks_ok, b + 1)
                if i == 0:
                    need(pe, oraw_ok, 2 * b - 1 + r)
                pe.wait_ge(exp_done, 16 * b + 4 * g + 4)
                for t in range(TPB):
                    for j in range(4):
                        last = pe.matmul(pv_bank[r][VW * j:VW * (j + 1), 0:SEQ], v_blocks[:, p, t, 8 * r + 2 * j + i, :],
                                         prob[:, (4 * g + j) % 8, SEQ * t:SEQ * (t + 1)],
                                         start=(i == 0 and t == 0), stop=(i == 1 and t == TPB - 1))
                last.then_inc(pv_done, 1)

            def o_transposes(b, r, bank):
                pe.wait_ge(oraw_ok, 2 * b + r + 1)
                for t in range(TPB):
                    last = pe.transpose(bank[:, P * t:P * (t + 1)], o_raw[:, r, P * t:P * (t + 1)], ident[:])
                last.then_inc(o_turned, 1)

            def o_back(b):
                pe.wait_ge(o_norm, 2 * b + 2)
                for t in range(TPB):
                    last = pe.transpose(my[:, P * t:P * (t + 1)], o_tok[:, t, :], ident[:])
                last.then_inc(o_back_done, 1)

            def project(b, par):
                pe.wait_ge(ot_ok, b + 1)
                pe.wait_ge(gated_ok, b + 1)
                for t in range(TPB):
                    last = pe.matmul(mx[:, EMB * t:EMB * (t + 1)], o_t[:, P * t:P * (t + 1)], wo_gated[:, par], start=True, stop=True)
                last.then_inc(y_done, 1)

            def max_transposes(b, r, bank):
                pe.wait_ge(max_split, 2 * b + r + 1)
                pe.transpose(bank[0:2 * 8 * TPB, 0:P], max_parts[:, r].bitcast(F32).rearrange("p a h -> p (a h)"), ident[:]).then_inc(max_turned, 1)

            def square_turn(m, bank=pv_bank[0]):
                need(pe, rot_ok, m - 1)
                for g in range(NG):
                    last = pe.transpose(bank[:, P * g:P * (g + 1)], rot[:, g, :], ident[:])
                last.then_inc(rot_turned_sq, 1)

            def square(m, bank=pv_bank[0]):
                pe.wait_ge(rot_t_sq_ok, m)
                for g in range(NG):
                    last = pe.matmul(bank[:, P * g:P * (g + 1)], rot_t[:, g, :], rot[:, g, :], start=True, stop=True)
                last.then_inc(square_done, 1)

            def horner(k):
                if k:
                    pe.wait_ge(series_ok, k)
                else:
                    pe.wait_ge(gen_t_ok, 1)
                    pe.wait_ge(const_ok, 8)
                for g in range(NG):
                    last = pe.matmul(pv_bank[1][:, P * g:P * (g + 1)], gen_t[:, g, :], (rot if k else ident4)[:, g, :], start=True, stop=True)
                last.then_inc(series_done, 1)

            def turn_block(q1, bank):
                pe.wait_ge(xn_ok, q1 + 1)
                for t in range(BT):
                    last = pe.transpose(bank[:, P * t:P * (t + 1)], xn_tok[:, t, :], ident[:])
                last.then_inc(xn_turned, 1)

            def logits(q1, bank):
                pe.wait_ge(xn_t_ok, q1 + 1)
                for t in range(BT):
                    last = pe.matmul(bank[:, 8 * t:8 * t + EXPERTS], xn_t[:, P * t:P * (t + 1)], gate_w, start=True, stop=True)
                last.then_inc(logits_done, 1)

            def rotate_product(k):
                if k == 0:
                    pe.wait_ge(rot_t_ok, 1)
                need(pe, rot_product_ok, k)
                pe.matmul(smax_bank[1][:, 0:P], rot_t[:, NG - 2 - k, :], rot[:, NG - 1, :] if k == 0 else rot_all[:, k - 1, :],
                          start=True, stop=True).then_inc(rot_product_done, 1)

            def rotate_weights(k):
                if k < 3:
                    for c in range(4):
                        last = pe.matmul(st_bank[k % 2][:, P * c:P * (c + 1)], ew2_t[:, 4 * k + c, :], rot_all[:, NG - 2, :], start=True, stop=True)
                else:
                    last = pe.matmul(st_bank[1][:, 0:EMB], eb2_t[:].rearrange("p i r -> p (i r)"), rot_all[:, NG - 2, :], start=True, stop=True)
                last.then_inc(ew2_rot_done, 1)

            def step(b, f, p):
                live, smax, pre, post = 0 <= f < BATCH, 0 <= f + 1 < BATCH, 0 <= f + 2 < BATCH, 0 <= f - 1 < BATCH
                for n in range(HEADS):
                    if smax:
                        if n % 8 == 0:
                            pe.wait_ge(stack_in[n // 8], 128 * (b + 2))
                        need(pe, row_max_ok, 16 * (b + 1) + n - 1)
                        for t in range(TPB):
                            last = pe.matmul(smax_bank[n % 2][:, SEQ * t:SEQ * (t + 1)],
                                             q_stack[0:MAXROW, 1 - p, n, P * t:P * (t + 1)],
                                             k_stack[0:MAXROW, 1 - p, n, :], start=True, stop=True)
                        last.then_inc(scores_done, 1)
                    if live:
                        h = head_at(n)
                        if n % 8 == 0:
                            pe.wait_ge(max_in[n // 8], 16 * (b + 1))
                        need(pe, exp_done, 16 * b + n - 1)
                        for t in range(TPB):
                            last = pe.matmul(st_bank[n % 2][:, SEQ * t:SEQ * (t + 1)], k_stack[:, p, h, P * t:P * (t + 1)],
                                             q_stack[:, p, h, :], start=True, stop=True)
                        last.then_inc(scores_t_done, 1)
                    if n == SLOT["x_turn"] and pre:
                        pe.wait_ge(xhat_ok, b + 3)
                        if f == -2:
                            pe.wait_ge(mod_ok, 3)
                        if f == -1:
                            pe.wait_ge(qk_ok, 1)
                        need(pe, max_row_ok, 2 * b + 1)
                        for t in range(TPB):
                            last = pe.transpose(mx[:, P * t:P * (t + 1)], xhat[:, t, :], ident[:])
                        last.then_inc(x_turned, 1)
                    if n == SLOT["max_turn1"] and live:
                        need(pe, o_norm, 2 * b - 1)
                        if f == 0:
                            pe.wait_ge(v_ok, 2)
                        max_transposes(b, 1, my)
                    if n == SLOT["pv3"] and post:
                        pv(b - 1, 1 - p, 3)
                    if n == SLOT["qk"] and pre:
                        pe.wait_ge(h_ok, b + 3)
                        for i, w in enumerate((wq, wk)):
                            last = pe.matmul(mx[:, SEQ * i:SEQ * (i + 1)], w, h_t[:], start=True, stop=True)
                        last.then_inc(qk_done, 1)
                    if n == SLOT["v"] and pre:
                        need(pe, max_row_ok, 2 * b + 2)
                        if f == -1:
                            pe.wait_ge(v_ok, 1)
                        for t in range(TPB):
                            last = pe.matmul(my[:, EMB * t:EMB * (t + 1)], h_t[:, P * t:P * (t + 1)], wv, start=True, stop=True)
                        last.then_inc(v_done, 1)
                    if n == SLOT["o_turn1"] and post:
                        if pre:
                            pe.wait_ge(qk_ok, b + 3)
                        else:
                            pe.wait_ge(max_row_ok, 2 * b + 1)
                        o_transposes(b - 1, 1, mx)
                    if n == SLOT["pv0"] and live:
                        if f == 0:
                            pe.wait_ge(ew2_t_ok, 4)
                        else:
                            pe.wait_ge(rot_ok, squared(b - 1))
                        pv(b, p, 0)
                    if n == SLOT["o_back"] and post:
                        if pre:
                            pe.wait_ge(v_ok, b + 3)
                        else:
                            pe.wait_ge(max_row_ok, 2 * b + 2)
                        o_back(b - 1)
                    if n == SLOT["project"] and post:
                        project(b - 1, 1 - p)
                    if n == SLOT["pv1"] and live:
                        pv(b, p, 1)
                    if n == SLOT["max_turn0"] and smax:
                        if post:
                            pe.wait_ge(residual_ok, b)
                        else:
                            pe.wait_ge(qk_ok, b + 3)
                        max_transposes(b + 1, 0, mx)
                    if n == SLOT["o_turn0"] and live:
                        if post:
                            pe.wait_ge(ot_ok, b)
                        else:
                            pe.wait_ge(v_ok, 3)
                        o_transposes(b, 0, my)
                    if n == SLOT["pv2"] and live:
                        if f == 0:
                            pe.wait_ge(series_ok, TAYLOR)
                        pv(b, p, 2)
                    if n == SLOT["square_turn"] and live and f < BATCH - 1:
                        if f == 0:
                            pe.wait_ge(series_ok, TAYLOR)
                        pe.wait_ge(oraw_ok, 2 * b + 1)
                        square_turn(squared(b))
                    if n == SLOT["square"] and live and f < BATCH - 1:
                        square(squared(b))
                    if (f, n) in SERIES_AT:
                        horner(SERIES_AT.index((f, n)))
                    if f == -1:
                        if n == 1:
                            pe.wait_ge(gen_steps, 8)
                            for g in range(NG):
                                last = pe.transpose(pv_bank[1][:, P * g:P * (g + 1)], gen[:, g, :], ident[:])
                            last.then_inc(gen_turned, 1)
                        if n == 8:
                            pe.wait_ge(w_ffn_in, 16)
                        if n in (8, 10, 12):
                            k = (n - 8) // 2
                            need(pe, ew2_t_ok, k)
                            for c in range(4):
                                last = pe.transpose(pv_bank[0][:, P * c:P * (c + 1)], ew2[:, 4 * k + c, :], ident[:])
                            last.then_inc(ew2_turned, 1)
                        if n == 14:
                            pe.wait_ge(ew2_t_ok, 3)
                            pe.wait_ge(eb2_in, 16)
                            pe.transpose(pv_bank[0][:, 0:EXPERTS], eb2[:], ident[0:EXPERTS, 0:EXPERTS]).then_inc(ew2_turned, 1)
                    if f == BATCH - 1:
                        if n == 1:
                            pe.wait_ge(row_max_ok, 16 * BATCH)
                            square_turn(SQUARINGS, smax_bank[1])
                        if n == 4:
                            square(SQUARINGS, smax_bank[1])
                        if n == 7:
                            pe.wait_ge(rot_ok, SQUARINGS)
                            for g in range(NG):
                                last = pe.transpose(smax_bank[1][:, P * g:P * (g + 1)], rot[:, g, :], ident[:])
                            last.then_inc(rot_turned, 1)
                        if n == 1:
                            turn_block(0, smax_bank[0])
                        if n == 4:
                            logits(0, smax_bank[0])
                        if n in (10, 12, 14):
                            rotate_product((n - 10) // 2)

            def between():
                pe.wait_ge(gen_abs_ok, 1)
                pe.matmul(pv_bank[0][:], ones[:], gen_abs[:].rearrange("p g j -> p (g j)"), start=True, stop=True).then_inc(gen_sums_done, 1)

            iterations(pe, step, between)

            def m2(q, p, c):
                pe.wait_ge(gelu_ok, CHUNKS * q + c + 1)
                if c < ACH:
                    bank, w, first, final = pv_bank[0], aw2[:, c, :], c == 0, c == ACH - 1
                    if first:
                        need(pe, abel_ok, q)
                else:
                    e = (c - ACH) // 2
                    bank, w, first, final = st_bank[e % 2], ew2_rot[:, c - ACH, :], c % 2 == 0, c % 2 == 1
                    if first:
                        need(pe, acc_ok, EXPERTS * q + e - 1)
                for t in range(BT):
                    last = pe.matmul(bank[:, EMB * t:EMB * (t + 1)], hid[:, c % 4, P * t:P * (t + 1)], w,
                                     start=first and t == 0, stop=final, skip_group_check=True)
                last.then_inc(layer2_done, 1)

            def ffn(q, f, p):
                live, front = 0 <= f < BLOCKS, 0 <= f + 1 < BLOCKS
                for c in range(CHUNKS):
                    if live:
                        if c == 0:
                            pe.wait_ge(xn_parts_ok, q + 1)
                            if f == 0:
                                pe.wait_ge(w1_ok, 1)
                                pe.wait_ge(rank_steps, 1)
                                pe.wait_ge(rot_product_ok, NG - 1)
                        need(pe, gelu_ok, CHUNKS * q + c - 1)
                        for i, (wi, xi) in enumerate(((0, 0), (1, 0), (0, 1))):
                            last = pe.matmul(smax_bank[c % 2][:], w1_parts[:, wi, P * c:P * (c + 1)], xn_parts[:, p, xi, :],
                                             start=i == 0, stop=i == 2)
                        last.then_inc(layer1_done, 1)
                    if c == 0:
                        if 0 <= f - 1 < BLOCKS:
                            m2(q - 1, 1 - p, CHUNKS - 1)
                    elif live:
                        m2(q, p, c - 1)
                    if f == 0:
                        if c == 0:
                            pv(BATCH - 1, 1, 3)
                            pe.wait_ge(exp_done, 16 * BATCH)
                            rotate_weights(0)
                            rotate_weights(1)
                        if c == 1:
                            pe.wait_ge(residual_ok, BATCH - 1)
                            o_transposes(BATCH - 1, 1, mx)
                            pe.wait_ge(ew2_rot_ok, 2)
                            rotate_weights(2)
                            rotate_weights(3)
                        if c == 3:
                            o_back(BATCH - 1)
                        if c == 4:
                            pe.wait_ge(ew2_rot_ok, 4)
                            pe.wait_ge(ot_ok, BATCH)
                        if c == 10:
                            pe.wait_ge(residual_ok, BATCH)
                    if live and c == CHUNK["gates_turn"]:
                        pe.wait_ge(w_ok, q + 1)
                        if f == 0:
                            pe.wait_ge(o_norm, 2 * BATCH)
                        pe.transpose(mx[:, 0:P], gate_parts[:].bitcast(F32).rearrange("p i r -> p (i r)"), ident[:]).then_inc(wt_done, 1)
                    if f == 0 and c == 5:
                        pe.wait_ge(wt_ok, 1)
                        project(BATCH - 1, 1)
                    if live and c == CHUNK["biases"]:
                        pe.wait_ge(wt_ok, q + 1)
                        pe.matmul(my[:], w_t[:], eb2_parts[:].rearrange("p t e -> p (t e)"), start=True, stop=True).then_inc(biases_done, 1)
                    if front and c == CHUNK["xn_turn"]:
                        turn_block(q + 1, mx)
                    if front and c == CHUNK["logits"]:
                        pe.wait_ge(acc0_ok, q + 1)
                        logits(q + 1, my)

            blocks(pe, ffn)

        @block.vector
        def _(dve):
            dve.memset(k_stack[:, 0, 0:8, :].bitcast(F32), 1.0).then_inc(stack_init[0], 1)
            dve.wait_ge(c_exp_ok, 1)
            dve.tensor_scalar(c_exp[:], c_exp[:], 1.0, None, ALU.add).then_inc(c_steps, 1)
            dve.wait_ge(c_steps, 1)
            dve.reciprocal(c_sig[:], c_exp[:]).then_inc(c_steps, 1)
            dve.wait_ge(c_steps, 2)
            dve.tensor_tensor(c_silu[:], c_row[:], c_sig[:], ALU.mult).then_inc(c_steps, 1)

            def modulations():
                dve.wait_ge(mod_pe, 1)
                dve.tensor_copy(mod_t[:], mx[:, 32:32 + 2 * BATCH].rearrange("p (j b) -> p j b", j=2)).then_inc(mod_ok, 1)
                dve.wait_ge(mod_ok, 1)
                dve.tensor_scalar(mod_t[:, 1, :], mod_t[:, 1, :], 1.0, None, ALU.add).then_inc(mod_dve, 1)
                dve.tensor_copy(mod_rows[:, 0:3], mx[0:BATCH, 128:128 + 3 * EMB].rearrange("p (j e) -> p j e", j=3)).then_inc(mod_ok, 1)
                dve.tensor_copy(mod_rows[:, 3], my[0:BATCH, 0:EMB]).then_inc(mod_ok, 1)
                dve.wait_ge(mod_ok, 3)
                dve.tensor_scalar(mod_rows[:, 1, :], mod_rows[:, 1, :], 1.0, None, ALU.add).then_inc(mod_rows_steps, 1)
                gates, sign, size = mod_rows[:, 2:4], mod_tmp[:, 1], mod_tmp[:, 0]
                dve.tensor_scalar(sign, gates, 0.0, None, ALU.is_ge).then_inc(mod_rows_steps, 1)
                dve.wait_ge(mod_rows_steps, 2)
                dve.tensor_scalar(sign, sign, 2.0, -1.0, ALU.mult, ALU.add).then_inc(mod_rows_steps, 1)
                dve.wait_ge(mod_rows_steps, 3)
                dve.tensor_tensor(size, gates, sign, ALU.mult).then_inc(mod_rows_steps, 1)
                dve.wait_ge(mod_rows_steps, 4)
                dve.scalar_tensor_tensor(out=gates, in0=size, scalar=0.25, in1=sign, op0=ALU.max, op1=ALU.mult).then_inc(mod_rows_steps, 1)
                dve.wait_ge(mod_rows_steps, 5)
                dve.wait_ge(bcast_in, 16)
                dve.tensor_tensor(mod_rows[:, 4], mod_rows[:, 3], bob[0:BATCH, :], ALU.mult).then_inc(mod_rows_steps, 2)

            def series(k):
                if k == 0:
                    dve.wait_ge(const_ok, 8)
                dve.wait_ge(series_done, k + 1)
                dve.scalar_tensor_tensor(out=rot[:].rearrange("p g j -> p (g j)"), in0=pv_bank[1][:], scalar=1.0 / (TAYLOR - k),
                                         in1=ident4[:].rearrange("p g j -> p (g j)"), op0=ALU.mult, op1=ALU.add).then_inc(series_ok, 1)

            def between():
                dve.wait_ge(gen_sums_done, 1)
                dve.tensor_reduce(nrm[:], pv_bank[0][:].rearrange("p (g j) -> p g j", g=NG), AX_X, ALU.max).then_inc(gen_steps, 1)
                dve.wait_ge(gen_steps, 1)
                dve.tensor_scalar(nrm[:], nrm[:], 2.0, 2.0 ** -100, ALU.mult, ALU.max).then_inc(gen_steps, 1)
                dve.wait_ge(gen_steps, 2)
                dve.tensor_scalar(nrm[:].bitcast(U32), nrm[:].bitcast(U32), 0x7F800000, None, ALU.bitwise_and).then_inc(gen_steps, 1)
                dve.wait_ge(gen_steps, 3)
                dve.reciprocal(gscale[:], nrm[:]).then_inc(gen_steps, 1)
                dve.wait_ge(gen_steps, 4)
                dve.tensor_scalar(gscale[:], gscale[:], 1.0, 2.0 ** -SQUARINGS, ALU.min, ALU.max).then_inc(gen_steps, 1)
                dve.wait_ge(gen_steps, 5)
                for g in range(NG):
                    last = dve.tensor_scalar(gen[:, g, :], gen[:, g, :], gscale[:, g:g + 1], None, ALU.mult)
                last.then_inc(gen_steps, 3)

            def split_max(b, p, r):
                hs = slice(8 * r, 8 * r + 8)
                dve.wait_ge(row_max_ok, 16 * b + 8 * r + 8)
                need(dve, max_turned, 2 * b - 1 + r)
                new = row_max[:, p, hs, :].rearrange("p h t -> p (h t)")
                dve.tensor_scalar(max_parts[:, r, 0, :], new, -1.0, None, ALU.mult).then_inc(max_high_ok, 1)
                dve.wait_ge(max_high_ok, 2 * b + r + 1)
                dve.scalar_tensor_tensor(out=max_parts[:, r, 1, :], in0=new, scalar=-1.0,
                                         in1=max_parts[:, r, 0, :].bitcast(F32), op0=ALU.mult, op1=ALU.subtract).then_inc(max_split, 1)

            def max_row(b, r, bank):
                dve.wait_ge(max_turned, 2 * b + r + 1)
                need(dve, max_in[r], 16 * b)
                dve.tensor_copy(max_rows[:, r, :], bank[0:2 * 8 * TPB, 0:P]).then_inc(max_row_ok, 1)

            def normalise(b, r, bank):
                dve.wait_ge(o_turned, 2 * b + r + 1)
                o = bank[:, 0:SEQ].rearrange("p (m w) -> p m w", w=VW)[:, :, 0:2 * OW].rearrange("p m (i d) -> p m i d", i=2)
                dve.reciprocal(o_rsum[:, r, :].rearrange("p (m i) -> p m i", i=2), o[:, :, :, HDIM]).then_inc(o_rsum_ok, 1)
                dve.wait_ge(o_rsum_ok, 2 * b + r + 1)
                need(dve, o_back_done, b)
                dve.tensor_tensor(o_tok[:, :, 64 * r:64 * r + 64].rearrange("p t (j i d) -> p t j i d", i=2, d=HDIM),
                                  o[:, :, :, 0:HDIM].rearrange("p (t j) i d -> p t j i d", t=TPB),
                                  o_rsum[:, r, :].rearrange("p (t j i o) -> p t j i o", t=TPB, i=2, o=1).to_broadcast([P, TPB, 4, 2, HDIM]),
                                  ALU.mult).then_inc(o_norm, 1)

            def add_attention(b):
                dve.wait_ge(y_done, b + 1)
                xs = x_keep[:, bass.ds(TPB * b, TPB), :]
                dve.tensor_tensor(xs, mx[:, 0:SEQ].rearrange("p (t e) -> p t e", t=TPB), xs, ALU.add).then_inc(residual_ok, 1)

            def squaring_due(m):
                need(dve, rot_ok, m - 1)
                dve.tensor_scalar(todo[:], gscale[:], 0.75, None, ALU.is_lt).then_inc(square_steps, 1)
                dve.wait_ge(square_steps, 2 * m - 1)
                dve.scalar_tensor_tensor(out=gscale[:], in0=todo[:], scalar=1.0, in1=gscale[:], op0=ALU.add, op1=ALU.mult).then_inc(square_steps, 1)

            def take_square(m, bank=pv_bank[0]):
                dve.wait_ge(square_done, m)
                dve.wait_ge(square_steps, 2 * m)
                settle(dve, d_settled)
                dve.copy_predicated(out=rot[:], mask=todo[:].bitcast(U32).rearrange("p (g o) -> p g o", o=1).to_broadcast([P, NG, P]),
                                    data=bank[:].rearrange("p (g j) -> p g j", g=NG)).then_inc(rot_ok, 1)

            def tile(t):
                return x_keep[:, bass.ds(t, 1), :].rearrange("p o e -> p (o e)")

            def four_stats(k, q1, src):
                for t in range(BT):
                    last = dve.bn_stats(st2[:, k, t, :], src(t))
                last.then_inc(ffn_bn_ok, 1)
                dve.wait_ge(ffn_bn_ok, 2 * q1 + k + 1)
                settle(dve, d_settled)
                for t in range(BT):
                    last = dve.bn_aggr(mv2[:, k, t, :], st2[:, k, t, :])
                last.then_inc(ffn_stat_ok, 1)

            def four_hat(k, q1, src, dst, ready):
                dve.wait_ge(ffn_rstd_ok, 2 * q1 + k + 1)
                for t in range(BT):
                    last = dve.tensor_scalar(dst(t), src(t), mv2[:, k, t, 0:1], rs2[:, k, t:t + 1], ALU.subtract, ALU.mult)
                last.then_inc(ready, 1)

            def stats_x(q1):
                four_stats(0, q1, lambda t: tile(BT * q1 + t))

            def hat_x(q1, r):
                four_hat(0, q1, lambda t: tile(BT * q1 + t), lambda t: h2[:, r, t, :], x_hat_ok)

            def stats_h(q1, r):
                dve.wait_ge(h2_ok, q1 + 1)
                four_stats(1, q1, lambda t: h2[:, r, t, :])

            def hat_h(q1, r):
                need(dve, xn_turned, q1)
                four_hat(1, q1, lambda t: h2[:, r, t, :], lambda t: xn_tok[:, t, :], xn_ok)

            def split_xn(q1, r):
                dve.wait_ge(xn_t_ok, q1 + 1)
                dve.tensor_copy(xn_parts[:, r, 0, :], xn_t[:]).then_inc(xn_high_ok, 1)
                dve.wait_ge(xn_high_ok, q1 + 1)
                dve.tensor_tensor(xn_parts[:, r, 1, :], xn_t[:], xn_parts[:, r, 0, :].bitcast(F32), ALU.subtract).then_inc(xn_parts_ok, 1)

            RANK_STEPS = 13

            def rank_experts(q1, bank):
                n = [RANK_STEPS * q1]

                def then(ins):
                    ins.then_inc(rank_steps, 1)
                    n[0] = n[0] + 1
                    dve.wait_ge(rank_steps, n[0])
                dve.wait_ge(logits_done, q1 + 1)
                then(dve.tensor_tensor(lg[:], bank[:, 0:8 * BT].rearrange("p (t e) -> p t e", t=BT)[:, :, 0:EXPERTS],
                                       gate_bb.rearrange("p (o e) -> p o e", o=1).to_broadcast([P, BT, EXPERTS]), ALU.add))
                other = lg[:].rearrange("p t (o e) -> p t o e", o=1).to_broadcast([P, BT, EXPERTS, EXPERTS])
                own = lg[:].rearrange("p t (e o) -> p t e o", o=1).to_broadcast([P, BT, EXPERTS, EXPERTS])
                dve.tensor_tensor(cmp_gt[:], other, own, ALU.is_gt)
                then(dve.tensor_tensor(cmp_eq[:], other, own, ALU.is_equal))
                then(dve.tensor_tensor(cmp_eq[:], cmp_eq[:], tri[:].rearrange("p (o e) g -> p o e g", o=1).to_broadcast([P, BT, EXPERTS, EXPERTS]), ALU.mult))
                then(dve.tensor_tensor(cmp_gt[:], cmp_gt[:], cmp_eq[:], ALU.add))
                then(dve.tensor_reduce(rank[:], cmp_gt[:], AX_X, ALU.add))
                dve.tensor_scalar(sel[:, 0], rank[:], 0.0, None, ALU.is_equal)
                then(dve.tensor_scalar(sel[:, 1], rank[:], 1.0, None, ALU.is_equal))
                then(dve.tensor_tensor(pick[:], lg[:], sel[:, 1], ALU.mult))
                dve.tensor_reduce(top[:, 1], pick[:], AX_X, ALU.add)
                then(dve.tensor_reduce(top[:, 0], lg[:], AX_X, ALU.max))
                dve.tensor_tensor(top[:, 2], top[:, 0], top[:, 1], ALU.subtract).then_inc(top_ok, 1)

            def weigh_experts(q1, r):
                dve.wait_ge(gate_tanh_ok, q1 + 1)
                dve.tensor_tensor(pick[:], sel[:, 0], sel[:, 1], ALU.subtract).then_inc(rank_steps, 1)
                dve.wait_ge(rank_steps, RANK_STEPS * q1 + 9)
                dve.tensor_tensor(pick[:], pick[:], th[:].rearrange("p (t o) -> p t o", o=1).to_broadcast([P, BT, EXPERTS]), ALU.mult)
                dve.tensor_tensor(rank[:], sel[:, 0], sel[:, 1], ALU.add).then_inc(rank_steps, 1)
                dve.wait_ge(rank_steps, RANK_STEPS * q1 + 10)
                dve.tensor_tensor(rank[:], pick[:], rank[:], ALU.add).then_inc(rank_steps, 1)
                dve.wait_ge(rank_steps, RANK_STEPS * q1 + 11)
                dve.tensor_scalar(w_gate[:, r], rank[:], 0.5, None, ALU.mult).then_inc(rank_steps, 1)
                dve.wait_ge(rank_steps, RANK_STEPS * q1 + 12)
                whole = w_gate[:, r].rearrange("p (o t) e -> p o (t e)", o=1).to_broadcast([P, 2, BT * EXPERTS])
                high, low = (gate_parts[:, i:4:2, 0:BT * EXPERTS] for i in range(2))
                if isinstance(q1, int) and q1 == 0:
                    dve.wait_ge(parts_zero, 2)
                dve.tensor_copy(high, whole).then_inc(rank_steps, 1)
                dve.wait_ge(rank_steps, RANK_STEPS * q1 + 13)
                dve.tensor_tensor(low, whole, high.bitcast(F32), ALU.subtract).then_inc(w_ok, 1)

            def step(b, f, p):
                live, smax, pre, post = 0 <= f < BATCH, 0 <= f + 1 < BATCH, 0 <= f + 2 < BATCH, 0 <= f - 1 < BATCH
                if live:
                    split_max(b, p, 1)
                for n in range(HEADS):
                    if smax:
                        dve.wait_ge(scores_done, 16 * (b + 1) + n + 1)
                        dve.tensor_reduce(row_max[:, 1 - p, n, :], smax_bank[n % 2][:].rearrange("p (t k) -> p t k", t=TPB),
                                          AX_X, ALU.max).then_inc(row_max_ok, 1)
                    if n == SLOT["square_take"] and post:
                        take_square(squared(b - 1))
                    if n == SLOT["max_row1"] and live:
                        max_row(b, 1, my)
                    if n == SLOT["v_bias"] and pre:
                        dve.wait_ge(v_done, b + 3)
                        need(dve, v_blocks_ok, b + 2)
                        dve.tensor_tensor(v_tok[:], my[:, 0:SEQ].rearrange("p (t e) -> p t e", t=TPB), bvb, ALU.add).then_inc(v_ok, 1)
                    if n == SLOT["normalise1"] and post:
                        normalise(b - 1, 1, mx)
                    if n == SLOT["max_split0"] and smax:
                        split_max(b + 1, 1 - p, 0)
                    if n == SLOT["stats"] and 0 <= f + 3 < BATCH:
                        b3 = b + 3
                        if f in (-3, -2, 0):
                            dve.wait_ge(x_in[(-3, -2, 0).index(f)], 16)
                        need(dve, xhat_ok, b3)
                        for t in range(TPB):
                            last = dve.bn_stats(stats[:, t, :], tile(TPB * b3 + t))
                        last.then_inc(bn_ok, 1)
                        dve.wait_ge(bn_ok, b3 + 1)
                        settle(dve, d_settled)
                        for t in range(TPB):
                            last = dve.bn_aggr(mv[:, t, :], stats[:, t, :])
                        last.then_inc(stat_ok, 1)
                        if f == -3:
                            dve.memset(k_stack[:, 0, 8:HEADS, :].bitcast(F32), 1.0).then_inc(stack_init[0], 1)
                    if n == SLOT["residual"] and post:
                        add_attention(b - 1)
                    if n == SLOT["max_row0"] and smax:
                        max_row(b + 1, 0, mx)
                    if n == SLOT["normalise0"] and live:
                        normalise(b, 0, my)
                    if n == SLOT["xhat"] and 0 <= f + 3 < BATCH:
                        b3 = b + 3
                        dve.wait_ge(rstd_ok, b3 + 1)
                        need(dve, x_turned, b3)
                        for t in range(TPB):
                            last = dve.tensor_scalar(xhat[:, t, :], tile(TPB * b3 + t), mv[:, t, 0:1], rstd[:, t:t + 1], ALU.subtract, ALU.mult)
                        last.then_inc(xhat_ok, 1)
                    if n == SLOT["square_due"] and live and f < BATCH - 1:
                        squaring_due(squared(b))
                    if (f, n) in SERIES_AT:
                        series(SERIES_AT.index((f, n)))
                    if f == -2 and n == 3:
                        dve.wait_ge(qk_ok, 1)
                        split_qk(dve, 0)
                    if (f, n) == (BATCH - 3, 5):
                        stats_x(0)
                    if (f, n) == (BATCH - 2, 2):
                        hat_x(0, 0)
                    if (f, n) == (BATCH - 2, 7):
                        stats_h(0, 0)
                    if (f, n) == (BATCH - 2, 11):
                        hat_h(0, 0)
                    if f == BATCH - 1:
                        if n == 1:
                            squaring_due(SQUARINGS)
                        if n == 5:
                            take_square(SQUARINGS, smax_bank[1])
                        if n == 3:
                            dve.wait_ge(scores_t_done, 16 * (BATCH - 1))
                            dve.tensor_copy(w1_parts[:, 0, :], w1).then_inc(w1_hi, 1)
                            dve.wait_ge(w1_hi, 1)
                            dve.tensor_tensor(w1_parts[:, 1, :], w1, w1_parts[:, 0, :].bitcast(F32), ALU.subtract).then_inc(w1_ok, 1)
                        if n == 5:
                            split_xn(0, 0)
                        if n in (11, 13, 15):
                            k = (n - 11) // 2
                            dve.wait_ge(rot_product_done, k + 1)
                            dve.tensor_copy(rot_all[:, k, :], smax_bank[1][:, 0:P]).then_inc(rot_product_ok, 1)
                        if n == 7:
                            rank_experts(0, smax_bank[0])
                if f == -3:
                    modulations()

            iterations(dve, step, between)

            def add_expert(q, p, e):
                dve.wait_ge(layer2_done, CHUNKS * q + ACH + 2 * e + 2)
                need(dve, acc_ok, EXPERTS * q + e)
                if e == 0:
                    dve.wait_ge(acc0_ok, q + 1)
                for t in range(BT):
                    last = dve.scalar_tensor_tensor(out=acc[:, p, t, :], in0=st_bank[e % 2][:, EMB * t:EMB * (t + 1)],
                                                    scalar=w_gate[:, p, t, e:e + 1], in1=acc[:, p, t, :], op0=ALU.mult, op1=ALU.add)
                last.then_inc(acc_ok, 1)

            def gate_logit(i, v):
                for t in range(BT):
                    last = dve.tensor_tensor_reduce((gen_abs, gen_t)[i][:, t, :], v[:, t, :], gcwb[:, i, :], 1.0, 0.0, ALU.mult, ALU.add, zpart[:, i, t:t + 1])
                return last

            def ffn(q, f, p):
                for c in range(CHUNKS):
                    if c == 1 and 0 <= f - 1 < BLOCKS:
                        add_expert(q - 1, 1 - p, EXPERTS - 1)
                        dve.wait_ge(acc_ok, EXPERTS * q)
                        gate_logit(1, acc[:, 1 - p]).then_inc(mix_steps, 1)
                        dve.wait_ge(mix_steps, 2 * q - 1)
                        dve.wait_ge(dense_logit_ok, q)
                        dve.tensor_tensor(zsum[:], zpart[:, 0], zpart[:, 1], ALU.add).then_inc(mix_logit_ok, 1)
                    if f == 0:
                        if c in (0, 1):
                            for k in (2 * c, 2 * c + 1):
                                dve.wait_ge(ew2_rot_done, k + 1)
                                if k < 3:
                                    dve.tensor_copy(ew2_rot[:, 4 * k:4 * k + 4, :], st_bank[k % 2][:].rearrange("p (c j) -> p c j", c=4)).then_inc(ew2_rot_ok, 1)
                                else:
                                    dve.wait_ge(diag_steps, 8)
                                    dve.tensor_tensor(eb2_rot[:], st_bank[1][:, 0:EMB].rearrange("p (o e) -> p o e", o=1).to_broadcast([P, BT, EMB]),
                                                      diag[:], ALU.mult).then_inc(eb2_steps, 1)
                                    dve.wait_ge(eb2_steps, 1)
                                    dve.tensor_copy(eb2_parts[:], eb2_rot[:]).then_inc(eb2_steps, 1)
                                    dve.wait_ge(eb2_steps, 2)
                                    dve.tensor_tensor(eb2_parts[64:P], eb2_rot[64:P], eb2_parts[64:P].bitcast(F32), ALU.subtract).then_inc(ew2_rot_ok, 1)
                            if c == 0:
                                normalise(BATCH - 1, 1, mx)
                        if c == 6:
                            add_attention(BATCH - 1)
                    if 0 <= f < BLOCKS:
                        if c == CHUNK["weigh"]:
                            weigh_experts(q, p)
                        if c == CHUNK["gates_evac"]:
                            dve.wait_ge(wt_done, q + 1)
                            dve.tensor_copy(w_t[:], mx[:, 0:P]).then_inc(wt_ok, 1)
                    if c == CHUNK["mix"] and 0 <= f - 1 < BLOCKS:
                        dve.wait_ge(mix_tanh_ok, q)
                        dve.tensor_scalar(gmix[:], gth[:], 0.5, 0.5, ALU.mult, ALU.add).then_inc(mix_steps, 1)
                        dve.wait_ge(mix_steps, 2 * q)
                        dve.wait_ge(diff_ok, q)
                        dve.wait_ge(base_ok, q)
                        for t in range(BT):
                            last = dve.scalar_tensor_tensor(out=y_out[:, 1 - p, t, :], in0=diff[:, t, :], scalar=gmix[:, t:t + 1],
                                                            in1=y_out[:, 1 - p, t, :], op0=ALU.mult, op1=ALU.add)
                        last.then_inc(y_fin, 1)
                    if 0 <= f < BLOCKS:
                        if c == CHUNK["biases_evac"]:
                            dve.wait_ge(biases_done, q + 1)
                            dve.tensor_copy(acc[:, p], my[:].rearrange("p (t e) -> p t e", t=BT)).then_inc(acc0_ok, 1)
                        if c == 5:
                            dve.wait_ge(layer2_done, CHUNKS * q + ACH)
                            dve.tensor_tensor(abel[:, p], pv_bank[0][:].rearrange("p (t e) -> p t e", t=BT),
                                              ab2b.rearrange("p (o e) -> p o e", o=1).to_broadcast([P, BT, EMB]), ALU.add).then_inc(abel_ok, 1)
                        if c >= 7 and c % 2 == 1:
                            add_expert(q, p, (c - 7) // 2)
                        if c == CHUNK["dense_logit"]:
                            dve.wait_ge(abel_ok, q + 1)
                            gate_logit(0, abel[:, p]).then_inc(dense_logit_ok, 1)
                    if 0 <= f + 1 < BLOCKS:
                        if c == CHUNK["x_stats"]:
                            stats_x(q + 1)
                        if c == CHUNK["x_hat"]:
                            need(dve, base_ok, q)
                            hat_x(q + 1, 1 - p)
                        if c == CHUNK["h_stats"]:
                            stats_h(q + 1, 1 - p)
                        if c == CHUNK["h_hat"]:
                            hat_h(q + 1, 1 - p)
                        if c == CHUNK["xn_split"]:
                            split_xn(q + 1, 1 - p)
                        if c == CHUNK["rank"]:
                            rank_experts(q + 1, my)

            dve.wait_ge(ffn_const, 5)
            blocks(dve, ffn)


def kernel(**inputs):
    import concourse.bacc as bacc
    from concourse.bass_utils import run_bass_kernel_spmd

    def of(name):
        return np.asarray(inputs[name])

    attn, ffn = "L0_attn_", "L0_ffn_"
    by_row = of(ffn + "ew1").transpose(1, 0, 2).reshape(EMB, EXPERTS * EH)
    down = [of(ffn + "aw2"), of(ffn + "ew2").reshape(EXPERTS * EH, EMB)]
    down = np.concatenate(down, axis=0).reshape(CHUNKS, P, EMB).transpose(1, 0, 2).reshape(P, CHUNKS * EMB)


    def by_dim(w):
        return w.reshape(-1, 2, 8, HDIM).transpose(0, 1, 3, 2).reshape(-1, EMB)
    arrays = {
        "x": of(attn + "hidden_states").reshape(TILES, P, EMB),
        "c": of("L0_c"),
        "w_attn": np.concatenate([by_dim(of(attn + "wq")), by_dim(of(attn + "wk")), of(attn + "wv"), of(attn + "wo"), of("L0_wmod")], axis=1),
        "vec_rows": np.concatenate([of(ffn + "ab1").reshape(ACH, P), of(ffn + "eb1").reshape(ECH, P)]
                                   + [by_dim(of(attn + "bq")), by_dim(of(attn + "bk"))]
                                   + [of(n).reshape(1, P) for n in (ffn + "ln_g", ffn + "ln_b")], axis=0),
        "bcast": np.concatenate([of(attn + "bv"), of(attn + "bv"), of(ffn + "ab2"), of(ffn + "gc_w").reshape(2 * EMB), of(attn + "bo"),
                                 of(ffn + "gate_b"), of(ffn + "gc_b")]).reshape(1, NB),
        "gens": of(ffn + "gens"),
        "w_ffn": np.concatenate([of(ffn + "aw1"), by_row, down, of(ffn + "gate_w")], axis=1),
        "eb2": of(ffn + "eb2"),
    }
    arrays = {f"in_{n}": np.ascontiguousarray(v) for n, v in arrays.items()}
    nc = bacc.Bacc("TRN2", target_bir_lowering=False, num_devices=1)
    aps = {n[3:]: nc.dram_tensor(n, v.shape, mybir.dt.from_np(v.dtype), kind="ExternalInput").ap() for n, v in arrays.items()}
    out = nc.dram_tensor("out_0", (TILES, P, EMB), F32, kind="ExternalOutput").ap()
    build(nc, aps, out)
    r = run_bass_kernel_spmd(nc, [arrays], core_ids=[0])
    return np.asarray(r.results[0]["out_0"]).reshape(BATCH, SEQ, EMB)
```
